# Optimizing a Trainium2 kernel written in Bass

```python
import numpy as np
import jax
import jax.numpy as jnp

def _softmax(x, axis=-1):
    return jax.nn.softmax(x, axis=axis)

def _gelu(x):
    return jax.nn.gelu(x, approximate=True)

def _silu(x):
    return jax.nn.silu(x)

def _sigmoid(x):
    return jax.nn.sigmoid(x)

def _layernorm(x, axis=-1, eps=1e-05):
    m = jnp.mean(x, axis=axis, keepdims=True)
    v = jnp.var(x, axis=axis, keepdims=True)
    return (x - m) / jnp.sqrt(v + eps)

def _scatter_add(tgt, idx, src, axis=0):
    return tgt.at[idx].add(src)

def _segment_sum(src, seg, n):
    return jax.ops.segment_sum(src, seg, n)
kernel_name = 'mk_xattn_ffn_d4_seqx_r8_303d3d'

def setup_inputs(seed: int=0):
    np.random.seed(seed)
    _w = jnp.asarray

    def _rec_inputs():
        import jax
        import jax.numpy as jnp
        _rk = jax.random.key(seed)
        x = -0.0002928 + 1 * jax.random.normal(jax.random.fold_in(_rk, 1), (64, 64, 128), jnp.float32)
        _lenS = 64 - jax.random.randint(jax.random.fold_in(_rk, 7), (64,), 0, max(1, 64 // 4) + 1, jnp.int32)
        _lenS2 = 64 - jax.random.randint(jax.random.fold_in(_rk, 8), (64,), 0, max(1, 64 // 4) + 1, jnp.int32)
        _ctx_1024P = jax.random.normal(jax.random.fold_in(_rk, 11), (64, 16, 128), jnp.float32)
        _ctx_1024c = jax.random.dirichlet(jax.random.fold_in(_rk, 511), 0.3 * jnp.ones((16,), jnp.float32), (64, 64))
        _ctx_1024t = jnp.einsum('bsk,bkd->bsd', _ctx_1024c, _ctx_1024P)
        _ctx_1024t = _ctx_1024t * jax.lax.rsqrt(jnp.mean(jnp.square(_ctx_1024t)) + 1e-12) * 0.953939
        ctx_1024 = -1.39393e-06 + 0.999914 * (_ctx_1024t + 0.3 * jax.random.normal(jax.random.fold_in(_rk, 611), (64, 64, 128), jnp.float32))
        _validS = jnp.arange(64)[None, :] < _lenS[:, None]
        _validS2 = jnp.arange(64)[None, :] < _lenS2[:, None]
        _causal = jnp.tril(jnp.ones((64, 64), dtype=bool))
        mask_BxSxS2_ik1 = jnp.where(jnp.broadcast_to(_validS2[:, None, :], (64, 64, 64)), 1, 0).astype(jnp.int32)
        return (x, ctx_1024, mask_BxSxS2_ik1)
    x, ctx_1024, mask_BxSxS2_ik1 = _rec_inputs()

    def _L0_xattn_setup():
        import jax, jax.numpy as jnp
        import numpy as np
        HEADS = 16
        key = jax.random.key(seed)
        ks = jax.random.split(key, 5)
        B, N, D = (2, 256, 128)
        q = jax.random.normal(ks[0], (B, N, D), dtype=jnp.float32)
        kv = jax.random.normal(ks[1], (B, N, D), dtype=jnp.float32)
        s = 1.0 / np.sqrt(D)
        Wq = jax.random.normal(ks[2], (D, D), dtype=jnp.float32) * s
        Wkv = jax.random.normal(ks[3], (D, 2 * D), dtype=jnp.float32) * s
        Wout = jax.random.normal(ks[4], (D, D), dtype=jnp.float32) * s
        return {'q': q, 'kv': kv, 'Wq': Wq, 'Wkv': Wkv, 'Wout': Wout}
    _L0_xattn_all = _L0_xattn_setup()
    _L0_xattn_in = {k: v for k, v in _L0_xattn_all.items() if k in ('Wq', 'Wkv', 'Wout')}
    del _L0_xattn_all

    def _L0_ffn_setup():
        import jax, jax.numpy as jnp
        import numpy as np
        D = 128
        F = 512
        E = 8
        K = 2
        B, S = (4, 256)
        key = jax.random.key(seed)
        ks = jax.random.split(key, 6)
        scale_in = 1.0 / np.sqrt(D)
        scale_mid = 1.0 / np.sqrt(F)
        return {'x': jax.random.normal(ks[0], (B, S, D), dtype=jnp.float32), 'router_w': jax.random.normal(ks[1], (E, D), dtype=jnp.float32) * scale_in, 'w1': jax.random.normal(ks[2], (E, F, D), dtype=jnp.float32) * scale_in, 'b1': jax.random.normal(ks[3], (E, F), dtype=jnp.float32) * 0.01, 'w2': jax.random.normal(ks[4], (E, D, F), dtype=jnp.float32) * scale_mid, 'b2': jax.random.normal(ks[5], (E, D), dtype=jnp.float32) * 0.01}
    _L0_ffn_all = _L0_ffn_setup()
    _L0_ffn_in = {k: v for k, v in _L0_ffn_all.items() if k in ('router_w', 'w1', 'b1', 'w2', 'b2')}
    del _L0_ffn_all

    def _L1_xattn_setup():
        import jax, jax.numpy as jnp
        import numpy as np
        HID = 128
        HEADS = 16
        HEAD_DIM = HID // HEADS

        def _split_heads(x, W, b):
            B, S, _ = x.shape
            y = x @ W + b
            return y.reshape(B, S, HEADS, HEAD_DIM).transpose(0, 2, 1, 3)
        key = jax.random.key(seed)
        ks = jax.random.split(key, 12)
        B, S = (4, 256)
        inp = {'query': jax.random.normal(ks[0], (B, S, HID), dtype=jnp.float32), 'key': jax.random.normal(ks[1], (B, S, HID), dtype=jnp.float32), 'value': jax.random.normal(ks[2], (B, S, HID), dtype=jnp.float32), 'mask': jax.random.randint(ks[3], (B, S, S), 0, 2, dtype=jnp.int32), 'Wq': jax.random.normal(ks[4], (HID, HID), dtype=jnp.float32) * (1.0 / np.sqrt(HID)), 'bq': jnp.zeros((HID,), dtype=jnp.float32), 'Wk': jax.random.normal(ks[5], (HID, HID), dtype=jnp.float32) * (1.0 / np.sqrt(HID)), 'bk': jnp.zeros((HID,), dtype=jnp.float32), 'Wv': jax.random.normal(ks[6], (HID, HID), dtype=jnp.float32) * (1.0 / np.sqrt(HID)), 'bv': jnp.zeros((HID,), dtype=jnp.float32), 'Wo': jax.random.normal(ks[7], (HID, HID), dtype=jnp.float32) * (1.0 / np.sqrt(HID)), 'bo': jnp.zeros((HID,), dtype=jnp.float32)}
        return inp
    _L1_xattn_all = _L1_xattn_setup()
    _L1_xattn_in = {k: v for k, v in _L1_xattn_all.items() if k in ('Wq', 'bq', 'Wk', 'bk', 'Wv', 'bv', 'Wo', 'bo')}
    del _L1_xattn_all

    def _L1_ffn_setup():
        import jax, jax.numpy as jnp
        import numpy as np
        QMIN, QMAX = (-128.0, 127.0)

        def _affine_quantize(x):
            amin, amax = (jnp.min(x), jnp.max(x))
            scale = jnp.maximum((amax - amin) / 255.0, 1e-08)
            zp = jnp.clip(jnp.round(-amin / scale) + QMIN, QMIN, QMAX)
            q = jnp.clip(jnp.round(x / scale) + zp, QMIN, QMAX)
            return (q, scale, zp)

        def _sym_quantize(w):
            scale = jnp.maximum(jnp.max(jnp.abs(w)) / 127.0, 1e-08)
            q = jnp.clip(jnp.round(w / scale), -127.0, 127.0)
            return (q, scale)

        def _qlinear(x, W, b):
            xq, sx, zx = _affine_quantize(x)
            wq, sw = _sym_quantize(W)
            acc = jnp.einsum('bsh,oh->bso', xq - zx, wq)
            return acc * (sx * sw) + b
        key = jax.random.key(seed)
        k1, k2, k3, k4, k5 = jax.random.split(key, 5)
        d, h = (128, 512)
        x = jax.random.normal(k1, (4, 512, d), dtype=jnp.float32)
        W1 = jax.random.normal(k2, (h, d), dtype=jnp.float32) * (1.0 / np.sqrt(d))
        b1 = jax.random.normal(k3, (h,), dtype=jnp.float32) * 0.02
        W2 = jax.random.normal(k4, (d, h), dtype=jnp.float32) * (1.0 / np.sqrt(h))
        b2 = jax.random.normal(k5, (d,), dtype=jnp.float32) * 0.02
        return {'x': x, 'W1': W1, 'b1': b1, 'W2': W2, 'b2': b2}
    _L1_ffn_all = _L1_ffn_setup()
    _L1_ffn_in = {k: v for k, v in _L1_ffn_all.items() if k in ('W1', 'b1', 'W2', 'b2')}
    del _L1_ffn_all

    def _L2_xattn_setup():
        import jax, jax.numpy as jnp
        import numpy as np
        key = jax.random.key(seed)
        ks = jax.random.split(key, 5)
        b, n_q, n_kv = (16, 128, 512)
        query_dim, context_dim, heads, dim_head = (128, 128, 16, 64)
        inner = heads * dim_head
        x = jax.random.normal(ks[0], (b, n_q, query_dim), dtype=jnp.float32)
        context = jax.random.normal(ks[1], (b, n_kv, context_dim), dtype=jnp.float32)
        Wq = jax.random.normal(ks[2], (query_dim, inner), dtype=jnp.float32) * query_dim ** (-0.5)
        Wkv = jax.random.normal(ks[3], (context_dim, 2 * inner), dtype=jnp.float32) * context_dim ** (-0.5)
        Wout = jax.random.normal(ks[4], (inner, query_dim), dtype=jnp.float32) * inner ** (-0.5)
        bout = jnp.zeros((query_dim,), dtype=jnp.float32)
        return {'x': x, 'context': context, 'Wq': Wq, 'Wkv': Wkv, 'Wout': Wout, 'bout': bout}
    _L2_xattn_all = _L2_xattn_setup()
    _L2_xattn_in = {k: v for k, v in _L2_xattn_all.items() if k in ('Wq', 'Wkv', 'Wout', 'bout')}
    del _L2_xattn_all

    def _L2_ffn_setup():
        import jax, jax.numpy as jnp
        import numpy as np
        ALPHA = 2.0
        TOP_K = 2
        key = jax.random.key(seed)
        ks = jax.random.split(key, 8)
        B, S, D, H, E = (2, 256, 128, 512, 8)
        Er = E - 1
        s_in = 1.0 / np.sqrt(D)
        s_hid = 1.0 / np.sqrt(H)
        return {'x': jax.random.normal(ks[0], (B, S, D), dtype=jnp.float32), 'router_w': jax.random.normal(ks[1], (D, E), dtype=jnp.float32) * s_in, 'up_w': jax.random.normal(ks[2], (Er, D, H), dtype=jnp.float32) * s_in, 'gate_w': jax.random.normal(ks[3], (Er, D, H), dtype=jnp.float32) * s_in, 'down_w': jax.random.normal(ks[4], (Er, H, D), dtype=jnp.float32) * s_hid * 0.1, 'shared_up_w': jax.random.normal(ks[5], (D, H), dtype=jnp.float32) * s_in, 'shared_gate_w': jax.random.normal(ks[6], (D, H), dtype=jnp.float32) * s_in, 'shared_down_w': jax.random.normal(ks[7], (H, D), dtype=jnp.float32) * s_hid * 0.1}
    _L2_ffn_all = _L2_ffn_setup()
    _L2_ffn_in = {k: v for k, v in _L2_ffn_all.items() if k in ('router_w', 'up_w', 'gate_w', 'down_w', 'shared_up_w', 'shared_gate_w', 'shared_down_w')}
    del _L2_ffn_all

    def _L3_xattn_setup():
        import jax, jax.numpy as jnp
        import numpy as np
        DIM = 128
        NUM_HEADS = 16
        HEAD_DIM = DIM // NUM_HEADS
        key = jax.random.key(seed)
        ks = jax.random.split(key, 11)
        B, N, C = (2, 256, DIM)
        s = 1.0 / np.sqrt(C)
        inp = {'q': jax.random.normal(ks[0], (B, N, C), jnp.float32), 'k': jax.random.normal(ks[1], (B, N, C), jnp.float32), 'v': jax.random.normal(ks[2], (B, N, C), jnp.float32), 'Wq': jax.random.normal(ks[3], (C, C), jnp.float32) * s, 'bq': jnp.zeros((C,), jnp.float32), 'Wk': jax.random.normal(ks[4], (C, C), jnp.float32) * s, 'bk': jnp.zeros((C,), jnp.float32), 'Wv': jax.random.normal(ks[5], (C, C), jnp.float32) * s, 'bv': jnp.zeros((C,), jnp.float32), 'Wo': jax.random.normal(ks[6], (C, C), jnp.float32) * s, 'bo': jnp.zeros((C,), jnp.float32)}
        return inp
    _L3_xattn_all = _L3_xattn_setup()
    _L3_xattn_in = {k: v for k, v in _L3_xattn_all.items() if k in ('Wq', 'bq', 'Wk', 'bk', 'Wv', 'bv', 'Wo', 'bo')}
    del _L3_xattn_all

    def _L3_ffn_setup():
        import jax, jax.numpy as jnp
        import numpy as np
        B, S, H = (8, 512, 128)
        NAV = 128
        E = 8
        F = 2 * H
        key = jax.random.key(seed)
        ks = jax.random.split(key, 12)

        def w(k, shape, fan_in):
            return jax.random.normal(k, shape, dtype=jnp.float32) / np.sqrt(fan_in)
        return {'hidden_states': jax.random.normal(ks[0], (B, S, H), dtype=jnp.float32), 'Wp1': w(ks[1], (H, NAV), H), 'bp1': jnp.zeros((NAV,), jnp.float32), 'Wp2': w(ks[2], (NAV, E), NAV), 'bp2': jnp.zeros((E,), jnp.float32), 'W1': w(ks[3], (E, H, F), H), 'b1': jnp.zeros((E, F), jnp.float32), 'W2': w(ks[4], (E, F, H), F), 'b2': jnp.zeros((E, H), jnp.float32), 'Wo': w(ks[5], (H, H), H), 'bo': jnp.zeros((H,), jnp.float32)}
    _L3_ffn_all = _L3_ffn_setup()
    _L3_ffn_in = {k: v for k, v in _L3_ffn_all.items() if k in ('Wp1', 'bp1', 'Wp2', 'bp2', 'W1', 'b1', 'W2', 'b2', 'Wo', 'bo')}
    del _L3_ffn_all
    return {'x': x, 'ctx_1024': ctx_1024, 'mask_BxSxS2_ik1': mask_BxSxS2_ik1, 'L0_xattn_Wq': _L0_xattn_in['Wq'], 'L0_xattn_Wkv': _L0_xattn_in['Wkv'], 'L0_xattn_Wout': _L0_xattn_in['Wout'], 'L0_ffn_router_w': _L0_ffn_in['router_w'], 'L0_ffn_w1': _L0_ffn_in['w1'], 'L0_ffn_b1': _L0_ffn_in['b1'], 'L0_ffn_w2': _L0_ffn_in['w2'], 'L0_ffn_b2': _L0_ffn_in['b2'], 'L1_xattn_Wq': _L1_xattn_in['Wq'], 'L1_xattn_bq': _L1_xattn_in['bq'], 'L1_xattn_Wk': _L1_xattn_in['Wk'], 'L1_xattn_bk': _L1_xattn_in['bk'], 'L1_xattn_Wv': _L1_xattn_in['Wv'], 'L1_xattn_bv': _L1_xattn_in['bv'], 'L1_xattn_Wo': _L1_xattn_in['Wo'], 'L1_xattn_bo': _L1_xattn_in['bo'], 'L1_ffn_W1': _L1_ffn_in['W1'], 'L1_ffn_b1': _L1_ffn_in['b1'], 'L1_ffn_W2': _L1_ffn_in['W2'], 'L1_ffn_b2': _L1_ffn_in['b2'], 'L2_xattn_Wq': _L2_xattn_in['Wq'], 'L2_xattn_Wkv': _L2_xattn_in['Wkv'], 'L2_xattn_Wout': _L2_xattn_in['Wout'], 'L2_xattn_bout': _L2_xattn_in['bout'], 'L2_ffn_router_w': _L2_ffn_in['router_w'], 'L2_ffn_up_w': _L2_ffn_in['up_w'], 'L2_ffn_gate_w': _L2_ffn_in['gate_w'], 'L2_ffn_down_w': _L2_ffn_in['down_w'], 'L2_ffn_shared_up_w': _L2_ffn_in['shared_up_w'], 'L2_ffn_shared_gate_w': _L2_ffn_in['shared_gate_w'], 'L2_ffn_shared_down_w': _L2_ffn_in['shared_down_w'], 'L3_xattn_Wq': _L3_xattn_in['Wq'], 'L3_xattn_bq': _L3_xattn_in['bq'], 'L3_xattn_Wk': _L3_xattn_in['Wk'], 'L3_xattn_bk': _L3_xattn_in['bk'], 'L3_xattn_Wv': _L3_xattn_in['Wv'], 'L3_xattn_bv': _L3_xattn_in['bv'], 'L3_xattn_Wo': _L3_xattn_in['Wo'], 'L3_xattn_bo': _L3_xattn_in['bo'], 'L3_ffn_Wp1': _L3_ffn_in['Wp1'], 'L3_ffn_bp1': _L3_ffn_in['bp1'], 'L3_ffn_Wp2': _L3_ffn_in['Wp2'], 'L3_ffn_bp2': _L3_ffn_in['bp2'], 'L3_ffn_W1': _L3_ffn_in['W1'], 'L3_ffn_b1': _L3_ffn_in['b1'], 'L3_ffn_W2': _L3_ffn_in['W2'], 'L3_ffn_b2': _L3_ffn_in['b2'], 'L3_ffn_Wo': _L3_ffn_in['Wo'], 'L3_ffn_bo': _L3_ffn_in['bo']}

def reference(x, ctx_1024, mask_BxSxS2_ik1, L0_xattn_Wq, L0_xattn_Wkv, L0_xattn_Wout, L0_ffn_router_w, L0_ffn_w1, L0_ffn_b1, L0_ffn_w2, L0_ffn_b2, L1_xattn_Wq, L1_xattn_bq, L1_xattn_Wk, L1_xattn_bk, L1_xattn_Wv, L1_xattn_bv, L1_xattn_Wo, L1_xattn_bo, L1_ffn_W1, L1_ffn_b1, L1_ffn_W2, L1_ffn_b2, L2_xattn_Wq, L2_xattn_Wkv, L2_xattn_Wout, L2_xattn_bout, L2_ffn_router_w, L2_ffn_up_w, L2_ffn_gate_w, L2_ffn_down_w, L2_ffn_shared_up_w, L2_ffn_shared_gate_w, L2_ffn_shared_down_w, L3_xattn_Wq, L3_xattn_bq, L3_xattn_Wk, L3_xattn_bk, L3_xattn_Wv, L3_xattn_bv, L3_xattn_Wo, L3_xattn_bo, L3_ffn_Wp1, L3_ffn_bp1, L3_ffn_Wp2, L3_ffn_bp2, L3_ffn_W1, L3_ffn_b1, L3_ffn_W2, L3_ffn_b2, L3_ffn_Wo, L3_ffn_bo):
    import jax
    import jax.numpy as jnp

    def _L0_xattn_ref(q, kv, Wq, Wkv, Wout):
        import jax, jax.numpy as jnp
        import numpy as np
        HEADS = 16
        B, N, D = q.shape
        H = HEADS
        Dh = D // H
        scale = Dh ** (-0.5)
        qp = q @ Wq
        kvp = kv @ Wkv
        kp, vp = (kvp[..., :D], kvp[..., D:])

        def split_heads(t):
            return t.reshape(B, N, H, Dh).transpose(0, 2, 1, 3)
        qh, kh, vh = (split_heads(qp), split_heads(kp), split_heads(vp))
        dots = jnp.einsum('bhid,bhjd->bhij', qh, kh) * scale
        attn = jax.nn.softmax(dots.astype(jnp.float32), axis=-1).astype(dots.dtype)
        out = jnp.einsum('bhij,bhjd->bhid', attn, vh)
        out = out.transpose(0, 2, 1, 3).reshape(B, N, D)
        return out @ Wout

    def _L0_ffn_ref(x, router_w, w1, b1, w2, b2):
        import jax, jax.numpy as jnp
        import numpy as np
        D = 128
        F = 512
        E = 8
        K = 2
        B, S = (4, 256)
        orig_shape = x.shape
        xf = x.reshape(-1, D)
        logits = jnp.einsum('td,ed->te', xf, router_w)
        top_vals, top_idx = jax.lax.top_k(logits, K)
        probs = jax.nn.softmax(top_vals, axis=-1)
        out = jnp.zeros_like(xf)
        for e in range(E):
            w = jnp.sum(jnp.where(top_idx == e, probs, 0.0), axis=-1)
            h = jax.nn.gelu(jnp.einsum('td,fd->tf', xf, w1[e]) + b1[e], approximate=False)
            y = jnp.einsum('tf,df->td', h, w2[e]) + b2[e]
            out = out + w[:, None] * y
        return out.reshape(orig_shape)

    def _L1_xattn_ref(query, key, value, mask, Wq, bq, Wk, bk, Wv, bv, Wo, bo):
        import jax, jax.numpy as jnp
        import numpy as np
        HID = 128
        HEADS = 16
        HEAD_DIM = HID // HEADS

        def _split_heads(x, W, b):
            B, S, _ = x.shape
            y = x @ W + b
            return y.reshape(B, S, HEADS, HEAD_DIM).transpose(0, 2, 1, 3)
        B, S, _ = query.shape
        Q = _split_heads(query, Wq, bq)
        K = _split_heads(key, Wk, bk)
        V = _split_heads(value, Wv, bv)
        scale = 1.0 / jnp.sqrt(jnp.asarray(HEAD_DIM, dtype=Q.dtype))
        energy = jnp.einsum('bhqd,bhkd->bhqk', Q, K) * scale
        m = mask[:, None, :, :]
        energy = jnp.where(m == 0, jnp.asarray(-1000000000.0, dtype=energy.dtype), energy)
        attn = jax.nn.softmax(energy, axis=-1)
        out = jnp.einsum('bhqk,bhkd->bhqd', attn, V)
        out = out.transpose(0, 2, 1, 3).reshape(B, S, HID)
        return out @ Wo + bo

    def _L1_ffn_ref(x, W1, b1, W2, b2):
        import jax, jax.numpy as jnp
        import numpy as np
        QMIN, QMAX = (-128.0, 127.0)

        def _affine_quantize(x):
            amin, amax = (jnp.min(x), jnp.max(x))
            scale = jnp.maximum((amax - amin) / 255.0, 1e-08)
            zp = jnp.clip(jnp.round(-amin / scale) + QMIN, QMIN, QMAX)
            q = jnp.clip(jnp.round(x / scale) + zp, QMIN, QMAX)
            return (q, scale, zp)

        def _sym_quantize(w):
            scale = jnp.maximum(jnp.max(jnp.abs(w)) / 127.0, 1e-08)
            q = jnp.clip(jnp.round(w / scale), -127.0, 127.0)
            return (q, scale)

        def _qlinear(x, W, b):
            xq, sx, zx = _affine_quantize(x)
            wq, sw = _sym_quantize(W)
            acc = jnp.einsum('bsh,oh->bso', xq - zx, wq)
            return acc * (sx * sw) + b
        h = _qlinear(x, W1, b1)
        h = jax.nn.gelu(h, approximate=False)
        out = _qlinear(h, W2, b2)
        return out

    def _L2_xattn_ref(x, context, Wq, Wkv, Wout, bout):
        import jax, jax.numpy as jnp
        import numpy as np
        heads, dim_head = (16, 64)
        b, n_q, _ = x.shape
        n_kv = context.shape[1]
        scale = dim_head ** (-0.5)
        q = x @ Wq
        kv = context @ Wkv
        k, v = jnp.split(kv, 2, axis=-1)

        def split_heads(t):
            bb, n, _ = t.shape
            return t.reshape(bb, n, heads, dim_head).transpose(0, 2, 1, 3)
        q, k, v = map(split_heads, (q, k, v))
        i_idx = jnp.arange(n_q)[:, None]
        j_idx = jnp.arange(n_kv)[None, :]
        mask = j_idx % n_q == i_idx
        sim = jnp.einsum('bhid,bhjd->bhij', q, k) * scale
        max_neg = -jnp.finfo(sim.dtype).max
        sim = jnp.where(mask[None, None, :, :], sim, max_neg)
        attn = jax.nn.softmax(sim, axis=-1)
        out = jnp.einsum('bhij,bhjd->bhid', attn, v)
        out = out.transpose(0, 2, 1, 3).reshape(b, n_q, heads * dim_head)
        return out @ Wout + bout

    def _L2_ffn_ref(x, router_w, up_w, gate_w, down_w, shared_up_w, shared_gate_w, shared_down_w):
        import jax, jax.numpy as jnp
        import numpy as np
        ALPHA = 2.0
        TOP_K = 2
        logits = jnp.einsum('bsd,de->bse', x, router_w)
        probs = jax.nn.softmax(logits, axis=-1)
        topk_vals, topk_idx = jax.lax.top_k(probs, TOP_K)
        top1_val = topk_vals[..., 0]
        top1_idx = topk_idx[..., 0]
        hid = jnp.einsum('bsd,edh->ebsh', x, up_w) * jax.nn.silu(jnp.einsum('bsd,edh->ebsh', x, gate_w))
        Er = up_w.shape[0]
        mask = (top1_idx[None, :, :] == jnp.arange(Er)[:, None, None]).astype(x.dtype)
        routed = jnp.einsum('ebsh,ehd,ebs->bsd', hid, down_w, mask)
        shid = jnp.einsum('bsd,dh->bsh', x, shared_up_w) * jax.nn.silu(jnp.einsum('bsd,dh->bsh', x, shared_gate_w))
        shared = jnp.einsum('bsh,hd->bsd', shid, shared_down_w)
        return ALPHA * top1_val[..., None] * routed + shared

    def _L3_xattn_ref(q, k, v, Wq, bq, Wk, bk, Wv, bv, Wo, bo):
        import jax, jax.numpy as jnp
        import numpy as np
        DIM = 128
        NUM_HEADS = 16
        HEAD_DIM = DIM // NUM_HEADS
        B, Nq, C = q.shape
        Nkv = k.shape[1]
        H, D = (NUM_HEADS, HEAD_DIM)
        qh = (q @ Wq.T + bq).reshape(B, Nq, H, D).transpose(0, 2, 1, 3)
        kh = (k @ Wk.T + bk).reshape(B, Nkv, H, D).transpose(0, 2, 1, 3)
        vh = (v @ Wv.T + bv).reshape(B, Nkv, H, D).transpose(0, 2, 1, 3)
        scale = D ** (-0.5)
        attn = jax.nn.softmax(jnp.einsum('bhqd,bhkd->bhqk', qh, kh) * scale, axis=-1)
        out = jnp.einsum('bhqk,bhkd->bhqd', attn, vh)
        out = out.transpose(0, 2, 1, 3).reshape(B, Nq, C)
        return out @ Wo.T + bo

    def _L3_ffn_ref(hidden_states, Wp1, bp1, Wp2, bp2, W1, b1, W2, b2, Wo, bo):
        import jax, jax.numpy as jnp
        import numpy as np
        B, S, H = (8, 512, 128)
        NAV = 128
        E = 8
        F = 2 * H
        last = hidden_states[:, -1, :]
        logits = jax.nn.gelu(last @ Wp1 + bp1, approximate=False) @ Wp2 + bp2
        action_probs = jax.nn.softmax(logits, axis=-1)
        sel = jnp.argmax(action_probs, axis=-1)
        w1 = W1[sel]
        w2 = W2[sel]
        h = jax.nn.gelu(jnp.einsum('bsh,bhf->bsf', hidden_states, w1) + b1[sel][:, None, :], approximate=False)
        reasoned = jnp.einsum('bsf,bfh->bsh', h, w2) + b2[sel][:, None, :]
        out = reasoned @ Wo + bo
        return hidden_states + 0.3 * out
    x = x + _L0_xattn_ref(_layernorm(x, axis=-1), ctx_1024, L0_xattn_Wq, L0_xattn_Wkv, L0_xattn_Wout)
    x = x + _L0_ffn_ref(_layernorm(x, axis=-1), L0_ffn_router_w, L0_ffn_w1, L0_ffn_b1, L0_ffn_w2, L0_ffn_b2)
    x = x + _L1_xattn_ref(_layernorm(x, axis=-1), ctx_1024, ctx_1024, mask_BxSxS2_ik1, L1_xattn_Wq, L1_xattn_bq, L1_xattn_Wk, L1_xattn_bk, L1_xattn_Wv, L1_xattn_bv, L1_xattn_Wo, L1_xattn_bo)
    x = x + _L1_ffn_ref(_layernorm(x, axis=-1), L1_ffn_W1, L1_ffn_b1, L1_ffn_W2, L1_ffn_b2)
    x = x + _L2_xattn_ref(_layernorm(x, axis=-1), ctx_1024, L2_xattn_Wq, L2_xattn_Wkv, L2_xattn_Wout, L2_xattn_bout)
    x = x + _L2_ffn_ref(_layernorm(x, axis=-1), L2_ffn_router_w, L2_ffn_up_w, L2_ffn_gate_w, L2_ffn_down_w, L2_ffn_shared_up_w, L2_ffn_shared_gate_w, L2_ffn_shared_down_w)
    x = x + _L3_xattn_ref(_layernorm(x, axis=-1), ctx_1024, ctx_1024, L3_xattn_Wq, L3_xattn_bq, L3_xattn_Wk, L3_xattn_bk, L3_xattn_Wv, L3_xattn_bv, L3_xattn_Wo, L3_xattn_bo)
    x = x + _L3_ffn_ref(_layernorm(x, axis=-1), L3_ffn_Wp1, L3_ffn_bp1, L3_ffn_Wp2, L3_ffn_bp2, L3_ffn_W1, L3_ffn_b1, L3_ffn_W2, L3_ffn_b2, L3_ffn_Wo, L3_ffn_bo)
    return x

_drawn_inputs = setup_inputs


def setup_inputs(seed=0):
    import zlib

    import numpy as np

    out = dict(_drawn_inputs(seed))
    spreads = {'L1_xattn_bq': (0.0, 0.328),
     'L1_xattn_bk': (0.0, 0.8),
     'L1_xattn_bv': (0.0, 0.1),
     'L1_xattn_bo': (0.0, 0.1),
     'L2_xattn_bout': (0.0, 0.1),
     'L3_xattn_bq': (0.0, 0.366),
     'L3_xattn_bk': (0.0, 0.8),
     'L3_xattn_bv': (0.0, 0.1),
     'L3_xattn_bo': (0.0, 0.1),
     'L3_ffn_bp1': (0.0, 0.1),
     'L3_ffn_bp2': (0.0, 0.1),
     'L3_ffn_b1': (0.0, 0.8),
     'L3_ffn_b2': (0.0, 0.8),
     'L3_ffn_bo': (0.0, 0.7)}
    factors = {'L0_ffn_b1': 5.158, 'L0_ffn_b2': 5.12, 'L1_ffn_b1': 6.169, 'L1_ffn_b2': 5.214}
    for name, (base, spread) in spreads.items():
        noise = np.random.default_rng([zlib.crc32(name.encode()), seed]).standard_normal(out[name].shape)
        drawn = base * np.exp(spread * noise) if base else spread * noise
        out[name] = jnp.asarray(drawn.astype(out[name].dtype))
    for name, factor in factors.items():
        out[name] = (out[name] * factor).astype(out[name].dtype)
    return out
```

```python
from contextlib import ExitStack

import numpy as np
import concourse.bass as bass
from concourse import mybir

ALU = mybir.AluOpType
ACT = mybir.ActivationFunctionType
AX_X = mybir.AxisListType.X
F32 = mybir.dt.float32
BF16 = mybir.dt.bfloat16
F16 = mybir.dt.float16
I32 = mybir.dt.int32

P = 128
D = 128
B, S = 64, 64
TOKENS = B * S
TILES = TOKENS // P
GT = 4
GROUPS = TILES // GT
GTOK = GT * P
HEADS = 16
DH = D // HEADS
HQ = 32 // DH
ATT_SCALE = float(DH) ** -0.5
EPS = 1e-5
MASKED = -float(2 ** 31)
STEPS = 16


class Names:
    pass


LN_STEPS = 4


def layer_norm(dve, m, tiles, out, count, done):
    n0 = LN_STEPS * done
    even_mean, even_m2, odd_mean, odd_m2 = (m.ln_stats[:, 0:count, i] for i in (1, 2, 4, 5))
    both, diff, m2, sq, mean, var = (m.ln_work[:, i, 0:count] for i in range(6))
    for t in range(count):
        last = dve.bn_stats(m.ln_stats[:, t, :], tiles(t))
    last.then_inc(m.ln_step, 1)
    dve.wait_ge(m.ln_step, n0 + 1)
    dve.tensor_tensor(both, even_mean, odd_mean, ALU.add)
    dve.tensor_tensor(diff, even_mean, odd_mean, ALU.subtract)
    dve.tensor_tensor(m2, even_m2, odd_m2, ALU.add).then_inc(m.ln_step, 1)
    dve.wait_ge(m.ln_step, n0 + 2)
    dve.scalar_tensor_tensor(out=sq, in0=diff, scalar=0.25, in1=diff, op0=ALU.mult, op1=ALU.mult)
    dve.tensor_scalar(mean, both, 0.5, None, ALU.mult).then_inc(m.ln_step, 1)
    dve.wait_ge(m.ln_step, n0 + 3)
    dve.scalar_tensor_tensor(out=var, in0=m2, scalar=1.0 / D, in1=sq, op0=ALU.mult,
                             op1=ALU.add).then_inc(m.ln_step, 1)
    dve.wait_ge(m.ln_rstd_ready, done + 1)
    for t in range(count):
        last = dve.tensor_scalar(out(t), tiles(t), m.ln_work[:, 4, t:t + 1], m.ln_work[:, 7, t:t + 1],
                                 ALU.subtract, ALU.mult)
    return last


def layer_norm_power(pool, m, count, done):
    pool.wait_ge(m.ln_step, LN_STEPS * (done + 1))
    pool.tensor_tensor(m.ln_work[:, 6, 0:count], m.ln_work[:, 5, 0:count], m.eps[:, 0:count],
                       ALU.add).then_inc(m.ln_eps_added, 1)
    pool.wait_ge(m.ln_eps_added, done + 1)
    pool.tensor_tensor(m.ln_work[:, 7, 0:count], m.ln_work[:, 6, 0:count], m.minus_half[:, 0:count],
                       ALU.pow).then_inc(m.ln_rstd_ready, 1)


FRONT = ("xT", "Q0", "Q1", "K", "V0", "V1")


def fills(step, last):
    j, before, after = step % 8, [], []
    for k in range(4):
        if step == 4 * k + 6:
            before.append(("OT", k))
        if step == 4 * k + 7:
            before.append(("Y", k))
    if not (last and step >= 8) and step < STEPS:
        if j == 2:
            after.append(("xT", 0))
        if j == 3:
            after.append(("Q0", 0))
        if j == 4:
            before.append(("Q1", 0))
            after.append(("K", 0))
        if j == 5:
            before.append(("V0", 0))
            after.append(("V1", 0))
    return before, after


def fill_numbers(last):
    n, numbers = 0, {}
    for step in range(STEPS + 4):
        for where, part in enumerate(fills(step, last)):
            for f in part:
                numbers[step, where, f] = n
                n += 1
    return numbers, n


BODIES = GROUPS // 2
FULL, PER_BODY = fill_numbers(False)
LAST, PER_LAST = fill_numbers(True)
FILLS = len(FRONT) + (BODIES - 1) * PER_BODY + PER_LAST
ATT_STEPS = GROUPS * 8


def attention(nc, m, a, w, masked, biased, experts):
    fill0, step0, ln0, ctx0 = a * FILLS, a * ATT_STEPS, m.ln_count, a * GROUPS
    pair0 = a * 2 * GROUPS
    ctx_dma0 = a * 32 * GROUPS // 2
    m.ln_count += GROUPS
    with nc.Block(no_gpsimd_drain=True) as block:

        @block.sync
        def _(sp):
            def load_ctx(g, par):
                for copy in range(2):
                    sp.dma_start(m.ctx[:, par, :, copy, :], m.ctxT_dram[:, bass.ds(g * GTOK, GTOK)]
                                 .rearrange("d (c k) -> d c k", k=S)).then_inc(m.ctx_loaded[par], 16)
            load_ctx(0, 0)
            load_ctx(1, 1)
            sp.wait_ge(m.filled, fill0 + len(FRONT))
            load_ctx(2, 0)

            def body(it, more):
                base = fill0 + len(FRONT) + it * PER_BODY
                sp.wait_ge(m.filled, base + FULL[5, 1, ("V1", 0)] + 1)
                load_ctx(2 * it + 3, 1)
                if more:
                    sp.wait_ge(m.filled, base + FULL[13, 1, ("V1", 0)] + 1)
                    load_ctx(2 * it + 4, 0)
            with sp.Fori(0, BODIES - 2) as it:
                body(it, True)
            body(BODIES - 2, False)

        @block.tensor
        def _(pe):
            def front(f, par):
                if f == "xT":
                    for t in range(GT):
                        mm = pe.transpose(m.misc[:, t * P:(t + 1) * P], m.xn[:, t, :], m.ident[:, :])
                elif f in ("Q0", "Q1"):
                    mm = pe.matmul(m.misc[:, :], w.wq[:, int(f[1]), :], m.xnT[:, :], start=True, stop=True)
                elif f == "K":
                    for gp in range(2):
                        for b in range(2):
                            mm = pe.matmul(m.misc[:, gp * 256:(gp + 1) * 256], w.wk[:, b, gp, :],
                                           m.ctx[:, par, b::2, 0, :], start=(gp == 0 and b == 0),
                                           stop=(b == 1), skip_group_check=True)
                else:
                    for u in range(2):
                        for b in range(2):
                            c = (2 * u + b) * D
                            lhsT = m.ctx[:, par, 4 * int(f[1]) + 2 * u + b, :, :].rearrange("p c k -> p (c k)")
                            mm = pe.matmul(m.misc[:, c:c + D], lhsT, w.wv[:, :], start=True, stop=True,
                                           skip_group_check=True)
                mm.then_inc(m.filled, 1)

            def front_wait(f, par, g_expr, ctx_count, n):
                pe.wait_ge(m.emptied, n)
                if f == "xT":
                    pe.wait_ge(m.xn_ready, ctx0 + g_expr + 1)
                if f == "K":
                    pe.wait_ge(m.ctx_loaded[par], ctx_count)

            def out_part(kind, n, pair):
                pe.wait_ge(m.emptied, n)
                if kind == "OT":
                    pe.wait_ge(m.o_ready, pair + 1)
                    for u in range(2):
                        mm = pe.transpose(m.misc[:, u * P:(u + 1) * P], m.o_norm[:, u, :], m.ident[:, :])
                else:
                    for u in range(2):
                        mm = pe.matmul(m.misc[:, u * D:(u + 1) * D], m.oT[:, u * P:(u + 1) * P], w.wo[:, :],
                                       start=True, stop=True, skip_group_check=True)
                mm.then_inc(m.filled, 1)

            def scores(s, tile, par, ready):
                q, g = s // 4 % 2, s % 4
                if ready is not None:
                    pe.wait_ge(m.emptied, ready)
                rows = slice(64 * (g % 2), 64 * (g % 2) + 64)
                for u in range(2):
                    t = 2 * q + u
                    mm = pe.matmul(m.score[g][:, u * 256:(u + 1) * 256],
                                   m.qbd[rows, par, g // 2, t * P:(t + 1) * P],
                                   m.kexp[rows, par, g // 2, t, :, :].rearrange("p h k -> p (h k)"),
                                   start=(u == 0), stop=True, skip_group_check=True)
                if masked:
                    mm = pe.matmul(m.score[g][:, :], m.ident_b[:, :],
                                   m.penalty[:, bass.ds(tile, 2), :].unsqueeze(2).to_broadcast([P, 2, HQ, S]),
                                   start=False, stop=True, skip_group_check=True)
                mm.then_inc(m.scored, 1)

            def shift(s, n):
                pe.wait_ge(m.maxed, n + 1)
                pe.matmul(m.score[s % 4][:, :], m.ident_b[:, :],
                          m.neg_max[:, s % 4, :].unsqueeze(2).to_broadcast([P, 2 * HQ, S]),
                          start=False, stop=True, skip_group_check=True).then_inc(m.shifted, 1)

            def turn(s, n):
                pe.wait_ge(m.probs, n + 1)
                pe.wait_ge(m.turned_out, n)
                for x in range(4):
                    mm = pe.transpose(m.pT_ps[:, x * P:(x + 1) * P], m.prob[:, s % 2, x * P:(x + 1) * P],
                                      m.ident[:, :])
                mm.then_inc(m.turned, 1)

            def values(s, n, par, pair):
                q, g = s // 4 % 2, s % 4
                pe.wait_ge(m.turned_out, n + 1)
                if g == 0:
                    pe.wait_ge(m.o_copied, pair)
                for u in range(2):
                    for x in range(2):
                        slot = 2 * g + x
                        mm = pe.matmul(m.out_ps[u][:, slot * 36:(slot + 1) * 36],
                                       m.pT[:, s % 2, (2 * u + x) * P:(2 * u + x + 1) * P],
                                       m.v2[:, par, 2 * q + u, :, 2 * slot:2 * slot + 2, :]
                                       .rearrange("p b h e -> p b (h e)"),
                                       start=True, stop=True, skip_group_check=True)
                mm.then_inc(m.valued, 1)

            for i, f in enumerate(FRONT):
                front_wait(f, 0, 0, ctx_dma0 + 32, fill0 + i)
                front(f, 0)
            scores(0, 0, 0, fill0 + len(FRONT))
            scores(1, 0, 0, None)
            shift(0, step0)

            def body(it, last):
                numbers = LAST if last else FULL
                base = fill0 + len(FRONT) + it * PER_BODY
                n0 = step0 + it * STEPS
                for s in range(STEPS + 4):
                    for where, part in enumerate(fills(s, last)):
                        if where == 1:
                            if s + 2 < STEPS or (not last and s < STEPS):
                                t = s + 2
                                scores(t, 8 * it + 2 * (t // 4), t // 8 % 2,
                                       base + numbers[t - 2 - 1, 1, ("V1", 0)] + 1 if t % 8 == 0 else None)
                            if s + 1 < STEPS or (not last and s < STEPS):
                                shift(s + 1, n0 + s + 1)
                            if s < STEPS:
                                turn(s, n0 + s)
                        for f in part:
                            n = base + numbers[s, where, f]
                            if f[0] in ("OT", "Y"):
                                out_part(f[0], n, pair0 + 4 * it + f[1])
                            else:
                                par = (s // 8 + 1) % 2
                                front_wait(f[0], par, 2 * it + s // 8 + 1,
                                           ctx_dma0 + 32 * (it + 1 + s // 8), n)
                                front(f[0], par)
                    if 1 <= s <= STEPS:
                        values(s - 1, n0 + s - 1, (s - 1) // 8, pair0 + 4 * it + (s - 1) // 4)

            with pe.Fori(0, BODIES - 1) as it:
                body(it, False)
            body(BODIES - 1, True)

        @block.scalar
        def _(act):
            def take(f, n):
                if f == "xT":
                    act.wait_ge(m.filled, n + 1)
                    act.activation(m.xnT[:, :], m.misc[:, :], ACT.Copy).then_inc(m.emptied, 1)
                if f == "OT":
                    act.wait_ge(m.filled, n + 1)
                    act.activation(m.oT[:, :], m.misc[:, 0:2 * P], ACT.Copy).then_inc(m.emptied, 1)

            def exp(s, n):
                act.wait_ge(m.shifted, n + 1)
                act.activation(m.prob[:, s % 2, :], m.score[s % 4][:, :], ACT.Exp,
                               scale=ATT_SCALE).then_inc(m.probs, 1)

            def take_turned(s, n):
                act.wait_ge(m.turned, n + 1)
                act.activation(m.pT[:, s % 2, :], m.pT_ps[:, :], ACT.Copy).then_inc(m.turned_out, 1)

            def copy_out(pair):
                act.wait_ge(m.valued, pair * 4 + 4)
                act.wait_ge(m.o_ready, pair)
                for u in range(2):
                    for b in range(2):
                        rows = slice(64 * b, 64 * b + 64)
                        last = act.activation(
                            m.o_raw[rows, u, :, :].rearrange("p (s h) e -> p s (h e)", h=2),
                            m.out_ps[u][rows, 0:288].rearrange("p (s b e) -> p s b e", b=2, e=18)[:, :, b, :],
                            ACT.Copy)
                last.then_inc(m.o_copied, 1)

            take("xT", fill0)
            exp(0, step0)

            def body(it, last):
                numbers = LAST if last else FULL
                base = fill0 + len(FRONT) + it * PER_BODY
                n0 = step0 + it * STEPS
                for s in range(STEPS + 4):
                    before, after = fills(s, last)
                    for f in before:
                        take(f[0], base + numbers[s, 0, f])
                    if s + 1 < STEPS or (not last and s < STEPS):
                        exp(s + 1, n0 + s + 1)
                    if s < STEPS:
                        take_turned(s, n0 + s)
                    for f in after:
                        take(f[0], base + numbers[s, 1, f])
                    if s % 4 == 0 and 4 <= s <= STEPS:
                        copy_out(pair0 + 4 * it + s // 4 - 1)

            with act.Fori(0, BODIES - 1) as it:
                body(it, False)
            body(BODIES - 1, True)

        @block.vector
        def _(dve):
            def normalise(g, lnn):
                layer_norm(dve, m, lambda t: m.x[:, bass.ds(GT * g + t, 1), :].rearrange("p o d -> p (o d)"),
                           lambda t: m.xn[:, t, :], GT, lnn).then_inc(m.xn_ready, 1)

            def take(f, par, n, tile):
                if f in ("xT", "OT"):
                    return
                dve.wait_ge(m.filled, n + 1)
                if f in ("Q0", "Q1"):
                    gp = int(f[1])
                    last = dve.scalar_tensor_tensor(
                        out=m.qbd[:, par, gp, :], in0=m.misc[:, :], scalar=w.bq[:, gp:gp + 1],
                        in1=m.batch_mask[:, :], op0=ALU.add, op1=ALU.mult)
                elif f == "K":
                    for gp in range(2):
                        for h in range(HQ):
                            last = dve.tensor_scalar(
                                m.kexp[:, par, gp, :, h, :],
                                m.misc[:, gp * 256:(gp + 1) * 256].rearrange("p (t k) -> p t k", t=GT),
                                w.bk[:, gp:gp + 1], m.head_mask[:, h:h + 1], ALU.add, ALU.mult)
                elif f in ("V0", "V1"):
                    t = 2 * int(f[1])
                    last = dve.tensor_tensor(
                        m.v2[:, par, t:t + 2, :, :, 0:DH].rearrange("p t b h e -> p (t b) h e"),
                        m.misc[:, :].rearrange("p (c h e) -> p c h e", c=4, h=HEADS),
                        m.value_mask[:, :].rearrange("p (h e) -> p h e", h=HEADS).unsqueeze(1)
                        .to_broadcast([P, 4, HEADS, DH]), ALU.mult)
                else:
                    xs = m.x[:, bass.ds(tile, 2), :]
                    last = dve.tensor_tensor(xs, xs, m.misc[:, 0:2 * D].rearrange("p (t d) -> p t d", t=2), ALU.add)
                last.then_inc(m.emptied, 1)
                if f == "Y" and biased:
                    dve.wait_ge(m.emptied, n + 1)
                    dve.tensor_tensor(xs, xs, w.out_bias[:, :].unsqueeze(1).to_broadcast([P, 2, D]), ALU.add)

            def row_max(s, n):
                dve.wait_ge(m.scored, n + 1)
                dve.tensor_reduce(m.neg_max[:, s % 4, :], m.score[s % 4][:, :].rearrange("p (h k) -> p h k", k=S),
                                  AX_X, ALU.max, negate=True).then_inc(m.maxed, 1)

            def divide(pair):
                dve.wait_ge(m.o_copied, pair + 1)
                dve.reciprocal(m.o_rec[:, :, :], m.o_raw[:, :, :, DH]).then_inc(m.o_rec_ready, 1)
                dve.wait_ge(m.o_rec_ready, pair + 1)
                dve.tensor_tensor(m.o_norm[:, :, :].rearrange("p u (h e) -> p u h e", h=HEADS),
                                  m.o_raw[:, :, :, 0:DH],
                                  m.o_rec[:, :, :].unsqueeze(3).to_broadcast([P, 2, HEADS, DH]),
                                  ALU.mult).then_inc(m.o_ready, 1)

            normalise(0, ln0)
            for i, f in enumerate(FRONT):
                take(f, 0, fill0 + i, None)
            row_max(0, step0)
            row_max(1, step0 + 1)

            def body(it, last):
                numbers = LAST if last else FULL
                base = fill0 + len(FRONT) + it * PER_BODY
                n0 = step0 + it * STEPS
                for s in range(STEPS + 4):
                    before, after = fills(s, last)
                    if s % 8 == 0 and s < STEPS and not (last and s >= 8):
                        normalise(2 * it + s // 8 + 1, ln0 + 2 * it + s // 8 + 1)
                    for f in before:
                        take(f[0], (s // 8 + 1) % 2, base + numbers[s, 0, f], 8 * it + 2 * f[1])
                    if s + 2 < STEPS or (not last and s < STEPS):
                        row_max(s + 2, n0 + s + 2)
                    for f in after:
                        take(f[0], (s // 8 + 1) % 2, base + numbers[s, 1, f], 8 * it + 2 * f[1])
                    if s % 4 == 0 and 4 <= s <= STEPS:
                        divide(pair0 + 4 * it + s // 4 - 1)

            with dve.Fori(0, BODIES - 1) as it:
                body(it, False)
            body(BODIES - 1, True)

        @block.gpsimd
        def _(pool):
            stage_weights(pool, m, experts, 0)
            stage_weights(pool, m, experts, 1)
            layer_norm_power(pool, m, GT, ln0)
            for g in range(1, GROUPS):
                layer_norm_power(pool, m, GT, ln0 + g)
                if g - 1 < experts.chunks:
                    split_weights(pool, m, experts, g - 1, experts.chunk0 + g - 1)
                    stage_weights(pool, m, experts, g + 1)


EXPERTS = 8
F = 512
FB = F // P
SLOT_TILES = 72
ROUTED_ONE = 40
WSCALE = 64.0
ROUND = 1.5 * 2.0 ** 23
UNROLL = 4
FAR = 1e30
assert SLOT_TILES * P >= 2 * TOKENS + EXPERTS * (P - 1) and ROUTED_ONE * P >= TOKENS + EXPERTS * (P - 1)
assert ROUTED_ONE + TILES == SLOT_TILES and SLOT_TILES % UNROLL == 0


class Region:

    def __init__(self, buffer, at=0):
        self.buffer, self.at = buffer, at

    def take(self, shape, dt=F32):
        n = int(np.prod(shape)) * (2 if dt in (F16, BF16) else 4) // 4
        ap = self.buffer[:, self.at:self.at + n]
        self.at += n
        if dt is not F32:
            ap = ap.bitcast(dt)
        if len(shape) > 1:
            names = " ".join("abcdef"[:len(shape)])
            ap = ap.rearrange(f"p ({names}) -> p {names}", **dict(zip("abcdef", shape)))
        return ap


def flat(ap):
    names = " ".join("abcd"[:len(ap.shape) - 1])
    return ap.rearrange(f"p {names} -> p ({names})") if len(ap.shape) > 2 else ap


def group_of(buffer, g, count=GT):
    return lambda t: flat(buffer[:, bass.ds(count * g + t, 1), :])


def norm_block(nc, m, s, router, logits):
    with nc.Block(no_gpsimd_drain=True) as block:
        @block.vector
        def _(dve):
            def norm(g, par):
                if not isinstance(g, int):
                    dve.wait_ge(s.group_sb, g - 1)
                layer_norm(dve, m, group_of(m.x, g), lambda t: m.xn2[:, par, t, :], GT,
                           m.ln_count + g).then_inc(s.normed, 1)

            def take_logits(g, par):
                dve.wait_ge(s.logit_ps, g + 1)
                dve.tensor_copy(logits[:, bass.ds(GT * g, GT), :],
                                m.out_ps[par][:, 0:GT * EXPERTS].rearrange("p (t e) -> p t e", t=GT))
            norm(0, 0)
            norm(1, 1)
            take_logits(0, 0)
            with dve.Fori(1, GROUPS // 2) as i:
                norm(2 * i, 0)
                take_logits(2 * i - 1, 1)
                norm(2 * i + 1, 1)
                take_logits(2 * i, 0)
            take_logits(GROUPS - 1, 1)

        @block.gpsimd
        def _(pool):
            with pool.Fori(0, GROUPS) as g:
                layer_norm_power(pool, m, GT, m.ln_count + g)

        @block.tensor
        def _(pe):
            turned_ps = (m.pT_ps, m.misc)

            def turn(g, par):
                pe.wait_ge(s.normed, g + 1)
                if not isinstance(g, int):
                    pe.wait_ge(s.group_sb, g - 1)
                for t in range(GT):
                    mm = pe.transpose(turned_ps[par][:, t * P:(t + 1) * P], m.xn2[:, par, t, :], m.ident[:, :])
                mm.then_inc(s.turned, 1)

            def route(g, par):
                pe.wait_ge(s.group_sb, g + 1)
                for t in range(GT):
                    mm = pe.matmul(m.out_ps[par][:, t * EXPERTS:(t + 1) * EXPERTS],
                                   m.xnT2[:, par, t * P:(t + 1) * P], router[:, :],
                                   start=True, stop=True, skip_group_check=True)
                mm.then_inc(s.logit_ps, 1)
            turn(0, 0)
            turn(1, 1)
            route(0, 0)
            with pe.Fori(1, GROUPS // 2) as i:
                turn(2 * i, 0)
                route(2 * i - 1, 1)
                turn(2 * i + 1, 1)
                route(2 * i, 0)
            route(GROUPS - 1, 1)

        @block.scalar
        def _(act):
            turned_ps = (m.pT_ps, m.misc)
            with act.Fori(0, GROUPS // 2) as i:
                for par in range(2):
                    g = 2 * i + par
                    act.wait_ge(s.turned, g + 1)
                    act.activation(m.xnT2[:, par, :], turned_ps[par][:, :], ACT.Copy)
                    act.activation(m.xall[:, bass.ds(GT * g, GT), :], m.xn2[:, par, :, :],
                                   ACT.Copy).then_inc(s.group_sb, 1)
    m.ln_count += GROUPS


def stage_weights(pool, m, c, chunk):
    if chunk < c.chunks:
        n, done = m.stage.shape[-1], c.chunk0 + chunk
        if done >= 2:
            pool.wait_ge(m.split_step, 3 * (done - 1))
        pool.dma_start(m.stage[:, done % 2, :], c.weights[:, chunk * n:(chunk + 1) * n])\
            .then_inc(m.staged[done % 2], 16)


def split_weights(pool, m, c, chunk, done):
    n = m.stage.shape[-1]
    cols = slice(chunk * n, (chunk + 1) * n)
    st = m.stage[:, done % 2, :]
    pool.wait_ge(m.staged[done % 2], 16 * (done // 2 + 1))
    pool.tensor_scalar(st, st, WSCALE, None, ALU.mult).then_inc(m.split_step, 1)
    pool.wait_ge(m.split_step, 3 * done + 1)
    pool.tensor_copy(m.w_hi[:, cols], st).then_inc(m.split_step, 1)
    pool.wait_ge(m.split_step, 3 * done + 2)
    pool.tensor_tensor(m.w_lo[:, cols], st, m.w_hi[:, cols], ALU.subtract).then_inc(m.split_step, 1)


def moe(nc, m, k, c):
    swiglu = k == 1
    CH = 1 if swiglu else 2
    NJ = TILES * CH
    NW = EXPERTS * F
    r = Region(m.big)
    logits = r.take((TILES, EXPERTS))
    work = r.take((TILES, EXPERTS))
    work2 = r.take((TILES, EXPERTS))
    top = r.take((2, TILES))
    first = r.take((2, TILES))
    hot = r.take((TILES, CH, EXPERTS))
    hot_b = r.take((NJ, EXPERTS), BF16)
    cum = [r.take((NJ, EXPERTS)) for _ in range(2)]
    total = r.take((NJ, EXPERTS))
    upto = [r.take((EXPERTS,)) for _ in range(2)]
    tiles_of = r.take((EXPERTS,))
    row0 = r.take((EXPERTS,))
    slot_f = r.take((NJ,))
    slot = r.take((NJ,), I32)
    gate = r.take((2, TILES))
    expo = r.take((TILES, EXPERTS))
    denom = r.take((TILES,))
    tile_hit = r.take((SLOT_TILES, EXPERTS))
    tile_f = r.take((SLOT_TILES,))
    tile_e = r.take((SLOT_TILES,), I32)
    x_row = r.take((UNROLL, D))
    x_hi, x_lo = r.take((2, P), F16), r.take((2, P), F16)
    h_f = r.take((2, F))
    h_act = r.take((2, F))
    h_hi, h_lo = r.take((2, F), F16), r.take((2, F), F16)
    y_row = r.take((UNROLL, D))
    fetched = r.take((8, D))
    shared_y = r.take((TILES, D))
    s = m.s_moe[k]
    norm_block(nc, m, s, c.router, logits)

    with nc.Block(no_gpsimd_drain=True) as block:
        steps = [0]

        @block.vector
        def _(dve):
            def step(ins):
                steps[0] += 1
                ins.then_inc(s.route, 1)
                dve.wait_ge(s.route, steps[0])

            def over_e(ap):
                return ap.unsqueeze(2).to_broadcast([P, TILES, EXPERTS])

            rev = m.rev_index[:, :].unsqueeze(1).to_broadcast([P, TILES, EXPERTS])
            left = logits
            for j in range(CH):
                step(dve.tensor_reduce(top[:, j, :], left, AX_X, ALU.max))
                step(dve.tensor_tensor(work, left, over_e(top[:, j, :]), ALU.is_equal))
                step(dve.tensor_tensor(work, work, rev, ALU.mult))
                step(dve.tensor_reduce(first[:, j, :], work, AX_X, ALU.max))
                step(dve.tensor_tensor(hot[:, :, j, :], rev, over_e(first[:, j, :]), ALU.is_equal))
                if j + 1 < CH:
                    step(dve.scalar_tensor_tensor(out=work2, in0=hot[:, :, j, :], scalar=-FAR, in1=left,
                                                  op0=ALU.mult, op1=ALU.add))
                    left = work2
            dve.tensor_copy(hot_b, hot.rearrange("p a b c -> p (a b) c")).then_inc(s.hot, 1)

            if swiglu:
                dve.tensor_tensor(work2, logits, over_e(top[:, 0, :]), ALU.subtract).then_inc(s.gate_in, 1)
                dve.wait_ge(s.gate_exp, 1)
                step(dve.tensor_reduce(denom, expo, AX_X, ALU.add))
                step(dve.reciprocal(gate[:, 0, :], denom))
                step(dve.tensor_scalar(gate[:, 1, :], hot[:, :, 0, EXPERTS - 1], -2.0, 2.0, ALU.mult, ALU.add))
                step(dve.tensor_tensor(gate[:, 0, :], gate[:, 0, :], gate[:, 1, :], ALU.mult))
            else:
                dve.tensor_tensor(denom, top[:, 1, :], top[:, 0, :], ALU.subtract).then_inc(s.gate_in, 1)
                dve.wait_ge(s.gate_exp, 1)
                step(dve.tensor_scalar(denom, expo[:, :, 0], 1.0, None, ALU.add))
                step(dve.reciprocal(gate[:, 0, :], denom))
                step(dve.tensor_tensor(gate[:, 1, :], gate[:, 0, :], expo[:, :, 0], ALU.mult))

            dve.wait_ge(s.prefix, 1)
            step(dve.tensor_copy(total, m.score[1][:, 0:NJ * EXPERTS].rearrange("p (j e) -> p j e", e=EXPERTS)))
            src, n, at = total, 1, 0
            while n < NJ:
                dst = cum[at]
                dve.tensor_copy(dst[:, 0:n, :], src[:, 0:n, :])
                step(dve.tensor_tensor(dst[:, n:, :], src[:, n:, :], src[:, 0:NJ - n, :], ALU.add))
                src, n, at = dst, 2 * n, 1 - at
            spare = cum[at]
            step(dve.tensor_scalar(tiles_of, src[:, NJ - 1, :], (P - 1) / 2.0, 1.0 / P, ALU.add, ALU.mult))
            step(dve.tensor_scalar(tiles_of, tiles_of, ROUND, None, ALU.add))
            step(dve.tensor_scalar(tiles_of, tiles_of, ROUND, None, ALU.subtract))
            ends, n, at = tiles_of, 1, 0
            while n < EXPERTS:
                dst = upto[at]
                dve.tensor_copy(dst[:, 0:n], ends[:, 0:n])
                step(dve.tensor_tensor(dst[:, n:], ends[:, n:], ends[:, 0:EXPERTS - n], ALU.add))
                ends, n, at = dst, 2 * n, 1 - at
            step(dve.tensor_tensor(row0, ends, tiles_of, ALU.subtract))
            step(dve.tensor_scalar(row0, row0, float(P), None, ALU.mult))
            step(dve.tensor_tensor(spare, src, total, ALU.subtract))
            step(dve.tensor_tensor(spare, spare, m.score[0][:, 0:NJ * EXPERTS]
                                   .rearrange("p (j e) -> p j e", e=EXPERTS), ALU.add))
            step(dve.tensor_tensor(spare, spare, row0.unsqueeze(1).to_broadcast([P, NJ, EXPERTS]), ALU.add))
            step(dve.tensor_tensor(spare, spare, hot.rearrange("p a b c -> p (a b) c"), ALU.mult))
            step(dve.tensor_reduce(slot_f, spare, AX_X, ALU.add))
            step(dve.tensor_copy(slot, slot_f))
            NT = ROUTED_ONE if swiglu else SLOT_TILES
            step(dve.tensor_tensor(tile_hit, m.tile_index[:, :].unsqueeze(2).to_broadcast([P, SLOT_TILES, EXPERTS]),
                                   ends.unsqueeze(1).to_broadcast([P, SLOT_TILES, EXPERTS]), ALU.is_ge))
            step(dve.tensor_reduce(tile_f, tile_hit, AX_X, ALU.add))
            step(dve.tensor_scalar(tile_f, tile_f, float(EXPERTS - 1), None, ALU.min))
            if NT < SLOT_TILES:
                step(dve.memset(tile_f[:, NT:], float(EXPERTS - 1)))
            step(dve.tensor_copy(tile_e, tile_f))

        @block.scalar
        def _(act):
            act.wait_ge(s.gate_in, 1)
            if swiglu:
                act.activation(expo, work2, ACT.Exp).then_inc(s.gate_exp, 1)
            else:
                act.activation(expo[:, :, 0], denom, ACT.Exp).then_inc(s.gate_exp, 1)

        @block.tensor
        def _(pe):
            pe.wait_ge(s.hot, 1)
            pe.matmul(m.score[0][:, 0:NJ * EXPERTS], m.above[:, :], flat(hot_b), start=True, stop=True)
            pe.matmul(m.score[1][:, 0:NJ * EXPERTS], m.ones_b[:, :], flat(hot_b), start=True,
                      stop=True).then_inc(s.prefix, 1)

    h_ps = ((m.score[0], m.score[1]), (m.score[2], m.score[3]))
    x_ps = (m.pT_ps, m.misc)
    with nc.Block(no_gpsimd_drain=True) as block:
        @block.gpsimd
        def _(pool):
            pool.wait_ge(m.zeroed, 16)
            for t in range(TILES):
                for j in range(CH):
                    pool.indirect_dma_start(
                        out=m.sorted_in, out_offset=bass.IndirectOffsetOnAxis(
                            ap=slot[:, t * CH + j:t * CH + j + 1], axis=0),
                        in_=m.xall[:, t, :], in_offset=None).then_inc(s.scattered, 16)
            for u in range(UNROLL):
                pool.wait_ge(s.y_done[u], SLOT_TILES // UNROLL * 16)
            for n in range(NJ):
                if n >= 8:
                    pool.wait_ge(s.added, n - 7)
                pool.indirect_dma_start(
                    out=fetched[:, n % 8, :], out_offset=None, in_=m.sorted_out,
                    in_offset=bass.IndirectOffsetOnAxis(ap=slot[:, n:n + 1], axis=0)).then_inc(s.fetched[n % 8], 16)

        @block.sync
        def _(sp):
            rows = SLOT_TILES * P
            if swiglu:
                sp.dma_start(m.sorted_in[ROUTED_ONE * P:rows, :].rearrange("(t p) d -> p t d", p=P),
                             m.xall[:, :, :]).then_inc(s.shared_in, 16)
                sp.wait_ge(s.shared_in, 16)
            sp.wait_ge(s.scattered, 16 * NJ)

            def load(i, u):
                sp.dma_start(x_row[:, u, :], m.sorted_in[bass.ds(i * P, P), :]).then_inc(s.x_row[u], 16)
            for u in range(UNROLL):
                load(u, u)

            def body(j, more):
                for u in range(UNROLL):
                    i = UNROLL * j + u
                    if more:
                        sp.wait_ge(s.x_turned, i + 1)
                        load(i + UNROLL, u)
                    sp.wait_ge(s.y_row, i + 1)
                    sp.dma_start(m.sorted_out[bass.ds(i * P, P), :], y_row[:, u, :]).then_inc(s.y_done[u], 16)
            with sp.Fori(0, SLOT_TILES // UNROLL - 1) as j:
                body(j, True)
            body(SLOT_TILES // UNROLL - 1, False)
            if swiglu:
                for u in range(UNROLL):
                    sp.wait_ge(s.y_done[u], SLOT_TILES // UNROLL * 16)
                sp.dma_start(shared_y, m.sorted_out[ROUTED_ONE * P:rows, :].rearrange("(t p) d -> p t d", p=P))\
                  .then_inc(s.shared, 16)

        @block.tensor
        def _(pe):
            def expert(i):
                return pe.value_load(tile_e[0:1, bass.ds(i, 1)], min_val=0, max_val=EXPERTS - 1)

            def turn(i, u, par, j):
                pe.wait_ge(s.x_row[u], 16 * (j + 1))
                pe.transpose(x_ps[par][:, 0:P], x_row[:, u, :], m.ident[:, :]).then_inc(s.x_turned, 1)

            def hidden(i, par):
                e = expert(i)
                pe.wait_ge(s.x_split, i + 1)
                for which in range(2 if swiglu else 1):
                    for fb in range(FB):
                        at = e * F + (which * NW + fb * P)
                        o = h_ps[par][which][:, fb * P:(fb + 1) * P]
                        hi, lo = m.w_hi[:, bass.ds(at, P)], m.w_lo[:, bass.ds(at, P)]
                        pe.matmul(o, hi, x_hi[:, par, :], start=(fb == 0), stop=False, skip_group_check=True)
                        pe.matmul(o, hi, x_lo[:, par, :], start=False, stop=False, skip_group_check=True)
                        mm = pe.matmul(o, lo, x_hi[:, par, :], start=False, stop=True, skip_group_check=True)
                        if not swiglu:
                            mm = pe.matmul(o, m.b1_rows[:, bass.ds(e * F + fb * P, P)], m.ones3[:, :],
                                           start=False, stop=True, skip_group_check=True)
                mm.then_inc(s.h_ps, 1)

            def down(i, par):
                e = expert(i)
                pe.wait_ge(s.h_split, i + 1)
                o = m.out_ps[par][:, 0:D]
                for fb in range(FB):
                    at = e * F + ((1 + swiglu) * NW + fb * D)
                    f = slice(fb * P, (fb + 1) * P)
                    hi, lo = m.w_hi[:, bass.ds(at, D)], m.w_lo[:, bass.ds(at, D)]
                    pe.matmul(o, h_hi[:, par, f], hi, start=(fb == 0), stop=False, skip_group_check=True)
                    pe.matmul(o, h_lo[:, par, f], hi, start=False, stop=False, skip_group_check=True)
                    mm = pe.matmul(o, h_hi[:, par, f], lo, start=False, stop=True, skip_group_check=True)
                if not swiglu:
                    mm = pe.matmul(o, m.ones3[:, :], m.b2_rows[:, bass.ds(e * D, D)], start=False, stop=True,
                                   skip_group_check=True)
                mm.then_inc(s.y_ps, 1)

            turn(0, 0, 0, 0)

            def body(j, start, end):
                for u in range(UNROLL):
                    i = UNROLL * j + u
                    if not (end and u == UNROLL - 1):
                        turn(i + 1, (u + 1) % UNROLL, (u + 1) % 2, j + (u + 1) // UNROLL)
                    hidden(i, u % 2)
                    if not (start and u < 2):
                        down(i - 2, u % 2)
            body(0, True, False)
            with pe.Fori(1, SLOT_TILES // UNROLL - 1) as j:
                body(j, False, False)
            body(SLOT_TILES // UNROLL - 1, False, True)
            down(SLOT_TILES - 2, 0)
            down(SLOT_TILES - 1, 1)

        @block.scalar
        def _(act):
            def take_x(i, par):
                act.wait_ge(s.x_turned, i + 1)
                act.activation(x_hi[:, par, :], x_ps[par][:, 0:P], ACT.Copy).then_inc(s.x_hi, 1)

            def activate(i, par):
                act.wait_ge(s.h_ps, i + 1)
                act.wait_ge(s.h_split, i - 1) if not isinstance(i, int) or i > 1 else None
                if swiglu:
                    act.activation(h_act[:, par, :], h_ps[par][1][:, :], ACT.Silu,
                                   scale=1.0 / WSCALE).then_inc(s.h_act, 1)
                else:
                    act.activation(h_f[:, par, :], h_ps[par][0][:, :], ACT.Gelu,
                                   scale=1.0 / WSCALE).then_inc(s.h_act, 1)
            take_x(0, 0)

            def body(j, start, end):
                for u in range(UNROLL):
                    i = UNROLL * j + u
                    if not (end and u == UNROLL - 1):
                        take_x(i + 1, (u + 1) % 2)
                    activate(u if start else i, u % 2)
            body(0, True, False)
            with act.Fori(1, SLOT_TILES // UNROLL - 1) as j:
                body(j, False, False)
            body(SLOT_TILES // UNROLL - 1, False, True)

        @block.vector
        def _(dve):
            def split_x(i, par):
                dve.wait_ge(s.x_hi, i + 1)
                dve.tensor_tensor(x_lo[:, par, :], x_ps[par][:, 0:P], x_hi[:, par, :],
                                  ALU.subtract).then_inc(s.x_split, 1)

            def split_h(i, par):
                dve.wait_ge(s.h_act, i + 1)
                if swiglu:
                    dve.scalar_tensor_tensor(out=h_f[:, par, :], in0=h_ps[par][0][:, :], scalar=1.0 / WSCALE,
                                             in1=h_act[:, par, :], op0=ALU.mult, op1=ALU.mult).then_inc(s.h_f, 1)
                    dve.wait_ge(s.h_f, i + 1)
                dve.tensor_copy(h_hi[:, par, :], h_f[:, par, :]).then_inc(s.h_hi, 1)
                dve.wait_ge(s.h_hi, i + 1)
                dve.tensor_tensor(h_lo[:, par, :], h_f[:, par, :], h_hi[:, par, :],
                                  ALU.subtract).then_inc(s.h_split, 1)

            def take_y(i, u, par, j):
                dve.wait_ge(s.y_ps, i + 1)
                if not isinstance(j, int) or j > 0:
                    dve.wait_ge(s.y_done[u], 16 * j)
                dve.tensor_scalar(y_row[:, u, :], m.out_ps[par][:, 0:D], 1.0 / WSCALE, None,
                                  ALU.mult).then_inc(s.y_row, 1)
            split_x(0, 0)

            def body(j, start, end):
                for u in range(UNROLL):
                    i = UNROLL * j + u
                    if not (end and u == UNROLL - 1):
                        split_x(i + 1, (u + 1) % 2)
                    if not (start and u < 2):
                        take_y(i - 2, (u - 2) % UNROLL, u % 2, j - (u < 2))
                    split_h(i, u % 2)
            body(0, True, False)
            with dve.Fori(1, SLOT_TILES // UNROLL - 1) as j:
                body(j, False, False)
            body(SLOT_TILES // UNROLL - 1, False, True)
            last = SLOT_TILES // UNROLL - 1
            take_y(SLOT_TILES - 2, UNROLL - 2, 0, last)
            take_y(SLOT_TILES - 1, UNROLL - 1, 1, last)
            for n in range(NJ):
                t, j = divmod(n, CH)
                dve.wait_ge(s.fetched[n % 8], 16 * (n // 8 + 1))
                if j:
                    dve.wait_ge(s.added, n)
                dve.scalar_tensor_tensor(out=m.x[:, t, :], in0=fetched[:, n % 8, :], scalar=gate[:, j, t:t + 1],
                                         in1=m.x[:, t, :], op0=ALU.mult, op1=ALU.add).then_inc(s.added, 1)
            if swiglu:
                dve.wait_ge(s.shared, 16)
                dve.wait_ge(s.added, NJ)
                dve.tensor_tensor(m.x[:, :, :], m.x[:, :, :], shared_y, ALU.add)


def load_bias_rows(sp, m, s, bias_f, bias_b, b1, b2):
    n1, n2 = b1.shape[1], b2.shape[1]
    sp.dma_start(bias_f[:, 0, 0:n1], b1).then_inc(s.bias_in, 16)
    sp.dma_start(bias_f[:, 1, 0:n2], b2).then_inc(s.bias_in, 16)
    sp.wait_ge(s.bias_step, BIAS_STEPS)
    sp.wait_ge(s.rows_clear, 1)
    for i in range(3):
        sp.dma_start(m.b1_rows[i:i + 1, 0:n1 * P], bias_b[:, i, 0, 0:n1]).then_inc(s.bias_rows, 16)
        sp.dma_start(m.b2_rows[i:i + 1, 0:n2 * P], bias_b[:, i, 1, 0:n2]).then_inc(s.bias_rows, 16)
    sp.wait_ge(s.bias_rows, 16 * 6)


def clear_bias_rows(dve, m, s, bias_f):
    dve.memset(bias_f[:, 1, EXPERTS:], 0.0).then_inc(s.bias_step, 1)
    dve.memset(m.b1_rows[:, :], 0.0)
    dve.memset(m.b2_rows[:, :], 0.0).then_inc(s.rows_clear, 1)


BIAS_STEPS = 7


def split_bias_rows(pool, m, s, bias_f, bias_b):
    pool.wait_ge(s.bias_step, 1)
    pool.wait_ge(s.bias_in, 32)
    pool.tensor_scalar(bias_f, bias_f, WSCALE, None, ALU.mult).then_inc(s.bias_step, 1)
    n = 2
    for i in range(3):
        pool.wait_ge(s.bias_step, n)
        pool.tensor_copy(bias_b[:, i, :, :], bias_f).then_inc(s.bias_step, 1)
        n += 1
        if i < 2:
            pool.wait_ge(s.bias_step, n)
            pool.tensor_tensor(bias_f, bias_f, bias_b[:, i, :, :], ALU.subtract).then_inc(s.bias_step, 1)
            n += 1
    assert n == BIAS_STEPS


DIAG_BLOCKS = 1024 // P


def diagonal_attention(nc, m):
    s = m.s_diag
    r = Region(m.big)
    wv = r.take((DIAG_BLOCKS, D))
    wo = r.take((DIAG_BLOCKS, D))
    wvo = r.take((D,))
    bout = r.take((D,))
    ctx = r.take((2, GTOK))
    with nc.Block(no_gpsimd_drain=True) as block:
        @block.sync
        def _(sp):
            sp.dma_start(wv, m.d["diag_wvT"].rearrange("p (a b) -> p a b", a=DIAG_BLOCKS)).then_inc(s.weights, 16)
            sp.dma_start(wo, m.d["diag_wout"].rearrange("p (a b) -> p a b", a=DIAG_BLOCKS)).then_inc(s.weights, 16)
            sp.dma_start(bout, m.d["diag_bout"].partition_broadcast(P)).then_inc(s.weights, 16)

            def load(g, par):
                sp.dma_start(ctx[:, par, :], m.ctxT_dram[:, bass.ds(g * GTOK, GTOK)]).then_inc(s.ctx[par], 16)
            load(0, 0)
            load(1, 1)
            with sp.Fori(1, GROUPS // 2) as i:
                for par in range(2):
                    sp.wait_ge(s.y_ps, 2 * i + par - 1)
                    load(2 * i + par, par)

        @block.tensor
        def _(pe):
            pe.wait_ge(s.weights, 48)
            for j in range(DIAG_BLOCKS):
                mm = pe.matmul(m.misc[:, 0:D], wv[:, j, :], wo[:, j, :], start=(j == 0), stop=(j == DIAG_BLOCKS - 1))
            mm.then_inc(s.wvo_ps, 1)
            pe.wait_ge(s.wvo, 1)
            with pe.Fori(0, GROUPS // 2) as i:
                for par in range(2):
                    pe.wait_ge(s.ctx[par], 16 * (i + 1))
                    pe.wait_ge(s.added, 2 * i)
                    for t in range(GT):
                        mm = pe.matmul(m.score[par][:, t * D:(t + 1) * D], ctx[:, par, t * P:(t + 1) * P], wvo,
                                       start=True, stop=True, skip_group_check=True)
                    mm.then_inc(s.y_ps, 1)

        @block.vector
        def _(dve):
            dve.wait_ge(s.wvo_ps, 1)
            dve.tensor_copy(wvo, m.misc[:, 0:D]).then_inc(s.wvo, 1)
            with dve.Fori(0, GROUPS // 2) as i:
                for par in range(2):
                    g = 2 * i + par
                    x = m.x[:, bass.ds(GT * g, GT), :]
                    dve.wait_ge(s.y_ps, g + 1)
                    dve.tensor_tensor(x, x, m.score[par][:, :].rearrange("p (t d) -> p t d", t=GT),
                                      ALU.add).then_inc(s.added, 1)
                    dve.wait_ge(s.added, g + 1)
                    dve.tensor_tensor(x, x, bout.unsqueeze(1).to_broadcast([P, GT, D]), ALU.add)


QMIN, QMAX = -128.0, 127.0
H_COLS = FB * TOKENS


def quantized_ffn(nc, m):
    s = m.s_quant
    q = Region(m.quant)
    wf = q.take((2, F))
    wq = q.take((2, F), BF16)
    b1 = q.take((FB,))
    b2 = q.take((D,))
    ext = q.take((4,))
    ext_all = q.take((4,))
    h_ext = q.take((2, FB * GROUPS))
    h_most = q.take((2,))
    h_all = q.take((2,))
    par_x, par_h = q.take((8,)), q.take((8,))
    w_scale, w_inverse = q.take((2,)), q.take((2,))
    out_scale = q.take((2,))
    xq = m.b1_rows[:, :].rearrange("p (t d) -> p t d", t=TILES)
    xqT = q.take((2, GTOK), BF16)
    late = Region(m.kexp_buffer)
    hq = late.take((2, FB, GTOK), BF16)
    h = m.big[:, 0:H_COLS].rearrange("p (b n) -> p b n", b=FB)

    def parameters(step, dve, ext, par):
        one = lambda i: par[:, i:i + 1]
        step(dve.tensor_tensor(one(0), ext[:, 0:1], ext[:, 1:2], ALU.add))
        step(dve.tensor_scalar(one(0), one(0), 1.0 / 255.0, 1e-8, ALU.mult, ALU.max))
        step(dve.reciprocal(one(4), one(0)))
        step(dve.tensor_tensor(one(1), ext[:, 1:2], one(4), ALU.mult))
        step(dve.tensor_scalar(one(1), one(1), ROUND, None, ALU.add))
        step(dve.tensor_scalar(one(1), one(1), ROUND, QMIN, ALU.subtract, ALU.add))
        step(dve.tensor_scalar(one(1), one(1), QMIN, QMAX, ALU.max, ALU.min))
        dve.tensor_scalar(one(2), one(1), -1.0, QMIN, ALU.mult, ALU.add)
        step(dve.tensor_scalar(one(3), one(1), -1.0, QMAX, ALU.mult, ALU.add))

    with nc.Block(no_gpsimd_drain=True) as block:
        steps = [0]

        @block.sync
        def _(sp):
            sp.dma_start(wf[:, 0, :], m.d["quant_w1"]).then_inc(s.weights, 16)
            sp.dma_start(wf[:, 1, :], m.d["quant_w2"]).then_inc(s.weights, 16)
            sp.dma_start(b1, m.d["quant_b1"]).then_inc(s.weights, 16)
            sp.dma_start(b2, m.d["quant_b2"].partition_broadcast(P)).then_inc(s.weights, 16)

        @block.vector
        def _(dve):
            def step(ins):
                steps[0] += 1
                ins.then_inc(s.step, 1)
                dve.wait_ge(s.step, steps[0])
            with dve.Fori(0, GROUPS) as g:
                layer_norm(dve, m, group_of(m.x, g), group_of(m.xall, g), GT, m.ln_count + g).then_inc(s.normed, 1)
            dve.wait_ge(s.normed, GROUPS)
            dve.wait_ge(s.weights, 64)
            dve.tensor_reduce(ext[:, 0:1], flat(m.xall), AX_X, ALU.max)
            dve.tensor_reduce(ext[:, 1:2], flat(m.xall), AX_X, ALU.min)
            dve.tensor_reduce(ext[:, 2:4], wf, AX_X, ALU.max, apply_absolute_value=True).then_inc(s.step, 1)
            steps[0] += 1
            dve.wait_ge(s.step, steps[0])
            dve.tensor_scalar(ext[:, 1:2], ext[:, 1:2], -1.0, None, ALU.mult).then_inc(s.ext, 1)
            dve.wait_ge(s.ext_all, 1)
            parameters(step, dve, ext_all, par_x)
            step(dve.tensor_scalar(w_scale, ext_all[:, 2:4], 1.0 / QMAX, 1e-8, ALU.mult, ALU.max))
            step(dve.reciprocal(w_inverse, w_scale))
            dve.tensor_tensor(out_scale[:, 0:1], par_x[:, 0:1], w_scale[:, 0:1], ALU.mult)
            for i in range(2):
                step(dve.tensor_scalar(wf[:, i, :], wf[:, i, :], w_inverse[:, i:i + 1], ROUND, ALU.mult, ALU.add))
            step(dve.tensor_scalar(wf, wf, ROUND, -QMAX, ALU.subtract, ALU.max))
            step(dve.tensor_scalar(wq, wf, QMAX, None, ALU.min))
            half = TILES // 2
            for part in range(2):
                x = m.xall[:, part * half:(part + 1) * half, :]
                step(dve.tensor_scalar(x, x, par_x[:, 4:5], ROUND, ALU.mult, ALU.add))
                step(dve.tensor_scalar(x, x, ROUND, par_x[:, 2:3], ALU.subtract, ALU.max))
                step(dve.tensor_scalar(xq[:, part * half:(part + 1) * half, :], x, par_x[:, 3:4], None, ALU.min))

        @block.gpsimd
        def _(pool):
            with pool.Fori(0, GROUPS) as g:
                layer_norm_power(pool, m, GT, m.ln_count + g)
            pool.wait_ge(s.ext, 1)
            pool.partition_all_reduce(ext_all, ext, P, bass.bass_isa.ReduceOp.max).then_inc(s.ext_all, 1)
    m.ln_count += GROUPS

    with nc.Block(no_gpsimd_drain=True) as block:
        @block.tensor
        def _(pe):
            def turn(g, par):
                for t in range(GT):
                    mm = pe.matmul((m.pT_ps, m.misc)[par][:, t * P:(t + 1) * P],
                                   flat(xq[:, bass.ds(GT * g + t, 1), :]), m.ident_b[:, :],
                                   start=True, stop=True, skip_group_check=True)
                mm.then_inc(s.turned, 1)

            def product(g, par):
                pe.wait_ge(s.xqT, g + 1)
                for fb in range(FB):
                    if not isinstance(g, int) or g:
                        pe.wait_ge(s.gelu, FB * g + (fb + 1 - FB))
                    pe.matmul(m.score[fb][:, :], wq[:, 0, fb * P:(fb + 1) * P], xqT[:, par, :],
                              start=True, stop=True).then_inc(s.h_ps, 1)
            turn(0, 0)
            turn(1, 1)
            product(0, 0)
            with pe.Fori(1, GROUPS // 2) as i:
                turn(2 * i, 0)
                product(2 * i - 1, 1)
                turn(2 * i + 1, 1)
                product(2 * i, 0)
            product(GROUPS - 1, 1)

        @block.scalar
        def _(act):
            def take(g, par):
                act.wait_ge(s.turned, g + 1)
                act.activation(xqT[:, par, :], (m.pT_ps, m.misc)[par][:, :], ACT.Copy).then_inc(s.xqT, 1)

            def gelu(g):
                for fb in range(FB):
                    act.wait_ge(s.h_ps, FB * g + fb + 1)
                    act.activation(h[:, fb, bass.ds(GTOK * g, GTOK)], m.score[fb][:, :], ACT.Gelu,
                                   bias=b1[:, fb:fb + 1], scale=out_scale[:, 0:1]).then_inc(s.gelu, 1)
            take(0, 0)
            take(1, 1)
            gelu(0)
            with act.Fori(1, GROUPS // 2) as i:
                take(2 * i, 0)
                gelu(2 * i - 1)
                take(2 * i + 1, 1)
                gelu(2 * i)
            gelu(GROUPS - 1)

        @block.vector
        def _(dve):
            with dve.Fori(0, GROUPS) as g:
                dve.wait_ge(s.gelu, FB * g + FB)
                part = h[:, :, bass.ds(GTOK * g, GTOK)]
                dve.tensor_reduce(h_ext[:, 0, bass.ds(FB * g, FB)], part, AX_X, ALU.max)
                dve.tensor_reduce(h_ext[:, 1, bass.ds(FB * g, FB)], part, AX_X, ALU.min).then_inc(s.h_ext, 1)

    with nc.Block(no_gpsimd_drain=True) as block:
        steps = [0]

        @block.vector
        def _(dve):
            def step(ins):
                steps[0] += 1
                ins.then_inc(s.step2, 1)
                dve.wait_ge(s.step2, steps[0])
            dve.tensor_reduce(h_most[:, 0:1], h_ext[:, 0, :], AX_X, ALU.max)
            step(dve.tensor_reduce(h_most[:, 1:2], h_ext[:, 1, :], AX_X, ALU.min))
            dve.tensor_scalar(h_most[:, 1:2], h_most[:, 1:2], -1.0, None, ALU.mult).then_inc(s.ext, 1)
            dve.wait_ge(s.ext_all, 2)
            parameters(step, dve, h_all, par_h)
            step(dve.tensor_tensor(out_scale[:, 1:2], par_h[:, 0:1], w_scale[:, 1:2], ALU.mult))

            def quantise(g, par):
                part = h[:, :, bass.ds(GTOK * g, GTOK)]
                dve.tensor_scalar(part, part, par_h[:, 4:5], ROUND, ALU.mult, ALU.add).then_inc(s.hq_step, 1)
                dve.wait_ge(s.hq_step, 2 * g + 1)
                dve.tensor_scalar(part, part, ROUND, par_h[:, 2:3], ALU.subtract, ALU.max).then_inc(s.hq_step, 1)
                dve.wait_ge(s.hq_step, 2 * g + 2)
                if not isinstance(g, int):
                    dve.wait_ge(s.y_ps, g - 1)
                dve.tensor_scalar(hq[:, par, :, :], part, par_h[:, 3:4], None, ALU.min).then_inc(s.hq, 1)

            def add(g, par):
                x = m.x[:, bass.ds(GT * g, GT), :]
                dve.wait_ge(s.y_ps, g + 1)
                dve.scalar_tensor_tensor(out=flat(x), in0=m.out_ps[par][:, :], scalar=out_scale[:, 1:2],
                                         in1=flat(x), op0=ALU.mult, op1=ALU.add).then_inc(s.added, 1)
                dve.wait_ge(s.added, g + 1)
                dve.tensor_tensor(x, x, b2.unsqueeze(1).to_broadcast([P, GT, D]), ALU.add)
            quantise(0, 0)
            quantise(1, 1)
            add(0, 0)
            with dve.Fori(1, GROUPS // 2) as i:
                quantise(2 * i, 0)
                add(2 * i - 1, 1)
                quantise(2 * i + 1, 1)
                add(2 * i, 0)
            add(GROUPS - 1, 1)

        @block.gpsimd
        def _(pool):
            pool.wait_ge(s.ext, 2)
            pool.partition_all_reduce(h_all, h_most, P, bass.bass_isa.ReduceOp.max).then_inc(s.ext_all, 1)

        @block.tensor
        def _(pe):
            with pe.Fori(0, GROUPS // 2) as i:
                for par in range(2):
                    g = 2 * i + par
                    pe.wait_ge(s.hq, g + 1)
                    for t in range(GT):
                        for fb in range(FB):
                            mm = pe.matmul(m.out_ps[par][:, t * D:(t + 1) * D], hq[:, par, fb, t * P:(t + 1) * P],
                                           wq[:, 1, fb * D:(fb + 1) * D], start=(fb == 0), stop=(fb == FB - 1),
                                           skip_group_check=True)
                    mm.then_inc(s.y_ps, 1)


F3 = 2 * D
FB3 = F3 // P


def chosen_ffn(nc, m, out):
    s = m.s_chosen
    r = Region(m.big)
    xT_hi, xT_lo = r.take((TOKENS,), F16), r.take((TOKENS,), F16)
    last_T = r.take((B,))
    wp1, wp2 = r.take((D,)), r.take((EXPERTS,))
    bp1, bp2 = r.take((1,)), r.take((EXPERTS,))
    wo, bo = r.take((D,)), r.take((D,))
    nav = r.take((B,))
    logits = r.take((EXPERTS,))
    best = r.take((1,))
    hit = r.take((EXPERTS,))
    first = r.take((1,))
    sel_f = r.take((1,))
    sel = r.take((B,), I32)
    h_f = r.take((2, F3))
    h_hi, h_lo = r.take((2, F3), F16), r.take((2, F3), F16)
    reasoned = r.take((2, P))
    bias_f = r.take((2, F3 * EXPERTS // P))
    bias_b = r.take((3, 2, F3 * EXPERTS // P), BF16)

    with nc.Block(no_gpsimd_drain=True) as block:
        @block.sync
        def _(sp):
            for dst, name in ((wp1, "chosen_wp1"), (wp2, "chosen_wp2"), (bp1, "chosen_bp1"), (wo, "chosen_wo")):
                sp.dma_start(dst, m.d[name]).then_inc(s.weights, 16)
            sp.dma_start(bp2, m.d["chosen_bp2"].partition_broadcast(P)).then_inc(s.weights, 16)
            sp.dma_start(bo, m.d["chosen_bo"].partition_broadcast(P)).then_inc(s.weights, 16)
            load_bias_rows(sp, m, s, bias_f, bias_b, m.d["chosen_b1"], m.d["chosen_b2"])

        @block.vector
        def _(dve):
            clear_bias_rows(dve, m, s, bias_f)

            def norm(g, par):
                if not isinstance(g, int):
                    dve.wait_ge(s.xT_lo, g - 1)
                    dve.wait_ge(s.copied, g - 1)
                layer_norm(dve, m, group_of(m.x, g), lambda t: m.xn2[:, par, t, :], GT,
                           m.ln_count + g).then_inc(s.normed, 1)

            def low(g, par):
                dve.wait_ge(s.xT_hi, g + 1)
                cols = bass.ds(GTOK * g, GTOK)
                dve.tensor_tensor(xT_lo[:, cols], (m.pT_ps, m.misc)[par][:, :], xT_hi[:, cols],
                                  ALU.subtract).then_inc(s.xT_lo, 1)
            norm(0, 0)
            norm(1, 1)
            low(0, 0)
            with dve.Fori(1, GROUPS // 2) as i:
                norm(2 * i, 0)
                low(2 * i - 1, 1)
                norm(2 * i + 1, 1)
                low(2 * i, 0)
            low(GROUPS - 1, 1)

        @block.gpsimd
        def _(pool):
            split_bias_rows(pool, m, s, bias_f, bias_b)
            with pool.Fori(0, GROUPS) as g:
                layer_norm_power(pool, m, GT, m.ln_count + g)

        @block.tensor
        def _(pe):
            with pe.Fori(0, GROUPS // 2) as i:
                for par in range(2):
                    g = 2 * i + par
                    pe.wait_ge(s.normed, g + 1)
                    for t in range(GT):
                        mm = pe.transpose((m.pT_ps, m.misc)[par][:, t * P:(t + 1) * P], m.xn2[:, par, t, :],
                                          m.ident[:, :])
                    mm.then_inc(s.turned, 1)

        @block.scalar
        def _(act):
            with act.Fori(0, GROUPS // 2) as i:
                for par in range(2):
                    g = 2 * i + par
                    turned = (m.pT_ps, m.misc)[par]
                    act.wait_ge(s.turned, g + 1)
                    act.activation(last_T[:, bass.ds(2 * GT * g, 2 * GT)], turned[:, S - 1::S], ACT.Copy)
                    act.activation(xT_hi[:, bass.ds(GTOK * g, GTOK)], turned[:, :], ACT.Copy).then_inc(s.xT_hi, 1)
                    act.activation(m.xall[:, bass.ds(GT * g, GT), :], m.xn2[:, par, :, :],
                                   ACT.Copy).then_inc(s.copied, 1)
    m.ln_count += GROUPS

    with nc.Block(no_gpsimd_drain=True) as block:
        @block.tensor
        def _(pe):
            pe.wait_ge(s.weights, 16 * 6)
            pe.matmul(m.misc[:, 0:B], wp1, last_T, start=True, stop=True).then_inc(s.nav_ps, 1)
            pe.wait_ge(s.nav, 1)
            pe.matmul(m.pT_ps[0:B, 0:EXPERTS], nav, wp2, start=True, stop=True).then_inc(s.nav_ps, 1)
            pe.wait_ge(s.pick, 5)
            pe.matmul(m.misc[0:1, 0:B], sel_f[0:B, :], m.ident[0:B, 0:B], start=True, stop=True).then_inc(s.nav_ps, 1)

        @block.scalar
        def _(act):
            act.wait_ge(s.nav_ps, 1)
            act.activation(nav, m.misc[:, 0:B], ACT.Gelu, bias=bp1).then_inc(s.nav, 1)

        @block.vector
        def _(dve):
            rows = slice(0, B)
            dve.wait_ge(s.nav_ps, 2)
            dve.tensor_tensor(logits[rows, :], m.pT_ps[rows, 0:EXPERTS], bp2[rows, :], ALU.add).then_inc(s.pick, 1)
            dve.wait_ge(s.pick, 1)
            dve.tensor_reduce(best[rows, :], logits[rows, :], AX_X, ALU.max).then_inc(s.pick, 1)
            dve.wait_ge(s.pick, 2)
            dve.scalar_tensor_tensor(out=hit[rows, :], in0=logits[rows, :], scalar=best[rows, 0:1],
                                     in1=m.rev_index[rows, :], op0=ALU.is_equal, op1=ALU.mult).then_inc(s.pick, 1)
            dve.wait_ge(s.pick, 3)
            dve.tensor_reduce(first[rows, :], hit[rows, :], AX_X, ALU.max).then_inc(s.pick, 1)
            dve.wait_ge(s.pick, 4)
            dve.tensor_scalar(sel_f[rows, :], first[rows, :], -1.0, float(EXPERTS), ALU.mult,
                              ALU.add).then_inc(s.pick, 1)
            dve.wait_ge(s.nav_ps, 3)
            dve.tensor_copy(sel[0:1, :], m.misc[0:1, 0:B])

    h_ps, r_ps, y_ps = m.score[0:2], m.score[2:4], m.out_ps
    with nc.Block(no_gpsimd_drain=True) as block:
        @block.tensor
        def _(pe):
            def chosen(i, b):
                return pe.value_load(sel[0:1, bass.ds(2 * i + b, 1)], min_val=0, max_val=EXPERTS - 1)

            def hidden(i, par):
                for b in range(2):
                    e = chosen(i, b)
                    cols = bass.ds(P * i + S * b, S)
                    for fb in range(FB3):
                        o = h_ps[par][:, fb * P + b * S:fb * P + (b + 1) * S]
                        w = bass.ds(e * F3 + fb * P, P)
                        pe.matmul(o, m.w_hi[:, w], xT_hi[:, cols], start=(fb == 0 and b == 0), stop=False,
                                  skip_group_check=True)
                        pe.matmul(o, m.w_hi[:, w], xT_lo[:, cols], start=False, stop=False, skip_group_check=True)
                        pe.matmul(o, m.w_lo[:, w], xT_hi[:, cols], start=False, stop=False, skip_group_check=True)
                        mm = pe.matmul(o, m.b1_rows[:, w], m.ones3[:, 0:S], start=False, stop=True,
                                       skip_group_check=True)
                mm.then_inc(s.h_ps, 1)

            def down(i, par):
                for b in range(2):
                    e = chosen(i, b)
                    if b == 0:
                        pe.wait_ge(s.h_split, i + 1)
                    o = r_ps[par][:, b * S:(b + 1) * S]
                    for fb in range(FB3):
                        w = bass.ds(e * F3 + (EXPERTS * F3 + fb * D), D)
                        f = slice(fb * P + b * S, fb * P + (b + 1) * S)
                        pe.matmul(o, m.w_hi[:, w], h_hi[:, par, f], start=(fb == 0 and b == 0), stop=False,
                                  skip_group_check=True)
                        pe.matmul(o, m.w_hi[:, w], h_lo[:, par, f], start=False, stop=False, skip_group_check=True)
                        pe.matmul(o, m.w_lo[:, w], h_hi[:, par, f], start=False, stop=False, skip_group_check=True)
                    mm = pe.matmul(o, m.b2_rows[:, bass.ds(e * D, D)], m.ones3[:, 0:S], start=False, stop=True,
                                   skip_group_check=True)
                mm.then_inc(s.r_ps, 1)

            def last(i, par):
                pe.wait_ge(s.reasoned, i + 1)
                pe.wait_ge(s.y_free, i + 1)
                pe.matmul(y_ps[par][:, 0:D], reasoned[:, par, :], wo, start=True, stop=True).then_inc(s.y_ps, 1)

            hidden(0, 0)
            hidden(1, 1)
            down(0, 0)
            with pe.Fori(1, TILES // 2) as i:
                hidden(2 * i, 0)
                down(2 * i - 1, 1)
                last(2 * i - 2, 0)
                hidden(2 * i + 1, 1)
                down(2 * i, 0)
                last(2 * i - 1, 1)
            down(TILES - 1, 1)
            last(TILES - 2, 0)
            last(TILES - 1, 1)

        @block.scalar
        def _(act):
            def gelu(i, par):
                act.wait_ge(s.h_ps, i + 1)
                act.activation(h_f[:, par, :], h_ps[par][:, 0:F3], ACT.Gelu, scale=1.0 / WSCALE).then_inc(s.gelu, 1)

            def take(i, par):
                act.wait_ge(s.r_ps, i + 1)
                act.activation(reasoned[:, par, :], r_ps[par][:, 0:P], ACT.Copy,
                               scale=1.0 / WSCALE).then_inc(s.reasoned, 1)
            gelu(0, 0)
            gelu(1, 1)
            take(0, 0)
            with act.Fori(1, TILES // 2) as i:
                gelu(2 * i, 0)
                take(2 * i - 1, 1)
                gelu(2 * i + 1, 1)
                take(2 * i, 0)
            take(TILES - 1, 1)

        @block.vector
        def _(dve):
            def split(i, par):
                dve.wait_ge(s.gelu, i + 1)
                dve.tensor_copy(h_hi[:, par, :], h_f[:, par, :]).then_inc(s.h_hi, 1)
                dve.wait_ge(s.h_hi, i + 1)
                dve.tensor_tensor(h_lo[:, par, :], h_f[:, par, :], h_hi[:, par, :], ALU.subtract)\
                   .then_inc(s.h_split, 1)

            def add(i, par):
                dve.wait_ge(s.y_ps, i + 1)
                xn = flat(m.xall[:, bass.ds(i, 1), :])
                dve.scalar_tensor_tensor(out=xn, in0=y_ps[par][:, 0:D], scalar=0.3, in1=xn, op0=ALU.mult,
                                         op1=ALU.add).then_inc(s.y_free, 1)
            dve.wait_ge(s.weights, 16 * 6)
            dve.tensor_scalar(bo, bo, 0.3, None, ALU.mult).then_inc(s.y_free, 2)
            split(0, 0)
            split(1, 1)
            with dve.Fori(1, TILES // 2) as i:
                split(2 * i, 0)
                add(2 * i - 2, 0)
                split(2 * i + 1, 1)
                add(2 * i - 1, 1)
            add(TILES - 2, 0)
            add(TILES - 1, 1)
            dve.wait_ge(s.y_free, TILES + 2)
            for q in range(4):
                rows = slice(q * TILES // 4, (q + 1) * TILES // 4)
                x = m.x[:, rows, :]
                dve.tensor_tensor(x, x, m.xall[:, rows, :], ALU.add).then_inc(s.final, 1)
                dve.wait_ge(s.final, 2 * q + 1)
                dve.tensor_tensor(x, x, bo.unsqueeze(1).to_broadcast([P, TILES // 4, D]), ALU.add)\
                   .then_inc(s.final, 1)

        @block.sync
        def _(sp):
            for q in range(4):
                rows = slice(q * TILES // 4, (q + 1) * TILES // 4)
                sp.wait_ge(s.final, 2 * q + 2)
                sp.dma_start(out.rearrange("(t p) d -> p t d", p=P)[:, rows, :], m.x[:, rows, :])\
                  .then_inc(m.stored, 16)
            sp.wait_ge(m.stored, 64)


def moe_semaphores(sem, k):
    s = Names()
    s.group_sb = sem(f"moe{k}_group_sb")
    s.normed = sem(f"moe{k}_normed")
    s.logit_ps = sem(f"moe{k}_logit_ps")
    s.turned = sem(f"moe{k}_turned")
    s.route = sem(f"moe{k}_route")
    s.hot = sem(f"moe{k}_hot")
    s.gate_in = sem(f"moe{k}_gate_in")
    s.gate_exp = sem(f"moe{k}_gate_exp")
    s.prefix = sem(f"moe{k}_prefix")
    s.scattered = sem(f"moe{k}_scattered")
    s.added = sem(f"moe{k}_added")
    s.x_turned = sem(f"moe{k}_x_turned")
    s.y_row = sem(f"moe{k}_y_row")
    s.shared = sem(f"moe{k}_shared")
    s.shared_in = sem(f"moe{k}_shared_in")
    s.x_split = sem(f"moe{k}_x_split")
    s.h_ps = sem(f"moe{k}_h_ps")
    s.h_split = sem(f"moe{k}_h_split")
    s.y_ps = sem(f"moe{k}_y_ps")
    s.x_hi = sem(f"moe{k}_x_hi")
    s.h_act = sem(f"moe{k}_h_act")
    s.h_f = sem(f"moe{k}_h_f")
    s.h_hi = sem(f"moe{k}_h_hi")
    s.x_row = [sem(f"moe{k}_x_row{u}") for u in range(UNROLL)]
    s.y_done = [sem(f"moe{k}_y_done{u}") for u in range(UNROLL)]
    s.fetched = [sem(f"moe{k}_fetched{u}") for u in range(8)]
    return s


def bias0_semaphores(sem):
    s = Names()
    s.bias_in = sem("bias0_bias_in")
    s.bias_step = sem("bias0_bias_step")
    s.bias_rows = sem("bias0_bias_rows")
    s.rows_clear = sem("bias0_rows_clear")
    return s


def diag_semaphores(sem):
    s = Names()
    s.weights = sem("diag_weights")
    s.y_ps = sem("diag_y_ps")
    s.wvo_ps = sem("diag_wvo_ps")
    s.wvo = sem("diag_wvo")
    s.added = sem("diag_added")
    s.ctx = [sem("diag_ctx0"), sem("diag_ctx1")]
    return s


def quant_semaphores(sem):
    s = Names()
    s.weights = sem("quant_weights")
    s.step = sem("quant_step")
    s.step2 = sem("quant_step2")
    s.normed = sem("quant_normed")
    s.ext = sem("quant_ext")
    s.ext_all = sem("quant_ext_all")
    s.turned = sem("quant_turned")
    s.xqT = sem("quant_xqT")
    s.h_ps = sem("quant_h_ps")
    s.gelu = sem("quant_gelu")
    s.h_ext = sem("quant_h_ext")
    s.hq_step = sem("quant_hq_step")
    s.hq = sem("quant_hq")
    s.y_ps = sem("quant_y_ps")
    s.added = sem("quant_added")
    return s


def chosen_semaphores(sem):
    s = Names()
    s.weights = sem("chosen_weights")
    s.bias_in = sem("chosen_bias_in")
    s.bias_step = sem("chosen_bias_step")
    s.bias_rows = sem("chosen_bias_rows")
    s.rows_clear = sem("chosen_rows_clear")
    s.xT_lo = sem("chosen_xT_lo")
    s.xT_hi = sem("chosen_xT_hi")
    s.copied = sem("chosen_copied")
    s.normed = sem("chosen_normed")
    s.turned = sem("chosen_turned")
    s.nav_ps = sem("chosen_nav_ps")
    s.nav = sem("chosen_nav")
    s.pick = sem("chosen_pick")
    s.h_ps = sem("chosen_h_ps")
    s.h_split = sem("chosen_h_split")
    s.r_ps = sem("chosen_r_ps")
    s.reasoned = sem("chosen_reasoned")
    s.y_ps = sem("chosen_y_ps")
    s.gelu = sem("chosen_gelu")
    s.h_hi = sem("chosen_h_hi")
    s.y_free = sem("chosen_y_free")
    s.final = sem("chosen_final")
    return s


def build(nc, d, out):
    m = Names()
    m.ln_count = 0
    with ExitStack() as ctx:
        def sb(name, shape, dt=F32):
            return ctx.enter_context(nc.sbuf_tensor(name, shape, dt))

        def ps(name):
            return ctx.enter_context(nc.psum_tensor(name, [P, 512], F32))

        def sem(name):
            return ctx.enter_context(nc.semaphore(name))

        m.d = d
        m.ctxT_dram = d["ctxT"]
        m.x = sb("x", [P, TILES, D])
        m.xn2 = sb("xn", [P, 2, GT, D])
        m.xnT2 = sb("xnT", [P, 2, GTOK])
        m.xn, m.xnT = m.xn2[:, 0, :, :], m.xnT2[:, 0, :]
        m.big = sb("big", [P, 16384])
        m.stage = m.big[:, 0:4096].rearrange("p (a n) -> p a n", a=2)
        m.w_hi = sb("w_hi", [P, 3 * EXPERTS * F], F16)
        m.w_lo = sb("w_lo", [P, 3 * EXPERTS * F], F16)
        m.b1_rows = sb("b1_rows", [P, EXPERTS * F], BF16)
        m.b2_rows = sb("b2_rows", [P, EXPERTS * D], BF16)
        m.ones3 = sb("ones3", [P, P], BF16)
        m.ones_b = sb("ones_b", [P, P], BF16)
        m.above = sb("above", [P, P], BF16)
        m.rev_index = sb("rev_index", [P, EXPERTS])
        m.tile_index = sb("tile_index", [P, SLOT_TILES])
        m.consts_in = sb("consts_in", [P, 3 * P])
        m.sorted_in = nc.dram_tensor("sorted_in", [SLOT_TILES * P, D], F32, kind="Internal").ap()
        m.sorted_out = nc.dram_tensor("sorted_out", [SLOT_TILES * P, D], F32, kind="Internal").ap()
        m.ln_stats = sb("ln_stats", [P, GT, 6])
        m.ln_work = sb("ln_work", [P, 8, GT])
        m.eps = sb("eps", [P, GT])
        m.minus_half = sb("minus_half", [P, GT])
        m.ident = sb("ident", [P, P])
        m.ident_b = sb("ident_b", [P, P], BF16)
        att = Region(m.big, 4096)
        m.ctx = att.take((2, 2 * GT, 2, S))
        m.qbd = att.take((2, 2, GTOK))
        kexp = sb("kexp", [P, 2 * 2 * GT * HQ * S])
        m.kexp_buffer = kexp
        m.quant = sb("quant", [P, 2300])
        m.xall = kexp[:, :].rearrange("p (t d) -> p t d", t=TILES)
        m.kexp = kexp[:, :].rearrange("p (a g t h k) -> p a g t h k", a=2, g=2, t=GT, h=HQ)
        m.v2 = sb("v2", [P, 2, GT, 2, HEADS, DH + 1])
        m.neg_max = sb("neg_max", [P, 4, 2 * HQ], BF16)
        m.prob = att.take((2, 512))
        m.pT = att.take((2, 512))
        m.o_raw = sb("o_raw", [P, 2, HEADS, DH + 1])
        m.o_rec = sb("o_rec", [P, 2, HEADS])
        m.o_norm = sb("o_norm", [P, 2, D])
        m.oT = sb("oT", [P, 2 * P])
        m.batch_mask = sb("batch_mask", [P, GTOK])
        m.head_mask = sb("head_mask", [P, HQ])
        m.value_mask = sb("value_mask", [P, D])
        m.penalty = sb("penalty", [P, TILES, S], BF16)
        m.mask_in = att.take((TILES, S), I32)
        m.score = [ps(f"score{g}") for g in range(4)]
        m.pT_ps = ps("pT_ps")
        m.out_ps = [ps("out_ps0"), ps("out_ps1")]
        m.misc = ps("misc")
        m.xn_ready = sem("xn_ready")
        m.ln_step = sem("ln_step")
        m.ln_eps_added = sem("ln_eps_added")
        m.ln_rstd_ready = sem("ln_rstd_ready")
        m.filled = sem("filled")
        m.emptied = sem("emptied")
        m.scored = sem("scored")
        m.maxed = sem("maxed")
        m.shifted = sem("shifted")
        m.probs = sem("probs")
        m.turned = sem("turned")
        m.turned_out = sem("turned_out")
        m.valued = sem("valued")
        m.o_copied = sem("o_copied")
        m.o_rec_ready = sem("o_rec_ready")
        m.o_ready = sem("o_ready")
        m.consts = sem("consts")
        m.x_in = sem("x_in")
        m.att_w = sem("att_w")
        m.bias_ps = sem("bias_ps")
        m.stored = sem("stored")
        m.zeroed = sem("zeroed")
        m.split_step = sem("split_step")
        m.zero_tile = sem("zero_tile")
        m.staged = [sem("staged0"), sem("staged1")]
        m.s_moe = [moe_semaphores(sem, k) for k in range(2)]
        m.s_bias0 = bias0_semaphores(sem)
        m.s_diag = diag_semaphores(sem)
        m.s_quant = quant_semaphores(sem)
        m.s_chosen = chosen_semaphores(sem)
        moes, chunk0 = [], 0
        for weights, chunks in ((d["moe0_w"], 4), (d["moe1_w"], 6), (d["chosen_w"], 2)):
            c = Names()
            c.weights, c.chunks, c.chunk0 = weights, chunks, chunk0
            chunk0 += chunks
            moes.append(c)
        for k, c in enumerate(moes[0:2]):
            c.router = sb(f"router{k}", [P, EXPERTS])
        m.ctx_loaded = [sem("ctx_loaded0"), sem("ctx_loaded1")]

        ws = []
        for a, layer in enumerate((0, 1, 3)):
            w = Names()
            w.wq = sb(f"wq{a}", [P, 2, P])
            w.wk = sb(f"wk{a}", [P, 2, 2, P])
            w.wv = sb(f"wv{a}", [P, D])
            w.wo = sb(f"wo{a}", [P, D])
            w.bq = sb(f"bq{a}", [P, 2])
            w.bk = sb(f"bk{a}", [P, 2])
            if a:
                w.bv = sb(f"bv{a}", [P, 1])
                w.bo = sb(f"bo{a}", [P, D])
                w.out_bias = sb(f"out_bias{a}", [P, D])
            w.layer = layer
            ws.append(w)

        setup = Region(m.big, att.at)
        bias_f = setup.take((2, 32))
        bias_b = setup.take((3, 2, 32), BF16)
        zero_tile = setup.take((P,))
        with nc.Block(no_gpsimd_drain=True) as block:
            @block.sync
            def _(sp):
                sp.dma_start(m.ident[:, :], d["ident"]).then_inc(m.consts, 16)
                sp.dma_start(m.batch_mask[:, :], d["batch_mask"]).then_inc(m.consts, 16)
                sp.dma_start(m.head_mask[:, :], d["head_mask"]).then_inc(m.consts, 16)
                sp.dma_start(m.value_mask[:, :], d["value_mask"]).then_inc(m.consts, 16)
                sp.dma_start(m.x[:, :, :], d["x"].rearrange("(t p) d -> p t d", p=P)).then_inc(m.x_in, 16)
                sp.dma_start(m.mask_in[:, :, :], d["mask"].rearrange("(t p) k -> p t k", p=P)).then_inc(m.x_in, 16)
                sp.dma_start(m.consts_in[:, :], d["consts"]).then_inc(m.consts, 16)
                sp.dma_start(m.rev_index[:, :], d["rev_index"].partition_broadcast(P)).then_inc(m.consts, 16)
                sp.dma_start(m.tile_index[:, :], d["tile_index"].partition_broadcast(P)).then_inc(m.consts, 16)
                for k, c in enumerate(moes[0:2]):
                    sp.dma_start(c.router[:, :], d[f"router{k}"]).then_inc(m.consts, 16)
                sp.wait_ge(m.zero_tile, 1)
                sp.dma_start(m.sorted_in.rearrange("(t p) d -> p t d", p=P),
                             zero_tile.unsqueeze(1).to_broadcast([P, SLOT_TILES, P])).then_inc(m.zeroed, 16)
                load_bias_rows(sp, m, m.s_bias0, bias_f, bias_b, d["moe0_b1"], d["moe0_b2"])

            @block.scalar
            def _(act):
                for a, w in enumerate(ws):
                    n = w.layer
                    act.dma_start(w.wq[:, :, :], d[f"wq{n}"].rearrange("c (g r) -> c g r", g=2)).then_inc(m.att_w, 16)
                    act.dma_start(w.wk[:, :, :, :], d[f"wk{n}"].rearrange("c (b g r) -> c b g r", g=2, b=2))\
                       .then_inc(m.att_w, 16)
                    act.dma_start(w.wv[:, :], d[f"wv{n}"]).then_inc(m.att_w, 16)
                    act.dma_start(w.wo[:, :], d[f"wo{n}"]).then_inc(m.att_w, 16)
                    if a:
                        act.dma_start(w.bq[:, :], d[f"bq{n}"]).then_inc(m.att_w, 16)
                        act.dma_start(w.bk[:, :], d[f"bk{n}"]).then_inc(m.att_w, 16)
                        act.dma_start(w.bv[:, :], d[f"bv{n}"]).then_inc(m.att_w, 16)
                        act.dma_start(w.bo[:, :], d[f"bo{n}"].partition_broadcast(P)).then_inc(m.att_w, 16)

            @block.tensor
            def _(pe):
                pe.wait_ge(m.att_w, 16 * 20)
                for a, w in enumerate(ws[1:]):
                    mm = pe.matmul(m.misc[:, a * D:(a + 1) * D], w.bv[:, :].to_broadcast([P, P]), w.wo[:, :],
                                   start=True, stop=True, skip_group_check=True)
                mm.then_inc(m.bias_ps, 1)

            @block.gpsimd
            def _(pool):
                split_bias_rows(pool, m, m.s_bias0, bias_f, bias_b)

            @block.vector
            def _(dve):
                dve.memset(m.eps[:, :], EPS)
                dve.memset(m.minus_half[:, :], -0.5)
                dve.memset(ws[0].bq[:, :], 0.0)
                dve.memset(ws[0].bk[:, :], 0.0)
                dve.memset(zero_tile, 0.0).then_inc(m.zero_tile, 1)
                clear_bias_rows(dve, m, m.s_bias0, bias_f)
                dve.wait_ge(m.consts, 64 + 16 * 5)
                dve.tensor_copy(m.ones3[:, :], m.consts_in[:, 0:P])
                dve.tensor_copy(m.ones_b[:, :], m.consts_in[:, P:2 * P])
                dve.tensor_copy(m.above[:, :], m.consts_in[:, 2 * P:3 * P])
                dve.tensor_copy(m.ident_b[:, :], m.ident[:, :])
                for par in range(2):
                    for t in range(GT):
                        dve.tensor_copy(m.v2[:, par, t, :, :, DH],
                                        m.value_mask[:, 0:D:DH].unsqueeze(1).to_broadcast([P, 2, HEADS]))
                dve.wait_ge(m.x_in, 32)
                dve.tensor_scalar(m.penalty[:, :, :], m.mask_in[:, :, :], 0, MASKED, ALU.is_equal, ALU.mult)
                dve.wait_ge(m.bias_ps, 1)
                for a, w in enumerate(ws[1:]):
                    dve.tensor_tensor(w.out_bias[:, :], m.misc[:, a * D:(a + 1) * D], w.bo[:, :], ALU.add)

        attention(nc, m, 0, ws[0], masked=False, biased=False, experts=moes[0])
        moe(nc, m, 0, moes[0])
        attention(nc, m, 1, ws[1], masked=True, biased=True, experts=moes[1])
        quantized_ffn(nc, m)
        diagonal_attention(nc, m)
        moe(nc, m, 1, moes[1])
        attention(nc, m, 2, ws[2], masked=False, biased=True, experts=moes[2])
        chosen_ffn(nc, m, out)


def _layout(i):
    f = {k: np.asarray(v) for k, v in i.items()}
    r = np.arange(P)
    d = {"ident": np.eye(P, dtype=np.float32)}
    d["batch_mask"] = (r[:, None] % 64 // 32 == np.arange(GTOK) // S % 2).astype(np.float32)
    d["head_mask"] = (r[:, None] % 32 // DH == np.arange(HQ)).astype(np.float32)
    d["value_mask"] = (r[:, None] // S == r[None, :] // DH % 2).astype(np.float32)
    d["x"] = f["x"].reshape(TOKENS, D)
    d["ctxT"] = f["ctx_1024"].reshape(TOKENS, D).T
    d["mask"] = f["mask_BxSxS2_ik1"].reshape(TOKENS, S)
    d["consts"] = np.concatenate([np.repeat((r < 3)[:, None], P, 1), np.ones((P, P)), r[:, None] < r[None, :]],
                                 1).astype(np.float32)
    d["rev_index"] = (EXPERTS - np.arange(EXPERTS)).astype(np.float32)
    d["tile_index"] = np.arange(SLOT_TILES).astype(np.float32)
    def up_of(w):
        return w.transpose(1, 0, 2).reshape(D, EXPERTS * F)

    def down_of(w):
        return w.reshape(EXPERTS, FB, P, D).transpose(2, 0, 1, 3).reshape(P, EXPERTS * F)
    d["router0"], d["router1"] = f["L0_ffn_router_w"].T, f["L2_ffn_router_w"]
    d["moe0_w"] = np.concatenate([up_of(f["L0_ffn_w1"].transpose(0, 2, 1)),
                                  down_of(f["L0_ffn_w2"].transpose(0, 2, 1))], 1)
    d["moe0_b1"], d["moe0_b2"] = f["L0_ffn_b1"].reshape(P, -1), f["L0_ffn_b2"].reshape(P, -1)
    both = [np.concatenate([f[f"L2_ffn_{n}_w"], f[f"L2_ffn_shared_{n}_w"][None]]) for n in ("up", "gate", "down")]
    d["moe1_w"] = np.concatenate([up_of(both[0]), up_of(both[1]), down_of(both[2])], 1)
    d["quant_w1"] = f["L1_ffn_W1"].T
    d["quant_w2"] = f["L1_ffn_W2"].T.reshape(FB, P, D).transpose(1, 0, 2).reshape(P, F)
    d["quant_b1"], d["quant_b2"] = f["L1_ffn_b1"].reshape(FB, P).T, f["L1_ffn_b2"]
    wide = DIAG_BLOCKS * P
    d["diag_wvT"] = f["L2_xattn_Wkv"][:, wide:].T.reshape(DIAG_BLOCKS, P, D).transpose(1, 0, 2).reshape(P, -1)
    d["diag_wout"] = f["L2_xattn_Wout"].reshape(DIAG_BLOCKS, P, D).transpose(1, 0, 2).reshape(P, -1)
    d["diag_bout"] = f["L2_xattn_bout"]
    d["chosen_w"] = np.concatenate([f["L3_ffn_W1"].transpose(1, 0, 2).reshape(D, -1),
                                    f["L3_ffn_W2"].reshape(EXPERTS, FB3, P, D).transpose(2, 0, 1, 3).reshape(P, -1)], 1)
    d["chosen_b1"], d["chosen_b2"] = f["L3_ffn_b1"].reshape(P, -1), f["L3_ffn_b2"].reshape(P, -1)
    d["chosen_wp1"], d["chosen_wp2"], d["chosen_wo"] = f["L3_ffn_Wp1"], f["L3_ffn_Wp2"], f["L3_ffn_Wo"]
    d["chosen_bp1"], d["chosen_bp2"], d["chosen_bo"] = f["L3_ffn_bp1"].reshape(P, 1), f["L3_ffn_bp2"], f["L3_ffn_bo"]
    w0 = f["L0_xattn_Wkv"]
    att = {0: (f["L0_xattn_Wq"], w0[:, :D], w0[:, D:], f["L0_xattn_Wout"]),
           1: tuple(f[f"L1_xattn_W{c}"] for c in "qkvo"),
           3: tuple(f[f"L3_xattn_W{c}"].T for c in "qkvo")}
    for n, (wq, wk, wv, wo) in att.items():
        def blocks(w):
            return w.reshape(-1, 2, 2, 32)
        d[f"wq{n}"] = np.stack([blocks(wq)] * 2, axis=3).reshape(D, 2 * P)
        k, z = blocks(wk), np.zeros_like(blocks(wk))
        d[f"wk{n}"] = np.stack([np.stack([k, z], 3), np.stack([z, k], 3)], 1).reshape(D, 4 * P)
        d[f"wv{n}"], d[f"wo{n}"] = wv, wo
        if n:
            for c in "qk":
                b = f[f"L{n}_xattn_b{c}"].reshape(2, 2, 32)
                d[f"b{c}{n}"] = np.stack([b] * 2, axis=2).reshape(2, P).T
            d[f"bv{n}"] = f[f"L{n}_xattn_bv"].reshape(D, 1)
            d[f"bo{n}"] = f[f"L{n}_xattn_bo"]
    return {k: np.ascontiguousarray(v) for k, v in d.items()}


def kernel(**inputs):
    import concourse.bacc as bacc
    from concourse.bass_utils import run_bass_kernel_spmd

    nc = bacc.Bacc("TRN2", target_bir_lowering=False, num_devices=1)
    arrays = _layout(inputs)
    d = {k: nc.dram_tensor(f"in_{k}", v.shape, mybir.dt.from_np(v.dtype), kind="ExternalInput").ap()
         for k, v in arrays.items()}
    out = nc.dram_tensor("out", (TOKENS, D), F32, kind="ExternalOutput").ap()
    build(nc, d, out)
    r = run_bass_kernel_spmd(nc, [{f"in_{k}": v for k, v in arrays.items()}], core_ids=[0])
    return r.results[0]["out"].reshape(B, S, D)
```

```python
from contextlib import ExitStack

import numpy as np
import concourse.bass as bass
from concourse import mybir

ALU = mybir.AluOpType
ACT = mybir.ActivationFunctionType
AX_X = mybir.AxisListType.X
F32 = mybir.dt.float32
BF16 = mybir.dt.bfloat16
F16 = mybir.dt.float16
I32 = mybir.dt.int32

P = 128
D = 128
B, S = 64, 64
TOKENS = B * S
TILES = TOKENS // P
GT = 4
GROUPS = TILES // GT
GTOK = GT * P
HEADS = 16
DH = D // HEADS
HQ = 32 // DH
ATT_SCALE = float(DH) ** -0.5
EPS = 1e-5
MASKED = -float(2 ** 31)
STEPS = 16


class Names:
    pass


LN_STEPS = 4


def group_statistics(dve, m, g, par, done):
    n0 = LN_STEPS * done
    stats, work = m.ln_stats[:, par, :, :], m.ln_work[:, par, :, :]
    even_mean, even_m2, odd_mean, odd_m2 = (stats[:, :, i] for i in (1, 2, 4, 5))
    both, diff, m2, sq, mean, var = (work[:, i, :] for i in range(6))
    for t in range(GT):
        last = dve.bn_stats(stats[:, t, :], flat(m.x[:, bass.ds(GT * g + t, 1), :]))
    last.then_inc(m.ln_step, 1)
    dve.wait_ge(m.ln_step, n0 + 1)
    dve.tensor_tensor(both, even_mean, odd_mean, ALU.add)
    dve.tensor_tensor(diff, even_mean, odd_mean, ALU.subtract)
    dve.tensor_tensor(m2, even_m2, odd_m2, ALU.add).then_inc(m.ln_step, 1)
    dve.wait_ge(m.ln_step, n0 + 2)
    dve.scalar_tensor_tensor(out=sq, in0=diff, scalar=0.25, in1=diff, op0=ALU.mult, op1=ALU.mult)
    dve.tensor_scalar(mean, both, 0.5, None, ALU.mult).then_inc(m.ln_step, 1)
    dve.wait_ge(m.ln_step, n0 + 3)
    dve.scalar_tensor_tensor(out=var, in0=m2, scalar=1.0 / D, in1=sq, op0=ALU.mult,
                             op1=ALU.add).then_inc(m.ln_step, 1)


def group_power(pool, m, par, done):
    pool.wait_ge(m.ln_step, LN_STEPS * (done + 1))
    pool.tensor_tensor(m.ln_work[:, par, 6, :], m.ln_work[:, par, 5, :], m.eps[:, 0:GT],
                       ALU.add).then_inc(m.ln_eps_added, 1)
    pool.wait_ge(m.ln_eps_added, done + 1)
    pool.tensor_tensor(m.ln_work[:, par, 7, :], m.ln_work[:, par, 6, :], m.minus_half[:, 0:GT],
                       ALU.pow).then_inc(m.ln_rstd_ready, 1)


def group_normalise(dve, m, g, par, out, done):
    dve.wait_ge(m.ln_rstd_ready, done + 1)
    for t in range(GT):
        last = dve.tensor_scalar(out(t), flat(m.x[:, bass.ds(GT * g + t, 1), :]), m.ln_work[:, par, 4, t:t + 1],
                                 m.ln_work[:, par, 7, t:t + 1], ALU.subtract, ALU.mult)
    return last


def whole_statistics(dve, m, done):
    n0 = LN_STEPS * done
    m.ln_count += GROUPS
    m.whole_count += 1
    even_mean, even_m2, odd_mean, odd_m2 = (m.whole_stats[:, :, i] for i in (1, 2, 4, 5))
    both, diff, m2, sq, mean, var = (m.whole_work[:, i, :] for i in range(6))
    for t in range(TILES):
        last = dve.bn_stats(m.whole_stats[:, t, :], m.x[:, t, :])
    last.then_inc(m.whole_rows, 1)
    dve.wait_ge(m.whole_rows, m.whole_count)
    dve.tensor_tensor(both, even_mean, odd_mean, ALU.add)
    dve.tensor_tensor(diff, even_mean, odd_mean, ALU.subtract)
    dve.tensor_tensor(m2, even_m2, odd_m2, ALU.add).then_inc(m.ln_step, 1)
    dve.wait_ge(m.ln_step, n0 + 1)
    dve.scalar_tensor_tensor(out=sq, in0=diff, scalar=0.25, in1=diff, op0=ALU.mult, op1=ALU.mult)
    dve.tensor_scalar(mean, both, 0.5, None, ALU.mult).then_inc(m.ln_step, 1)
    dve.wait_ge(m.ln_step, n0 + 2)
    dve.scalar_tensor_tensor(out=var, in0=m2, scalar=1.0 / D, in1=sq, op0=ALU.mult,
                             op1=ALU.add).then_inc(m.ln_step, LN_STEPS * GROUPS - 2)


def whole_power(pool, m, done):
    pool.wait_ge(m.ln_step, LN_STEPS * (done + GROUPS))
    pool.tensor_tensor(m.whole_work[:, 6, :], m.whole_work[:, 5, :], m.eps[:, :], ALU.add)\
        .then_inc(m.ln_eps_added, GROUPS)
    pool.wait_ge(m.ln_eps_added, done + GROUPS)
    for g in range(GROUPS):
        tiles = slice(g * GT, (g + 1) * GT)
        pool.tensor_tensor(m.whole_work[:, 7, tiles], m.whole_work[:, 6, tiles], m.minus_half[:, tiles],
                           ALU.pow).then_inc(m.ln_rstd_ready, 1)


def normalise(dve, m, g, done, out):
    dve.wait_ge(m.ln_rstd_ready, done + g + 1)
    for t in range(GT):
        at = bass.ds(GT * g + t, 1)
        last = dve.tensor_scalar(out(t), flat(m.x[:, at, :]), m.whole_work[:, 4, at], m.whole_work[:, 7, at],
                                 ALU.subtract, ALU.mult)
    return last


FRONT = ("xT", "Q0", "Q1", "K", "V0", "V1")
FRONT_STEPS = (1, 2, 3, 4, 6, 7)


def fills(step, first, last):
    j, before, after = step % 8, [], []
    for k in range(0 if first else -1, 4 if last else 3):
        if step == 4 * k + 6:
            before.append(("OT", k))
        if step == 4 * k + 7:
            before.append(("Y", k))
    if step < STEPS and not (last and step >= 8) and j in FRONT_STEPS:
        after.append((FRONT[FRONT_STEPS.index(j)], 0))
    return before, after


def fill_numbers(first, last):
    n, numbers = 0, {}
    for step in steps_of(last):
        for where, part in enumerate(fills(step, first, last)):
            for f in part:
                numbers[step, where, f] = n
                n += 1
    return numbers, n


def steps_of(last):
    return range(STEPS + 4 if last else STEPS)


BODIES = GROUPS // 2
NUMBERS = {(first, last): fill_numbers(first, last)[0] for first, last in ((True, False), (False, False), (False, True))}
PER_FIRST, PER_BODY, PER_LAST = (fill_numbers(*which)[1] for which in ((True, False), (False, False), (False, True)))
FILLS = len(FRONT) + PER_FIRST + (BODIES - 2) * PER_BODY + PER_LAST


def fills_before(it):
    if isinstance(it, int) and it == 0:
        return len(FRONT)
    return (it * PER_BODY) + (len(FRONT) + PER_FIRST - PER_BODY)


ATT_STEPS = GROUPS * 8


def load_attention_weights(queue, m, w, biased):
    d, n = m.d, w.layer
    queue.dma_start(w.wq[:, :, :], d[f"wq{n}"].rearrange("c (g r) -> c g r", g=2)).then_inc(m.att_w, 16)
    queue.dma_start(w.wk[:, :, :, :], d[f"wk{n}"].rearrange("c (b g r) -> c b g r", g=2, b=2)).then_inc(m.att_w, 16)
    queue.dma_start(w.wv[:, :], d[f"wv{n}"]).then_inc(m.att_w, 16)
    queue.dma_start(w.wo[:, :], d[f"wo{n}"]).then_inc(m.att_w, 16)
    if biased:
        queue.dma_start(w.bq[:, :], d[f"bq{n}"]).then_inc(m.att_w, 16)
        queue.dma_start(w.bk[:, :], d[f"bk{n}"]).then_inc(m.att_w, 16)
        queue.dma_start(w.bv[:, :], d[f"bv{n}"]).then_inc(m.att_w, 16)
        queue.dma_start(w.bo[:, :], d[f"bo{n}"].partition_broadcast(P)).then_inc(m.att_w, 16)


def attention(nc, m, a, w, masked, biased, experts, later=None, fetch=None):
    fill0, step0, ln0, ctx0 = a * FILLS, a * ATT_STEPS, m.ln_count, a * GROUPS
    pair0 = a * 2 * GROUPS
    ctx_dma0 = a * 32 * GROUPS // 2
    m.ln_count += GROUPS
    with nc.Block(no_gpsimd_drain=True) as block:

        @block.sync
        def _(sp):
            def load_ctx(g, par):
                for copy in range(2):
                    sp.dma_start(m.ctx[:, par, :, copy, :], m.ctxT_dram[:, bass.ds(g * GTOK, GTOK)]
                                 .rearrange("d (c k) -> d c k", k=S)).then_inc(m.ctx_loaded[par], 16)
            load_ctx(0, 0)
            load_ctx(1, 1)
            if later:
                later.loads(sp)
            sp.wait_ge(m.filled, fill0 + len(FRONT))
            load_ctx(2, 0)

            def body(it, first, more):
                base = fill0 + fills_before(it)
                numbers = NUMBERS[first, False]
                sp.wait_ge(m.filled, base + (numbers[7, 1, ("V1", 0)] + 1))
                load_ctx(2 * it + 3, 1)
                if more:
                    sp.wait_ge(m.filled, base + (numbers[15, 1, ("V1", 0)] + 1))
                    load_ctx(2 * it + 4, 0)
            body(0, True, True)
            with sp.Fori(1, BODIES - 2) as it:
                body(it, False, True)
            body(BODIES - 2, False, False)
            if later:
                later.rows(sp)

        @block.tensor
        def _(pe):
            def front(f, par):
                if f == "xT":
                    for t in range(GT):
                        mm = pe.transpose(m.misc[:, t * P:(t + 1) * P], m.xn[:, t, :], m.ident[:, :])
                elif f in ("Q0", "Q1"):
                    mm = pe.matmul(m.misc[:, :], w.wq[:, int(f[1]), :], m.xnT[:, :], start=True, stop=True)
                elif f == "K":
                    for gp in range(2):
                        for b in range(2):
                            mm = pe.matmul(m.misc[:, gp * 256:(gp + 1) * 256], w.wk[:, b, gp, :],
                                           m.ctx[:, par, b::2, 0, :], start=(gp == 0 and b == 0),
                                           stop=(b == 1), skip_group_check=True)
                else:
                    for u in range(2):
                        for b in range(2):
                            c = (2 * u + b) * D
                            lhsT = m.ctx[:, par, 4 * int(f[1]) + 2 * u + b, :, :].rearrange("p c k -> p (c k)")
                            mm = pe.matmul(m.misc[:, c:c + D], lhsT, w.wv[:, :], start=True, stop=True,
                                           skip_group_check=True)
                mm.then_inc(m.filled, 1)

            def front_wait(f, par, g_expr, ctx_count, n):
                pe.wait_ge(m.emptied, n)
                if f == "xT":
                    pe.wait_ge(m.xn_ready, ctx0 + g_expr + 1)
                if f == "K":
                    pe.wait_ge(m.ctx_loaded[par], ctx_count)

            def out_part(kind, n, pair):
                pe.wait_ge(m.emptied, n)
                if kind == "OT":
                    pe.wait_ge(m.o_ready, pair + 1)
                    for u in range(2):
                        mm = pe.transpose(m.misc[:, u * P:(u + 1) * P], m.o_norm[:, u, :], m.ident[:, :])
                else:
                    for u in range(2):
                        mm = pe.matmul(m.misc[:, u * D:(u + 1) * D], m.oT[:, u * P:(u + 1) * P], w.wo[:, :],
                                       start=True, stop=True, skip_group_check=True)
                mm.then_inc(m.filled, 1)

            def scores(s, tile, par, ready):
                q, g = s // 4 % 2, s % 4
                if ready is not None:
                    pe.wait_ge(m.emptied, ready)
                rows = slice(64 * (g % 2), 64 * (g % 2) + 64)
                for u in range(2):
                    t = 2 * q + u
                    mm = pe.matmul(m.score[g][:, u * 256:(u + 1) * 256],
                                   m.qbd[rows, par, g // 2, t * P:(t + 1) * P],
                                   m.kexp[rows, par, g // 2, t, :, :].rearrange("p h k -> p (h k)"),
                                   start=(u == 0), stop=True, skip_group_check=True)
                if masked:
                    mm = pe.matmul(m.score[g][:, :], m.ident_b[:, :],
                                   m.penalty[:, bass.ds(tile, 2), :].unsqueeze(2).to_broadcast([P, 2, HQ, S]),
                                   start=False, stop=True, skip_group_check=True)
                mm.then_inc(m.scored, 1)

            def shift(s, n):
                pe.wait_ge(m.maxed, n + 1)
                pe.matmul(m.score[s % 4][:, :], m.ident_b[:, :],
                          m.neg_max[:, s % 4, :].unsqueeze(2).to_broadcast([P, 2 * HQ, S]),
                          start=False, stop=True, skip_group_check=True).then_inc(m.shifted, 1)

            def turn(s, n):
                pe.wait_ge(m.probs, n + 1)
                pe.wait_ge(m.turned_out, n)
                for x in range(4):
                    mm = pe.transpose(m.pT_ps[:, x * P:(x + 1) * P], m.prob[:, s % 2, x * P:(x + 1) * P],
                                      m.ident[:, :])
                mm.then_inc(m.turned, 1)

            def values(s, n, par, pair, ready):
                q, g = s // 4 % 2, s % 4
                pe.wait_ge(m.turned_out, n + 1)
                if s % 8 == 0:
                    pe.wait_ge(m.emptied, ready)
                if g == 0:
                    pe.wait_ge(m.o_copied, pair)
                for u in range(2):
                    for x in range(2):
                        slot = 2 * g + x
                        mm = pe.matmul(m.out_ps[u][:, slot * 36:(slot + 1) * 36],
                                       m.pT[:, s % 2, (2 * u + x) * P:(2 * u + x + 1) * P],
                                       m.v2[:, par, 2 * q + u, :, 2 * slot:2 * slot + 2, :]
                                       .rearrange("p b h e -> p b (h e)"),
                                       start=True, stop=True, skip_group_check=True)
                mm.then_inc(m.valued, 1)

            for i, f in enumerate(FRONT):
                front_wait(f, 0, 0, ctx_dma0 + 32, fill0 + i)
                front(f, 0)
            scores(0, 0, 0, fill0 + len(FRONT))
            scores(1, 0, 0, None)
            shift(0, step0)

            def body(it, first, last):
                numbers = NUMBERS[first, last]
                base = fill0 + fills_before(it)
                n0 = step0 + it * STEPS
                for s in steps_of(last):
                    for where, part in enumerate(fills(s, first, last)):
                        if where == 1:
                            if s + 2 < STEPS or not last:
                                t = s + 2
                                scores(t, 8 * it + 2 * (t // 4), t // 8 % 2,
                                       base + (numbers[t - 4, 1, ("K", 0)] + 1) if t % 8 == 0 else None)
                            if s + 1 < STEPS or not last:
                                shift(s + 1, n0 + s + 1)
                            if s < STEPS:
                                turn(s, n0 + s)
                        for f in part:
                            n = base + numbers[s, where, f]
                            if f[0] in ("OT", "Y"):
                                out_part(f[0], n, pair0 + 4 * it + f[1])
                            else:
                                par = (s // 8 + 1) % 2
                                front_wait(f[0], par, 2 * it + s // 8 + 1,
                                           ctx_dma0 + 32 * (it + 1 + s // 8), n)
                                front(f[0], par)
                    if (s or not first) and s <= STEPS:
                        values(s - 1, n0 + (s - 1), (s - 1) // 8 % 2, pair0 + 4 * it + (s - 1) // 4,
                               base if s == 1 else base + (numbers[7, 1, ("V1", 0)] + 1))

            body(0, True, False)
            with pe.Fori(1, BODIES - 1) as it:
                body(it, False, False)
            body(BODIES - 1, False, True)
            if later:
                later.products(pe)

        @block.scalar
        def _(act):
            def take(f, n):
                if f == "xT":
                    act.wait_ge(m.filled, n + 1)
                    act.activation(m.xnT[:, :], m.misc[:, :], ACT.Copy).then_inc(m.emptied, 1)
                if f == "OT":
                    act.wait_ge(m.filled, n + 1)
                    act.activation(m.oT[:, :], m.misc[:, 0:2 * P], ACT.Copy).then_inc(m.emptied, 1)

            def take_keys(n, par, gp):
                act.wait_ge(m.filled, n + 1)
                for h in range(HQ):
                    last = act.activation(
                        m.kexp[:, par, gp, :, h, :],
                        m.misc[:, gp * 256:(gp + 1) * 256].rearrange("p (t k) -> p t k", t=GT),
                        ACT.Identity, bias=w.bk_heads[:, gp, h:h + 1], scale=m.head_mask[:, h:h + 1])
                if gp == 1:
                    last.then_inc(m.emptied, 1)

            def exp(s, n):
                act.wait_ge(m.shifted, n + 1)
                act.activation(m.prob[:, s % 2, :], m.score[s % 4][:, :], ACT.Exp,
                               scale=ATT_SCALE).then_inc(m.probs, 1)

            def take_turned(s, n):
                act.wait_ge(m.turned, n + 1)
                act.activation(m.pT[:, s % 2, :], m.pT_ps[:, :], ACT.Copy).then_inc(m.turned_out, 1)

            def copy_out(pair):
                act.wait_ge(m.valued, pair * 4 + 4)
                act.wait_ge(m.o_ready, pair)
                for u in range(2):
                    for b in range(2):
                        rows = slice(64 * b, 64 * b + 64)
                        last = act.activation(
                            m.o_raw[rows, u, :, :].rearrange("p (s h) e -> p s (h e)", h=2),
                            m.out_ps[u][rows, 0:288].rearrange("p (s b e) -> p s b e", b=2, e=18)[:, :, b, :],
                            ACT.Copy)
                last.then_inc(m.o_copied, 1)

            take("xT", fill0)
            for gp in range(2):
                take_keys(fill0 + FRONT.index("K"), 0, gp)
            exp(0, step0)

            def body(it, first, last):
                numbers = NUMBERS[first, last]
                base = fill0 + fills_before(it)
                n0 = step0 + it * STEPS
                for s in steps_of(last):
                    before, after = fills(s, first, last)
                    for f in before:
                        take(f[0], base + numbers[s, 0, f])
                    if s + 1 < STEPS or not last:
                        exp(s + 1, n0 + s + 1)
                    if s < STEPS:
                        take_turned(s, n0 + s)
                    for f in after:
                        take(f[0], base + numbers[s, 1, f])
                    keys = FRONT_STEPS[FRONT.index("K")]
                    if s % 8 in (keys, keys + 1) and s < STEPS and not (last and s >= 8):
                        half = s % 8 - keys
                        take_keys(base + numbers[s - half, 1, ("K", 0)], (s // 8 + 1) % 2, half)
                    if s % 4 == 0 and (s or not first) and s <= STEPS:
                        copy_out(pair0 + 4 * it + s // 4 - 1)

            body(0, True, False)
            with act.Fori(1, BODIES - 1) as it:
                body(it, False, False)
            body(BODIES - 1, False, True)

        @block.vector
        def _(dve):
            def normalise(g, par):
                group_normalise(dve, m, g, par, lambda t: m.xn[:, t, :], ln0 + g).then_inc(m.xn_ready, 1)

            def take(f, par, n, tile):
                if f in ("xT", "OT", "K"):
                    return
                dve.wait_ge(m.filled, n + 1)
                if f in ("Q0", "Q1"):
                    gp = int(f[1])
                    last = dve.scalar_tensor_tensor(
                        out=m.qbd[:, par, gp, :], in0=m.misc[:, :], scalar=w.bq[:, gp:gp + 1],
                        in1=m.batch_mask[:, :], op0=ALU.add, op1=ALU.mult)
                elif f in ("V0", "V1"):
                    t = 2 * int(f[1])
                    last = dve.tensor_tensor(
                        m.v2[:, par, t:t + 2, :, :, 0:DH].rearrange("p t b h e -> p (t b) h e"),
                        m.misc[:, :].rearrange("p (c h e) -> p c h e", c=4, h=HEADS),
                        m.value_mask[:, :].rearrange("p (h e) -> p h e", h=HEADS).unsqueeze(1)
                        .to_broadcast([P, 4, HEADS, DH]), ALU.mult)
                else:
                    xs = m.x[:, bass.ds(tile, 2), :]
                    last = dve.tensor_tensor(xs, xs, m.misc[:, 0:2 * D].rearrange("p (t d) -> p t d", t=2), ALU.add)
                last.then_inc(m.emptied, 1)
                if f == "Y" and biased:
                    dve.wait_ge(m.emptied, n + 1)
                    dve.tensor_tensor(xs, xs, w.out_bias[:, :].unsqueeze(1).to_broadcast([P, 2, D]), ALU.add)

            def row_max(s, n):
                dve.wait_ge(m.scored, n + 1)
                dve.tensor_reduce(m.neg_max[:, s % 4, :], m.score[s % 4][:, :].rearrange("p (h k) -> p h k", k=S),
                                  AX_X, ALU.max, negate=True).then_inc(m.maxed, 1)

            def divide(pair):
                dve.wait_ge(m.o_copied, pair + 1)
                dve.reciprocal(m.o_rec[:, :, :], m.o_raw[:, :, :, DH]).then_inc(m.o_rec_ready, 1)
                dve.wait_ge(m.o_rec_ready, pair + 1)
                dve.tensor_tensor(m.o_norm[:, :, :].rearrange("p u (h e) -> p u h e", h=HEADS),
                                  m.o_raw[:, :, :, 0:DH],
                                  m.o_rec[:, :, :].unsqueeze(3).to_broadcast([P, 2, HEADS, DH]),
                                  ALU.mult).then_inc(m.o_ready, 1)

            if fetch:
                dve.wait_ge(fetch.s.y_row, SLOT_TILES)
            for g in range(2):
                if fetch:
                    add_rows(dve, m, fetch, g, (0, g))
                group_statistics(dve, m, g, g, ln0 + g)
            normalise(0, 0)
            for i, f in enumerate(FRONT):
                take(f, 0, fill0 + i, None)
            row_max(0, step0)
            row_max(1, step0 + 1)

            def body(it, first, last):
                numbers = NUMBERS[first, last]
                base = fill0 + fills_before(it)
                n0 = step0 + it * STEPS
                for s in steps_of(last):
                    before, after = fills(s, first, last)
                    if s % 8 == 0 and s < STEPS and not (last and s >= 8):
                        normalise(2 * it + s // 8 + 1, (s // 8 + 1) % 2)
                    if s % 8 == 4 and not last:
                        g = 2 * it + s // 8 + 2
                        if later and first and s == 4:
                            dve.wait_ge(m.x_in, 32)
                        if fetch:
                            add_rows(dve, m, fetch, g, (it + 1, s // 8))
                    for f in before:
                        take(f[0], (s // 8 + 1) % 2, base + numbers[s, 0, f], 8 * it + 2 * f[1])
                    if s + 2 < STEPS or not last:
                        row_max(s + 2, n0 + s + 2)
                    if s % 8 == 4 and not last:
                        group_statistics(dve, m, g, s // 8, ln0 + g)
                    for f in after:
                        take(f[0], (s // 8 + 1) % 2, base + numbers[s, 1, f], 8 * it + 2 * f[1])
                    if s % 4 == 0 and (s or not first) and s <= STEPS:
                        divide(pair0 + 4 * it + s // 4 - 1)

            body(0, True, False)
            if later:
                later.constants(dve)
            with dve.Fori(1, BODIES - 1) as it:
                body(it, False, False)
            body(BODIES - 1, False, True)
            if later:
                later.biases(dve)

        @block.gpsimd
        def _(pool):
            if fetch:
                for u in range(UNROLL):
                    pool.wait_ge(fetch.s.y_done[u], fetch.stored)
                fetch_rows(pool, m, fetch, 0)
            stage_weights(pool, m, experts, 0)
            stage_weights(pool, m, experts, 1)
            group_power(pool, m, 0, ln0)
            for g in range(1, GROUPS):
                if fetch:
                    fetch_rows(pool, m, fetch, g)
                group_power(pool, m, g % 2, ln0 + g)
                if later and g == experts.chunks + 1:
                    later.split(pool)
                if g - 1 < experts.chunks:
                    split_weights(pool, m, experts, g - 1, experts.chunk0 + g - 1)
                    stage_weights(pool, m, experts, g + 1)


EXPERTS = 8
F = 512
FB = F // P
SLOT_TILES = 72
ROUTED_ONE = 40
WSCALE = 64.0
ROUND = 1.5 * 2.0 ** 23
UNROLL = 4
KEPT_AT = 13200
BODIES_MOE = SLOT_TILES // UNROLL
LAG = 2
FAR = 1e30
assert SLOT_TILES * P >= 2 * TOKENS + EXPERTS * (P - 1) and ROUTED_ONE * P >= TOKENS + EXPERTS * (P - 1)
assert ROUTED_ONE + TILES == SLOT_TILES and SLOT_TILES % UNROLL == 0


class Region:

    def __init__(self, buffer, at=0):
        self.buffer, self.at = buffer, at

    def take(self, shape, dt=F32):
        n = int(np.prod(shape)) * (2 if dt in (F16, BF16) else 4) // 4
        ap = self.buffer[:, self.at:self.at + n]
        self.at += n
        if dt is not F32:
            ap = ap.bitcast(dt)
        if len(shape) > 1:
            names = " ".join("abcdef"[:len(shape)])
            ap = ap.rearrange(f"p ({names}) -> p {names}", **dict(zip("abcdef", shape)))
        return ap


def flat(ap):
    names = " ".join("abcd"[:len(ap.shape) - 1])
    return ap.rearrange(f"p {names} -> p ({names})") if len(ap.shape) > 2 else ap


def group_of(buffer, g, count=GT):
    return lambda t: flat(buffer[:, bass.ds(count * g + t, 1), :])


def norm_block(nc, m, s, router, logits):
    norms_before = m.ln_count
    banks = (m.out_ps[0], m.out_ps[1], m.score[0])
    with nc.Block(no_gpsimd_drain=True) as block:
        @block.vector
        def _(dve):
            def norm(g, par):
                if not isinstance(g, int):
                    dve.wait_ge(s.group_sb, g - 1)
                normalise(dve, m, g, norms_before, lambda t: m.xn2[:, par, t, :]).then_inc(s.normed, 1)

            def take_logits(g, bank):
                dve.wait_ge(s.logit_ps, g + 1)
                dve.tensor_copy(logits[:, bass.ds(GT * g, GT), :],
                                banks[bank][:, 0:GT * EXPERTS].rearrange("p (t e) -> p t e", t=GT))
            whole_statistics(dve, m, norms_before)
            norm(0, 0)
            norm(1, 1)
            with dve.Fori(1, GROUPS // 2) as i:
                norm(2 * i, 0)
                take_logits(2 * i - 2, 0)
                norm(2 * i + 1, 1)
                take_logits(2 * i - 1, 1)
            take_logits(GROUPS - 2, 0)
            take_logits(GROUPS - 1, 2)

        @block.gpsimd
        def _(pool):
            whole_power(pool, m, norms_before)

        @block.tensor
        def _(pe):
            turned_ps = (m.pT_ps, m.misc)

            def turn(g, par):
                pe.wait_ge(s.normed, g + 1)
                if not isinstance(g, int):
                    pe.wait_ge(s.group_sb, g - 1)
                for t in range(GT):
                    mm = pe.transpose(turned_ps[par][:, t * P:(t + 1) * P], m.xn2[:, par, t, :], m.ident[:, :])
                mm.then_inc(s.turned, 1)

            def route(g, par, bank):
                pe.wait_ge(s.group_sb, g + 1)
                for t in range(GT):
                    mm = pe.matmul(banks[bank][:, t * EXPERTS:(t + 1) * EXPERTS],
                                   m.xnT2[:, par, t * P:(t + 1) * P], router[:, :],
                                   start=True, stop=True, skip_group_check=True)
                mm.then_inc(s.logit_ps, 1)
            turn(0, 0)
            turn(1, 1)
            route(0, 0, 0)
            with pe.Fori(1, GROUPS // 2) as i:
                turn(2 * i, 0)
                route(2 * i - 1, 1, 1)
                turn(2 * i + 1, 1)
                route(2 * i, 0, 0)
            route(GROUPS - 1, 1, 2)

        @block.scalar
        def _(act):
            turned_ps = (m.pT_ps, m.misc)
            with act.Fori(0, GROUPS // 2) as i:
                for par in range(2):
                    g = 2 * i + par
                    act.wait_ge(s.turned, g + 1)
                    act.activation(m.xnT2[:, par, :], turned_ps[par][:, :], ACT.Copy)
                    act.activation(m.xall[:, bass.ds(GT * g, GT), :], m.xn2[:, par, :, :],
                                   ACT.Copy).then_inc(s.group_sb, 1)


def stage_weights(pool, m, c, chunk):
    if chunk < c.chunks:
        n, done = m.stage.shape[-1], c.chunk0 + chunk
        if done >= 2:
            pool.wait_ge(m.split_step, 3 * (done - 1))
        pool.dma_start(m.stage[:, done % 2, :], c.weights[:, chunk * n:(chunk + 1) * n])\
            .then_inc(m.staged[done % 2], 16)


def split_weights(pool, m, c, chunk, done):
    n = m.stage.shape[-1]
    cols = slice(chunk * n, (chunk + 1) * n)
    st = m.stage[:, done % 2, :]
    pool.wait_ge(m.staged[done % 2], 16 * (done // 2 + 1))
    pool.tensor_scalar(st, st, WSCALE, None, ALU.mult).then_inc(m.split_step, 1)
    pool.wait_ge(m.split_step, 3 * done + 1)
    pool.tensor_copy(m.w_hi[:, cols], st).then_inc(m.split_step, 1)
    pool.wait_ge(m.split_step, 3 * done + 2)
    pool.tensor_tensor(m.w_lo[:, cols], st, m.w_hi[:, cols], ALU.subtract).then_inc(m.split_step, 1)


def moe(nc, m, k, c):
    swiglu = k == 1
    CH = 1 if swiglu else 2
    NJ = TILES * CH
    NW = EXPERTS * F
    SHARED = TILES if swiglu else 0
    SB = SHARED // UNROLL
    r = Region(m.big)
    kept = Region(m.big, KEPT_AT)
    logits = r.take((TILES, EXPERTS))
    work = r.take((TILES, EXPERTS))
    work2 = r.take((TILES, EXPERTS))
    top = r.take((2, TILES))
    first = r.take((2, TILES))
    hot = r.take((TILES, CH, EXPERTS))
    hot_b = r.take((NJ, EXPERTS), BF16)
    cum = [r.take((NJ, EXPERTS)) for _ in range(2)]
    total = r.take((NJ, EXPERTS))
    upto = [r.take((EXPERTS,)) for _ in range(2)]
    tiles_of = r.take((EXPERTS,))
    row0 = r.take((EXPERTS,))
    slot_f = r.take((NJ,))
    slot = kept.take((NJ,), I32)
    gate = kept.take((2, TILES))
    expo = r.take((TILES, EXPERTS))
    denom = r.take((TILES,))
    tile_hit = r.take((SLOT_TILES, EXPERTS))
    tile_f = r.take((SLOT_TILES,))
    tile_w = r.take((LAG + SLOT_TILES,), I32)
    x_row = r.take((UNROLL, D))
    x_hi, x_lo = r.take((2, P), F16), r.take((2, P), F16)
    h_f = r.take((2, F))
    h_act = r.take((2, F))
    h_hi, h_lo = r.take((UNROLL, F), F16), r.take((2, F), F16)
    y_row = r.take((UNROLL, D))
    fetched = kept.take((8, D))
    s = m.s_moe[k]
    norm_block(nc, m, s, c.router, logits)

    with nc.Block(no_gpsimd_drain=True) as block:
        steps = [0]

        @block.vector
        def _(dve):
            def step(ins):
                steps[0] += 1
                ins.then_inc(s.route, 1)
                dve.wait_ge(s.route, steps[0])

            def over_e(ap):
                return ap.unsqueeze(2).to_broadcast([P, TILES, EXPERTS])

            rev = m.rev_index[:, :].unsqueeze(1).to_broadcast([P, TILES, EXPERTS])
            left = logits
            for j in range(CH):
                step(dve.tensor_reduce(top[:, j, :], left, AX_X, ALU.max))
                step(dve.tensor_tensor(work, left, over_e(top[:, j, :]), ALU.is_equal))
                step(dve.tensor_tensor(work, work, rev, ALU.mult))
                step(dve.tensor_reduce(first[:, j, :], work, AX_X, ALU.max))
                step(dve.tensor_tensor(hot[:, :, j, :], rev, over_e(first[:, j, :]), ALU.is_equal))
                if j + 1 < CH:
                    step(dve.scalar_tensor_tensor(out=work2, in0=hot[:, :, j, :], scalar=-FAR, in1=left,
                                                  op0=ALU.mult, op1=ALU.add))
                    left = work2
            dve.tensor_copy(hot_b, hot.rearrange("p a b c -> p (a b) c")).then_inc(s.hot, 1)

            if swiglu:
                dve.tensor_tensor(work2, logits, over_e(top[:, 0, :]), ALU.subtract).then_inc(s.gate_in, 1)
                dve.wait_ge(s.gate_exp, 1)
                step(dve.tensor_reduce(denom, expo, AX_X, ALU.add))
                step(dve.reciprocal(gate[:, 0, :], denom))
                step(dve.tensor_scalar(gate[:, 1, :], hot[:, :, 0, EXPERTS - 1], -2.0, 2.0, ALU.mult, ALU.add))
                step(dve.tensor_tensor(gate[:, 0, :], gate[:, 0, :], gate[:, 1, :], ALU.mult))
            else:
                dve.tensor_tensor(denom, top[:, 1, :], top[:, 0, :], ALU.subtract).then_inc(s.gate_in, 1)
                dve.wait_ge(s.gate_exp, 1)
                step(dve.tensor_scalar(denom, expo[:, :, 0], 1.0, None, ALU.add))
                step(dve.reciprocal(gate[:, 0, :], denom))
                step(dve.tensor_tensor(gate[:, 1, :], gate[:, 0, :], expo[:, :, 0], ALU.mult))

            dve.wait_ge(s.prefix, 1)
            step(dve.tensor_copy(total, m.score[1][:, 0:NJ * EXPERTS].rearrange("p (j e) -> p j e", e=EXPERTS)))
            src, n, at = total, 1, 0
            while n < NJ:
                dst = cum[at]
                dve.tensor_copy(dst[:, 0:n, :], src[:, 0:n, :])
                step(dve.tensor_tensor(dst[:, n:, :], src[:, n:, :], src[:, 0:NJ - n, :], ALU.add))
                src, n, at = dst, 2 * n, 1 - at
            spare = cum[at]
            step(dve.tensor_scalar(tiles_of, src[:, NJ - 1, :], (P - 1) / 2.0, 1.0 / P, ALU.add, ALU.mult))
            step(dve.tensor_scalar(tiles_of, tiles_of, ROUND, None, ALU.add))
            step(dve.tensor_scalar(tiles_of, tiles_of, ROUND, None, ALU.subtract))
            ends, n, at = tiles_of, 1, 0
            while n < EXPERTS:
                dst = upto[at]
                dve.tensor_copy(dst[:, 0:n], ends[:, 0:n])
                step(dve.tensor_tensor(dst[:, n:], ends[:, n:], ends[:, 0:EXPERTS - n], ALU.add))
                ends, n, at = dst, 2 * n, 1 - at
            step(dve.tensor_tensor(row0, ends, tiles_of, ALU.subtract))
            step(dve.tensor_scalar(row0, row0, float(P), None, ALU.mult))
            step(dve.tensor_tensor(spare, src, total, ALU.subtract))
            step(dve.tensor_tensor(spare, spare, m.score[0][:, 0:NJ * EXPERTS]
                                   .rearrange("p (j e) -> p j e", e=EXPERTS), ALU.add))
            step(dve.tensor_tensor(spare, spare, row0.unsqueeze(1).to_broadcast([P, NJ, EXPERTS]), ALU.add))
            step(dve.tensor_tensor(spare, spare, hot.rearrange("p a b c -> p (a b) c"), ALU.mult))
            step(dve.tensor_reduce(slot_f, spare, AX_X, ALU.add))
            step(dve.tensor_copy(slot, slot_f))
            step(dve.tensor_tensor(tile_hit, m.tile_index[:, :].unsqueeze(2).to_broadcast([P, SLOT_TILES, EXPERTS]),
                                   ends.unsqueeze(1).to_broadcast([P, SLOT_TILES, EXPERTS]), ALU.is_ge))
            step(dve.tensor_reduce(tile_f, tile_hit, AX_X, ALU.add))
            step(dve.tensor_scalar(tile_f, tile_f, float(EXPERTS - 1), None, ALU.min))
            step(dve.tensor_scalar(tile_f, tile_f, float(F), None, ALU.mult))
            dve.memset(tile_w[:, 0:LAG], 0)
            step(dve.tensor_copy(tile_w[:, LAG:], tile_f))

        @block.scalar
        def _(act):
            act.wait_ge(s.gate_in, 1)
            if swiglu:
                act.activation(expo, work2, ACT.Exp).then_inc(s.gate_exp, 1)
            else:
                act.activation(expo[:, :, 0], denom, ACT.Exp).then_inc(s.gate_exp, 1)

        @block.tensor
        def _(pe):
            pe.wait_ge(s.hot, 1)
            pe.matmul(m.score[0][:, 0:NJ * EXPERTS], m.above[:, :], flat(hot_b), start=True, stop=True)
            pe.matmul(m.score[1][:, 0:NJ * EXPERTS], m.ones_b[:, :], flat(hot_b), start=True,
                      stop=True).then_inc(s.prefix, 1)

    h_ps = ((m.score[0], m.score[1]), (m.score[2], m.score[3]))
    x_ps = (m.pT_ps, m.misc)

    def in_shared(j):
        return j < SB if isinstance(j, int) else loop_shared[0]

    loop_shared = [False]

    def run_bodies(engine, body):
        body(0, True, False)
        if swiglu:
            loop_shared[0] = True
            with engine.Fori(1, SB) as j:
                body(j, False, False)
            loop_shared[0] = False
            body(SB, False, False)
        with engine.Fori(SB + 1, BODIES_MOE - 1) as j:
            body(j, False, False)
        body(BODIES_MOE - 1, False, True)

    with nc.Block(no_gpsimd_drain=True) as block:
        @block.gpsimd
        def _(pool):
            pool.wait_ge(m.zeroed, 16)
            for t in range(TILES):
                for j in range(CH):
                    pool.indirect_dma_start(
                        out=m.sorted_in, out_offset=bass.IndirectOffsetOnAxis(
                            ap=slot[:, t * CH + j:t * CH + j + 1], axis=0),
                        in_=m.xall[:, t, :], in_offset=None).then_inc(s.scattered, 16)
            with pool.Fori(SB, BODIES_MOE) as j:
                for u in range(UNROLL):
                    i = UNROLL * j + u
                    pool.wait_ge(s.y_row, i + 1)
                    pool.dma_start(m.sorted_out[bass.ds(i * P - SHARED * P, P), :],
                                   y_row[:, u, :]).then_inc(s.y_done[u], 16)

        @block.sync
        def _(sp):
            def load(i, u, shared):
                rows = flat(m.xall[:, bass.ds(i, 1), :]) if shared else m.sorted_in[bass.ds(i * P - SHARED * P, P), :]
                sp.dma_start(x_row[:, u, :], rows).then_inc(s.x_row[u], 16)

            def body(j, shared):
                for u in range(UNROLL):
                    i = UNROLL * j + u
                    sp.wait_ge(s.x_turned, i + 1)
                    load(i + UNROLL, u, shared)
            if swiglu:
                for u in range(UNROLL):
                    load(u, u, True)
                with sp.Fori(0, SB - 1) as j:
                    body(j, True)
            sp.wait_ge(s.scattered, 16 * NJ)
            if swiglu:
                body(SB - 1, False)
            else:
                for u in range(UNROLL):
                    load(u, u, False)
            with sp.Fori(SB, BODIES_MOE - 1) as j:
                body(j, False)

        @block.tensor
        def _(pe):
            def experts(j):
                regs = [pe.alloc_register(f"moe{k}_expert{u}_{j if isinstance(j, int) else 'loop'}") for u in range(LAG + UNROLL)]
                at = UNROLL * j - SHARED if isinstance(j, int) else bass.ds(UNROLL * j - SHARED, LAG + UNROLL)
                pe.load(regs, tile_w[0:1, at:at + LAG + UNROLL] if isinstance(j, int) else tile_w[0:1, at])
                return [pe.snap(reg, donate=True, min_val=0, max_val=(EXPERTS - 1) * F) for reg in regs]

            def turn(i, u, par, j):
                pe.wait_ge(s.x_row[u], 16 * (j + 1))
                pe.transpose(x_ps[par][:, 0:P], x_row[:, u, :], m.ident[:, :]).then_inc(s.x_turned, 1)

            def hidden(i, par, e):
                pe.wait_ge(s.x_split, i + 1)
                for which in range(2 if swiglu else 1):
                    for fb in range(FB):
                        at = e + (which * NW + fb * P)
                        o = h_ps[par][which][:, fb * P:(fb + 1) * P]
                        hi, lo = m.w_hi[:, bass.ds(at, P)], m.w_lo[:, bass.ds(at, P)]
                        pe.matmul(o, hi, x_hi[:, par, :], start=(fb == 0), stop=False, skip_group_check=True)
                        pe.matmul(o, hi, x_lo[:, par, :], start=False, stop=False, skip_group_check=True)
                        mm = pe.matmul(o, lo, x_hi[:, par, :], start=False, stop=True, skip_group_check=True)
                        if not swiglu:
                            mm = pe.matmul(o, m.b1_rows[:, bass.ds(e + fb * P, P)], m.ones3[:, :],
                                           start=False, stop=True, skip_group_check=True)
                mm.then_inc(s.h_ps, 1)

            def down(i, u, par, e):
                pe.wait_ge(s.h_split, i + 1)
                o = m.out_ps[par][:, 0:D]
                for fb in range(FB):
                    at = e + ((1 + swiglu) * NW + fb * D)
                    f = slice(fb * P, (fb + 1) * P)
                    hi, lo = m.w_hi[:, bass.ds(at, D)], m.w_lo[:, bass.ds(at, D)]
                    pe.matmul(o, h_hi[:, u, f], hi, start=(fb == 0), stop=False, skip_group_check=True)
                    pe.matmul(o, h_lo[:, par, f], hi, start=False, stop=False, skip_group_check=True)
                    mm = pe.matmul(o, h_hi[:, u, f], lo, start=False, stop=True, skip_group_check=True)
                if not swiglu:
                    mm = pe.matmul(o, m.ones3[:, :], m.b2_rows[:, bass.ds(e // (F // D), D)], start=False, stop=True,
                                   skip_group_check=True)
                mm.then_inc(s.y_ps, 1)

            turn(0, 0, 0, 0)

            def body(j, start, end):
                if in_shared(j):
                    e = [(EXPERTS - 1) * F] * (LAG + UNROLL)
                else:
                    e = experts(j)
                    if swiglu and isinstance(j, int) and j == SB:
                        e[0:LAG] = [(EXPERTS - 1) * F] * LAG
                for u in range(UNROLL):
                    i = UNROLL * j + u
                    if not (end and u == UNROLL - 1):
                        turn(i + 1, (u + 1) % UNROLL, (u + 1) % 2, j + (u + 1) // UNROLL)
                    hidden(i, u % 2, e[LAG + u])
                    if not (start and u < LAG):
                        down(i - LAG, (u - LAG) % UNROLL, u % 2, e[u])
                if end:
                    down(i - 1, UNROLL - 2, 0, e[UNROLL])
                    down(i, UNROLL - 1, 1, e[UNROLL + 1])
            run_bodies(pe, body)

        @block.scalar
        def _(act):
            def take_x(i, par):
                act.wait_ge(s.x_turned, i + 1)
                act.activation(x_hi[:, par, :], x_ps[par][:, 0:P], ACT.Copy).then_inc(s.x_hi, 1)

            def activate(i, u, par):
                act.wait_ge(s.h_ps, i + 1)
                if not isinstance(i, int) or i > 1:
                    act.wait_ge(s.h_split, i - 1)
                if swiglu:
                    act.activation(h_act[:, par, :], h_ps[par][1][:, :], ACT.Silu,
                                   scale=1.0 / WSCALE).then_inc(s.h_act, 1)
                else:
                    act.activation(h_hi[:, u, :], h_ps[par][0][:, :], ACT.Gelu, scale=1.0 / WSCALE)
                    act.activation(h_f[:, par, :], h_ps[par][0][:, :], ACT.Gelu,
                                   scale=1.0 / WSCALE).then_inc(s.h_act, 1)
            take_x(0, 0)

            def body(j, start, end):
                for u in range(UNROLL):
                    i = UNROLL * j + u
                    if not (end and u == UNROLL - 1):
                        take_x(i + 1, (u + 1) % 2)
                    activate(i, u, u % 2)
            run_bodies(act, body)

        @block.vector
        def _(dve):
            def split_x(i, par):
                dve.wait_ge(s.x_hi, i + 1)
                dve.tensor_tensor(x_lo[:, par, :], x_ps[par][:, 0:P], x_hi[:, par, :],
                                  ALU.subtract).then_inc(s.x_split, 1)

            def split_h(i, u, par):
                dve.wait_ge(s.h_act, i + 1)
                if swiglu:
                    dve.scalar_tensor_tensor(out=h_f[:, par, :], in0=h_ps[par][0][:, :], scalar=1.0 / WSCALE,
                                             in1=h_act[:, par, :], op0=ALU.mult, op1=ALU.mult).then_inc(s.h_f, 1)
                    dve.wait_ge(s.h_f, i + 1)
                    dve.tensor_copy(h_hi[:, u, :], h_f[:, par, :]).then_inc(s.h_hi, 1)
                    dve.wait_ge(s.h_hi, i + 1)
                dve.tensor_tensor(h_lo[:, par, :], h_f[:, par, :], h_hi[:, u, :],
                                  ALU.subtract).then_inc(s.h_split, 1)

            def take_y(i, u, par, j):
                dve.wait_ge(s.y_ps, i + 1)
                if in_shared(j):
                    x = flat(m.x[:, bass.ds(i, 1), :])
                    dve.scalar_tensor_tensor(out=x, in0=m.out_ps[par][:, 0:D], scalar=1.0 / WSCALE, in1=x,
                                             op0=ALU.mult, op1=ALU.add).then_inc(s.y_row, 1)
                    return
                if not isinstance(j, int) or j > SB:
                    dve.wait_ge(s.y_done[u], 16 * j - 16 * SB)
                dve.tensor_scalar(y_row[:, u, :], m.out_ps[par][:, 0:D], 1.0 / WSCALE, None,
                                  ALU.mult).then_inc(s.y_row, 1)
            split_x(0, 0)

            def body(j, start, end):
                before = SB - 1 if isinstance(j, int) and j == SB else j - 1
                for u in range(UNROLL):
                    i = UNROLL * j + u
                    if not (end and u == UNROLL - 1):
                        split_x(i + 1, (u + 1) % 2)
                    if not (start and u < LAG):
                        take_y(i - LAG, (u - LAG) % UNROLL, u % 2, before if u < LAG else j)
                    split_h(i, u, u % 2)
                if end:
                    take_y(i - 1, UNROLL - 2, 0, j)
                    take_y(i, UNROLL - 1, 1, j)
            run_bodies(dve, body)

    f = Names()
    f.s, f.slot, f.gate, f.fetched, f.choices, f.stored = s, slot, gate, fetched, CH, 16 * (BODIES_MOE - SB)
    return f


def fetch_rows(pool, m, f, g):
    for j in range(f.choices):
        for t in range(GT):
            n = GT * (f.choices * g + j) + t
            if n >= 8:
                pool.wait_ge(f.s.added, n - 7)
            at = (GT * g + t) * f.choices + j
            pool.indirect_dma_start(
                out=f.fetched[:, n % 8, :], out_offset=None, in_=m.sorted_out,
                in_offset=bass.IndirectOffsetOnAxis(ap=f.slot[:, at:at + 1], axis=0)).then_inc(f.s.fetched[n % 8], 16)


def add_rows(dve, m, f, g, half):
    half, odd = half
    for j in range(f.choices):
        for t in range(GT):
            c = GT * j + t
            buffer, times = (c, g + 1) if f.choices == 2 else (GT * odd + c, half + 1)
            dve.wait_ge(f.s.fetched[buffer], 16 * times)
            if j:
                dve.wait_ge(f.s.added, 2 * GT * g + (t + 1))
            x = flat(m.x[:, bass.ds(GT * g + t, 1), :])
            dve.scalar_tensor_tensor(out=x, in0=f.fetched[:, buffer, :], scalar=f.gate[:, j, bass.ds(GT * g + t, 1)],
                                     in1=x, op0=ALU.mult, op1=ALU.add).then_inc(f.s.added, 1)
    dve.wait_ge(f.s.added, GT * f.choices * g + GT * f.choices)


def load_bias_rows(sp, m, s, bias_f, bias_b, b1, b2):
    n1, n2 = b1.shape[1], b2.shape[1]
    sp.dma_start(bias_f[:, 0, 0:n1], b1).then_inc(s.bias_in, 16)
    sp.dma_start(bias_f[:, 1, 0:n2], b2).then_inc(s.bias_in, 16)
    sp.wait_ge(s.bias_step, BIAS_STEPS)
    sp.wait_ge(s.rows_clear, 1)
    for i in range(3):
        sp.dma_start(m.b1_rows[i:i + 1, 0:n1 * P], bias_b[:, i, 0, 0:n1]).then_inc(s.bias_rows, 16)
        sp.dma_start(m.b2_rows[i:i + 1, 0:n2 * P], bias_b[:, i, 1, 0:n2]).then_inc(s.bias_rows, 16)
    sp.wait_ge(s.bias_rows, 16 * 6)


def clear_bias_rows(dve, m, s, bias_f):
    dve.memset(bias_f[:, 1, EXPERTS:], 0.0).then_inc(s.bias_step, 1)
    dve.memset(m.b1_rows[:, :], 0.0)
    dve.memset(m.b2_rows[:, :], 0.0).then_inc(s.rows_clear, 1)


BIAS_STEPS = 7


def split_bias_rows(pool, m, s, bias_f, bias_b):
    pool.wait_ge(s.bias_step, 1)
    pool.wait_ge(s.bias_in, 32)
    pool.tensor_scalar(bias_f, bias_f, WSCALE, None, ALU.mult).then_inc(s.bias_step, 1)
    n = 2
    for i in range(3):
        pool.wait_ge(s.bias_step, n)
        pool.tensor_copy(bias_b[:, i, :, :], bias_f).then_inc(s.bias_step, 1)
        n += 1
        if i < 2:
            pool.wait_ge(s.bias_step, n)
            pool.tensor_tensor(bias_f, bias_f, bias_b[:, i, :, :], ALU.subtract).then_inc(s.bias_step, 1)
            n += 1
    assert n == BIAS_STEPS


DIAG_BLOCKS = 1024 // P


def diagonal_attention(nc, m):
    s = m.s_diag
    r = Region(m.big)
    wv = r.take((DIAG_BLOCKS, D))
    wo = r.take((DIAG_BLOCKS, D))
    wvo = r.take((D,))
    bout = r.take((D,))
    ctx = r.take((2, GTOK))
    with nc.Block(no_gpsimd_drain=True) as block:
        @block.sync
        def _(sp):
            sp.dma_start(wv, m.d["diag_wvT"].rearrange("p (a b) -> p a b", a=DIAG_BLOCKS)).then_inc(s.weights, 16)
            sp.dma_start(wo, m.d["diag_wout"].rearrange("p (a b) -> p a b", a=DIAG_BLOCKS)).then_inc(s.weights, 16)
            sp.dma_start(bout, m.d["diag_bout"].partition_broadcast(P)).then_inc(s.weights, 16)

            def load(g, par):
                sp.dma_start(ctx[:, par, :], m.ctxT_dram[:, bass.ds(g * GTOK, GTOK)]).then_inc(s.ctx[par], 16)
            load(0, 0)
            load(1, 1)
            with sp.Fori(1, GROUPS // 2) as i:
                for par in range(2):
                    sp.wait_ge(s.y_ps, 2 * i + par - 1)
                    load(2 * i + par, par)

        @block.tensor
        def _(pe):
            pe.wait_ge(s.weights, 48)
            for j in range(DIAG_BLOCKS):
                mm = pe.matmul(m.misc[:, 0:D], wv[:, j, :], wo[:, j, :], start=(j == 0), stop=(j == DIAG_BLOCKS - 1))
            mm.then_inc(s.wvo_ps, 1)
            pe.wait_ge(s.wvo, 1)
            with pe.Fori(0, GROUPS // 2) as i:
                for par in range(2):
                    pe.wait_ge(s.ctx[par], 16 * (i + 1))
                    pe.wait_ge(s.added, 2 * i)
                    for t in range(GT):
                        mm = pe.matmul(m.score[par][:, t * D:(t + 1) * D], ctx[:, par, t * P:(t + 1) * P], wvo,
                                       start=True, stop=True, skip_group_check=True)
                    mm.then_inc(s.y_ps, 1)

        @block.vector
        def _(dve):
            dve.wait_ge(s.wvo_ps, 1)
            dve.tensor_copy(wvo, m.misc[:, 0:D]).then_inc(s.wvo, 1)
            with dve.Fori(0, GROUPS // 2) as i:
                for par in range(2):
                    g = 2 * i + par
                    x = m.x[:, bass.ds(GT * g, GT), :]
                    dve.wait_ge(s.y_ps, g + 1)
                    dve.tensor_tensor(x, x, m.score[par][:, :].rearrange("p (t d) -> p t d", t=GT),
                                      ALU.add).then_inc(s.added, 1)
                    dve.wait_ge(s.added, g + 1)
                    dve.tensor_tensor(x, x, bout.unsqueeze(1).to_broadcast([P, GT, D]), ALU.add)


QMIN, QMAX = -128.0, 127.0
H_COLS = FB * TOKENS


def quantized_ffn(nc, m):
    s = m.s_quant
    q = Region(m.quant)
    wf = q.take((2, F))
    wq = q.take((2, F), BF16)
    b1 = q.take((FB,))
    b2 = q.take((D,))
    ext = q.take((4,))
    ext_all = q.take((4,))
    h_ext = q.take((2, FB * GROUPS))
    h_most = q.take((2,))
    h_all = q.take((2,))
    par_x, par_h = q.take((8,)), q.take((8,))
    w_scale, w_inverse = q.take((2,)), q.take((2,))
    out_scale = q.take((2,))
    xq = m.b1_rows[:, :].rearrange("p (t d) -> p t d", t=TILES)
    xqT = q.take((2, GTOK), BF16)
    late = Region(m.kexp_buffer)
    hq = late.take((2, FB, GTOK), BF16)
    h = m.big[:, 0:H_COLS].rearrange("p (b n) -> p b n", b=FB)

    def parameters(step, dve, ext, par):
        one = lambda i: par[:, i:i + 1]
        step(dve.tensor_tensor(one(0), ext[:, 0:1], ext[:, 1:2], ALU.add))
        step(dve.tensor_scalar(one(0), one(0), 1.0 / 255.0, 1e-8, ALU.mult, ALU.max))
        step(dve.reciprocal(one(4), one(0)))
        step(dve.tensor_tensor(one(1), ext[:, 1:2], one(4), ALU.mult))
        step(dve.tensor_scalar(one(1), one(1), ROUND, None, ALU.add))
        step(dve.tensor_scalar(one(1), one(1), ROUND, QMIN, ALU.subtract, ALU.add))
        step(dve.tensor_scalar(one(1), one(1), QMIN, QMAX, ALU.max, ALU.min))
        dve.tensor_scalar(one(2), one(1), -1.0, QMIN, ALU.mult, ALU.add)
        step(dve.tensor_scalar(one(3), one(1), -1.0, QMAX, ALU.mult, ALU.add))

    norms_before = m.ln_count
    with nc.Block(no_gpsimd_drain=True) as block:
        steps = [0]

        @block.sync
        def _(sp):
            sp.dma_start(wf[:, 0, :], m.d["quant_w1"]).then_inc(s.weights, 16)
            sp.dma_start(wf[:, 1, :], m.d["quant_w2"]).then_inc(s.weights, 16)
            sp.dma_start(b1, m.d["quant_b1"]).then_inc(s.weights, 16)
            sp.dma_start(b2, m.d["quant_b2"].partition_broadcast(P)).then_inc(s.weights, 16)

        @block.vector
        def _(dve):
            def step(ins):
                steps[0] += 1
                ins.then_inc(s.step, 1)
                dve.wait_ge(s.step, steps[0])
            whole_statistics(dve, m, norms_before)
            with dve.Fori(0, GROUPS) as g:
                normalise(dve, m, g, norms_before, group_of(m.xall, g)).then_inc(s.normed, 1)
            dve.wait_ge(s.normed, GROUPS)
            dve.wait_ge(s.weights, 64)
            dve.tensor_reduce(ext[:, 0:1], flat(m.xall), AX_X, ALU.max)
            dve.tensor_reduce(ext[:, 1:2], flat(m.xall), AX_X, ALU.min)
            dve.tensor_reduce(ext[:, 2:4], wf, AX_X, ALU.max, apply_absolute_value=True).then_inc(s.step, 1)
            steps[0] += 1
            dve.wait_ge(s.step, steps[0])
            dve.tensor_scalar(ext[:, 1:2], ext[:, 1:2], -1.0, None, ALU.mult).then_inc(s.ext, 1)
            dve.wait_ge(s.ext_all, 1)
            parameters(step, dve, ext_all, par_x)
            step(dve.tensor_scalar(w_scale, ext_all[:, 2:4], 1.0 / QMAX, 1e-8, ALU.mult, ALU.max))
            step(dve.reciprocal(w_inverse, w_scale))
            dve.tensor_tensor(out_scale[:, 0:1], par_x[:, 0:1], w_scale[:, 0:1], ALU.mult)
            for i in range(2):
                step(dve.tensor_scalar(wf[:, i, :], wf[:, i, :], w_inverse[:, i:i + 1], ROUND, ALU.mult, ALU.add))
            step(dve.tensor_scalar(wf, wf, ROUND, -QMAX, ALU.subtract, ALU.max))
            step(dve.tensor_scalar(wq, wf, QMAX, None, ALU.min))
            half = TILES // 2
            for part in range(2):
                x = m.xall[:, part * half:(part + 1) * half, :]
                step(dve.tensor_scalar(x, x, par_x[:, 4:5], ROUND, ALU.mult, ALU.add))
                step(dve.tensor_scalar(x, x, ROUND, par_x[:, 2:3], ALU.subtract, ALU.max))
                step(dve.tensor_scalar(xq[:, part * half:(part + 1) * half, :], x, par_x[:, 3:4], None, ALU.min))

        @block.gpsimd
        def _(pool):
            whole_power(pool, m, norms_before)
            pool.wait_ge(s.ext, 1)
            pool.partition_all_reduce(ext_all, ext, P, bass.bass_isa.ReduceOp.max).then_inc(s.ext_all, 1)

    with nc.Block(no_gpsimd_drain=True) as block:
        @block.tensor
        def _(pe):
            def turn(g, par):
                for t in range(GT):
                    mm = pe.matmul((m.pT_ps, m.misc)[par][:, t * P:(t + 1) * P],
                                   flat(xq[:, bass.ds(GT * g + t, 1), :]), m.ident_b[:, :],
                                   start=True, stop=True, skip_group_check=True)
                mm.then_inc(s.turned, 1)

            def product(g, par):
                pe.wait_ge(s.xqT, g + 1)
                for fb in range(FB):
                    if not isinstance(g, int) or g:
                        pe.wait_ge(s.gelu, FB * g + (fb + 1 - FB))
                    pe.matmul(m.score[fb][:, :], wq[:, 0, fb * P:(fb + 1) * P], xqT[:, par, :],
                              start=True, stop=True).then_inc(s.h_ps, 1)
            turn(0, 0)
            turn(1, 1)
            product(0, 0)
            with pe.Fori(1, GROUPS // 2) as i:
                turn(2 * i, 0)
                product(2 * i - 1, 1)
                turn(2 * i + 1, 1)
                product(2 * i, 0)
            product(GROUPS - 1, 1)

        @block.scalar
        def _(act):
            def take(g, par):
                act.wait_ge(s.turned, g + 1)
                act.activation(xqT[:, par, :], (m.pT_ps, m.misc)[par][:, :], ACT.Copy).then_inc(s.xqT, 1)

            def gelu(g):
                for fb in range(FB):
                    act.wait_ge(s.h_ps, FB * g + fb + 1)
                    act.activation(h[:, fb, bass.ds(GTOK * g, GTOK)], m.score[fb][:, :], ACT.Gelu,
                                   bias=b1[:, fb:fb + 1], scale=out_scale[:, 0:1]).then_inc(s.gelu, 1)
            take(0, 0)
            take(1, 1)
            gelu(0)
            with act.Fori(1, GROUPS // 2) as i:
                take(2 * i, 0)
                gelu(2 * i - 1)
                take(2 * i + 1, 1)
                gelu(2 * i)
            gelu(GROUPS - 1)

        @block.vector
        def _(dve):
            with dve.Fori(0, GROUPS) as g:
                dve.wait_ge(s.gelu, FB * g + FB)
                part = h[:, :, bass.ds(GTOK * g, GTOK)]
                dve.tensor_reduce(h_ext[:, 0, bass.ds(FB * g, FB)], part, AX_X, ALU.max)
                dve.tensor_reduce(h_ext[:, 1, bass.ds(FB * g, FB)], part, AX_X, ALU.min).then_inc(s.h_ext, 1)

    with nc.Block(no_gpsimd_drain=True) as block:
        steps = [0]

        @block.vector
        def _(dve):
            def step(ins):
                steps[0] += 1
                ins.then_inc(s.step2, 1)
                dve.wait_ge(s.step2, steps[0])
            dve.tensor_reduce(h_most[:, 0:1], h_ext[:, 0, :], AX_X, ALU.max)
            step(dve.tensor_reduce(h_most[:, 1:2], h_ext[:, 1, :], AX_X, ALU.min))
            dve.tensor_scalar(h_most[:, 1:2], h_most[:, 1:2], -1.0, None, ALU.mult).then_inc(s.ext, 1)
            dve.wait_ge(s.ext_all, 2)
            parameters(step, dve, h_all, par_h)
            step(dve.tensor_tensor(out_scale[:, 1:2], par_h[:, 0:1], w_scale[:, 1:2], ALU.mult))

            def quantise(g, par):
                part = h[:, :, bass.ds(GTOK * g, GTOK)]
                dve.tensor_scalar(part, part, par_h[:, 4:5], ROUND, ALU.mult, ALU.add).then_inc(s.hq_step, 1)
                dve.wait_ge(s.hq_step, 2 * g + 1)
                dve.tensor_scalar(part, part, ROUND, par_h[:, 2:3], ALU.subtract, ALU.max).then_inc(s.hq_step, 1)
                dve.wait_ge(s.hq_step, 2 * g + 2)
                if not isinstance(g, int):
                    dve.wait_ge(s.y_ps, g - 1)
                dve.tensor_scalar(hq[:, par, :, :], part, par_h[:, 3:4], None, ALU.min).then_inc(s.hq, 1)

            def add(g, par):
                x = m.x[:, bass.ds(GT * g, GT), :]
                dve.wait_ge(s.y_ps, g + 1)
                dve.scalar_tensor_tensor(out=flat(x), in0=m.out_ps[par][:, :], scalar=out_scale[:, 1:2],
                                         in1=flat(x), op0=ALU.mult, op1=ALU.add).then_inc(s.added, 1)
                dve.wait_ge(s.added, g + 1)
                dve.tensor_tensor(x, x, b2.unsqueeze(1).to_broadcast([P, GT, D]), ALU.add)
            quantise(0, 0)
            quantise(1, 1)
            add(0, 0)
            with dve.Fori(1, GROUPS // 2) as i:
                quantise(2 * i, 0)
                add(2 * i - 1, 1)
                quantise(2 * i + 1, 1)
                add(2 * i, 0)
            add(GROUPS - 1, 1)

        @block.gpsimd
        def _(pool):
            pool.wait_ge(s.ext, 2)
            pool.partition_all_reduce(h_all, h_most, P, bass.bass_isa.ReduceOp.max).then_inc(s.ext_all, 1)

        @block.tensor
        def _(pe):
            with pe.Fori(0, GROUPS // 2) as i:
                for par in range(2):
                    g = 2 * i + par
                    pe.wait_ge(s.hq, g + 1)
                    for t in range(GT):
                        for fb in range(FB):
                            mm = pe.matmul(m.out_ps[par][:, t * D:(t + 1) * D], hq[:, par, fb, t * P:(t + 1) * P],
                                           wq[:, 1, fb * D:(fb + 1) * D], start=(fb == 0), stop=(fb == FB - 1),
                                           skip_group_check=True)
                    mm.then_inc(s.y_ps, 1)


F3 = 2 * D
FB3 = F3 // P


def chosen_ffn(nc, m, out):
    s = m.s_chosen
    r = Region(m.big)
    xT_hi, xT_lo = r.take((TOKENS,), F16), r.take((TOKENS,), F16)
    last_T = r.take((B,))
    wp1, wp2 = r.take((D,)), r.take((EXPERTS,))
    bp1, bp2 = r.take((1,)), r.take((EXPERTS,))
    wo, bo = r.take((D,)), r.take((D,))
    nav = r.take((B,))
    logits = r.take((EXPERTS,))
    best = r.take((1,))
    hit = r.take((EXPERTS,))
    first = r.take((1,))
    sel_f = r.take((1,))
    sel = r.take((2 + B,), I32)
    h_f = r.take((2, F3))
    h_hi, h_lo = r.take((2, F3), F16), r.take((2, F3), F16)
    reasoned = r.take((2, P))
    bias_f = r.take((2, F3 * EXPERTS // P))
    bias_b = r.take((3, 2, F3 * EXPERTS // P), BF16)

    norms_before = m.ln_count
    with nc.Block(no_gpsimd_drain=True) as block:
        @block.sync
        def _(sp):
            for dst, name in ((wp1, "chosen_wp1"), (wp2, "chosen_wp2"), (bp1, "chosen_bp1"), (wo, "chosen_wo")):
                sp.dma_start(dst, m.d[name]).then_inc(s.weights, 16)
            sp.dma_start(bp2, m.d["chosen_bp2"].partition_broadcast(P)).then_inc(s.weights, 16)
            sp.dma_start(bo, m.d["chosen_bo"].partition_broadcast(P)).then_inc(s.weights, 16)
            load_bias_rows(sp, m, s, bias_f, bias_b, m.d["chosen_b1"], m.d["chosen_b2"])

        @block.vector
        def _(dve):
            clear_bias_rows(dve, m, s, bias_f)

            def norm(g, par):
                if not isinstance(g, int):
                    dve.wait_ge(s.xT_lo, g - 1)
                    dve.wait_ge(s.copied, g - 1)
                normalise(dve, m, g, norms_before, lambda t: m.xn2[:, par, t, :]).then_inc(s.normed, 1)

            def low(g, par):
                dve.wait_ge(s.xT_hi, g + 1)
                cols = bass.ds(GTOK * g, GTOK)
                dve.tensor_tensor(xT_lo[:, cols], (m.pT_ps, m.misc)[par][:, :], xT_hi[:, cols],
                                  ALU.subtract).then_inc(s.xT_lo, 1)
            whole_statistics(dve, m, norms_before)
            norm(0, 0)
            norm(1, 1)
            with dve.Fori(1, GROUPS // 2) as i:
                low(2 * i - 2, 0)
                norm(2 * i, 0)
                low(2 * i - 1, 1)
                norm(2 * i + 1, 1)
            low(GROUPS - 2, 0)
            low(GROUPS - 1, 1)

        @block.gpsimd
        def _(pool):
            split_bias_rows(pool, m, s, bias_f, bias_b)
            whole_power(pool, m, norms_before)

        @block.tensor
        def _(pe):
            with pe.Fori(0, GROUPS // 2) as i:
                for par in range(2):
                    g = 2 * i + par
                    pe.wait_ge(s.normed, g + 1)
                    for t in range(GT):
                        mm = pe.transpose((m.pT_ps, m.misc)[par][:, t * P:(t + 1) * P], m.xn2[:, par, t, :],
                                          m.ident[:, :])
                    mm.then_inc(s.turned, 1)

        @block.scalar
        def _(act):
            with act.Fori(0, GROUPS // 2) as i:
                for par in range(2):
                    g = 2 * i + par
                    turned = (m.pT_ps, m.misc)[par]
                    act.wait_ge(s.turned, g + 1)
                    act.activation(last_T[:, bass.ds(2 * GT * g, 2 * GT)], turned[:, S - 1::S], ACT.Copy)
                    act.activation(xT_hi[:, bass.ds(GTOK * g, GTOK)], turned[:, :], ACT.Copy).then_inc(s.xT_hi, 1)
                    act.activation(m.xall[:, bass.ds(GT * g, GT), :], m.xn2[:, par, :, :],
                                   ACT.Copy).then_inc(s.copied, 1)

    with nc.Block(no_gpsimd_drain=True) as block:
        @block.tensor
        def _(pe):
            pe.wait_ge(s.weights, 16 * 6)
            pe.matmul(m.misc[:, 0:B], wp1, last_T, start=True, stop=True).then_inc(s.nav_ps, 1)
            pe.wait_ge(s.nav, 1)
            pe.matmul(m.pT_ps[0:B, 0:EXPERTS], nav, wp2, start=True, stop=True).then_inc(s.nav_ps, 1)
            pe.wait_ge(s.pick, 5)
            pe.matmul(m.misc[0:1, 0:B], sel_f[0:B, :], m.ident[0:B, 0:B], start=True, stop=True).then_inc(s.nav_ps, 1)

        @block.scalar
        def _(act):
            act.wait_ge(s.nav_ps, 1)
            act.activation(nav, m.misc[:, 0:B], ACT.Gelu, bias=bp1).then_inc(s.nav, 1)

        @block.vector
        def _(dve):
            rows = slice(0, B)
            dve.wait_ge(s.nav_ps, 2)
            dve.tensor_tensor(logits[rows, :], m.pT_ps[rows, 0:EXPERTS], bp2[rows, :], ALU.add).then_inc(s.pick, 1)
            dve.wait_ge(s.pick, 1)
            dve.tensor_reduce(best[rows, :], logits[rows, :], AX_X, ALU.max).then_inc(s.pick, 1)
            dve.wait_ge(s.pick, 2)
            dve.scalar_tensor_tensor(out=hit[rows, :], in0=logits[rows, :], scalar=best[rows, 0:1],
                                     in1=m.rev_index[rows, :], op0=ALU.is_equal, op1=ALU.mult).then_inc(s.pick, 1)
            dve.wait_ge(s.pick, 3)
            dve.tensor_reduce(first[rows, :], hit[rows, :], AX_X, ALU.max).then_inc(s.pick, 1)
            dve.wait_ge(s.pick, 4)
            dve.tensor_scalar(sel_f[rows, :], first[rows, :], -1.0, float(EXPERTS), ALU.mult,
                              ALU.add).then_inc(s.pick, 1)
            dve.wait_ge(s.nav_ps, 3)
            dve.memset(sel[0:1, 0:2], 0)
            dve.tensor_copy(sel[0:1, 2:], m.misc[0:1, 0:B])

    h_ps, r_ps, y_ps = m.score[0:2], m.score[2:4], m.out_ps
    with nc.Block(no_gpsimd_drain=True) as block:
        @block.tensor
        def _(pe):
            def chosen(i, tiles, name):
                n = 2 + 2 * tiles
                regs = [pe.alloc_register(f"chosen_{name}{b}") for b in range(n)]
                pe.load(regs, sel[0:1, 2 * i:2 * i + n] if isinstance(i, int) else sel[0:1, bass.ds(2 * i, n)])
                return [pe.snap(reg, donate=True, min_val=0, max_val=EXPERTS - 1) for reg in regs]

            def hidden(i, par, experts):
                for b in range(2):
                    e = experts[b]
                    cols = bass.ds(P * i + S * b, S)
                    for fb in range(FB3):
                        o = h_ps[par][:, fb * P + b * S:fb * P + (b + 1) * S]
                        w = bass.ds(e * F3 + fb * P, P)
                        pe.matmul(o, m.w_hi[:, w], xT_hi[:, cols], start=(fb == 0 and b == 0), stop=False,
                                  skip_group_check=True)
                        pe.matmul(o, m.w_hi[:, w], xT_lo[:, cols], start=False, stop=False, skip_group_check=True)
                        pe.matmul(o, m.w_lo[:, w], xT_hi[:, cols], start=False, stop=False, skip_group_check=True)
                        mm = pe.matmul(o, m.b1_rows[:, w], m.ones3[:, 0:S], start=False, stop=True,
                                       skip_group_check=True)
                mm.then_inc(s.h_ps, 1)

            def down(i, par, experts):
                for b in range(2):
                    e = experts[b]
                    if b == 0:
                        pe.wait_ge(s.h_split, i + 1)
                    o = r_ps[par][:, b * S:(b + 1) * S]
                    for fb in range(FB3):
                        w = bass.ds(e * F3 + (EXPERTS * F3 + fb * D), D)
                        f = slice(fb * P + b * S, fb * P + (b + 1) * S)
                        pe.matmul(o, m.w_hi[:, w], h_hi[:, par, f], start=(fb == 0 and b == 0), stop=False,
                                  skip_group_check=True)
                        pe.matmul(o, m.w_hi[:, w], h_lo[:, par, f], start=False, stop=False, skip_group_check=True)
                        pe.matmul(o, m.w_lo[:, w], h_hi[:, par, f], start=False, stop=False, skip_group_check=True)
                    mm = pe.matmul(o, m.b2_rows[:, bass.ds(e * D, D)], m.ones3[:, 0:S], start=False, stop=True,
                                   skip_group_check=True)
                mm.then_inc(s.r_ps, 1)

            def last(i, par):
                pe.wait_ge(s.reasoned, i + 1)
                pe.wait_ge(s.y_free, i + 1)
                pe.matmul(y_ps[par][:, 0:D], reasoned[:, par, :], wo, start=True, stop=True).then_inc(s.y_ps, 1)

            e = chosen(0, 2, "first")
            hidden(0, 0, e[2:4])
            hidden(1, 1, e[4:6])
            down(0, 0, e[2:4])
            with pe.Fori(1, TILES // 2) as i:
                e = chosen(2 * i, 2, "next")
                hidden(2 * i, 0, e[2:4])
                down(2 * i - 1, 1, e[0:2])
                last(2 * i - 2, 0)
                hidden(2 * i + 1, 1, e[4:6])
                down(2 * i, 0, e[2:4])
                last(2 * i - 1, 1)
            down(TILES - 1, 1, chosen(TILES, 0, "last"))
            last(TILES - 2, 0)
            last(TILES - 1, 1)

        @block.scalar
        def _(act):
            def gelu(i, par):
                act.wait_ge(s.h_ps, i + 1)
                act.activation(h_f[:, par, :], h_ps[par][:, 0:F3], ACT.Gelu, scale=1.0 / WSCALE).then_inc(s.gelu, 1)

            def take(i, par):
                act.wait_ge(s.r_ps, i + 1)
                act.activation(reasoned[:, par, :], r_ps[par][:, 0:P], ACT.Copy,
                               scale=1.0 / WSCALE).then_inc(s.reasoned, 1)
            gelu(0, 0)
            gelu(1, 1)
            take(0, 0)
            with act.Fori(1, TILES // 2) as i:
                gelu(2 * i, 0)
                take(2 * i - 1, 1)
                gelu(2 * i + 1, 1)
                take(2 * i, 0)
            take(TILES - 1, 1)

        @block.vector
        def _(dve):
            def split(i, par):
                dve.wait_ge(s.gelu, i + 1)
                dve.tensor_copy(h_hi[:, par, :], h_f[:, par, :]).then_inc(s.h_hi, 1)
                dve.wait_ge(s.h_hi, i + 1)
                dve.tensor_tensor(h_lo[:, par, :], h_f[:, par, :], h_hi[:, par, :], ALU.subtract)\
                   .then_inc(s.h_split, 1)

            def add(i, par):
                dve.wait_ge(s.y_ps, i + 1)
                xn = flat(m.xall[:, bass.ds(i, 1), :])
                dve.scalar_tensor_tensor(out=xn, in0=y_ps[par][:, 0:D], scalar=0.3, in1=xn, op0=ALU.mult,
                                         op1=ALU.add).then_inc(s.y_free, 1)
            dve.wait_ge(s.weights, 16 * 6)
            dve.tensor_scalar(bo, bo, 0.3, None, ALU.mult).then_inc(s.y_free, 2)
            split(0, 0)
            split(1, 1)
            with dve.Fori(1, TILES // 2) as i:
                split(2 * i, 0)
                add(2 * i - 2, 0)
                split(2 * i + 1, 1)
                add(2 * i - 1, 1)
            add(TILES - 2, 0)
            add(TILES - 1, 1)
            dve.wait_ge(s.y_free, TILES + 2)
            for q in range(4):
                rows = slice(q * TILES // 4, (q + 1) * TILES // 4)
                x = m.x[:, rows, :]
                dve.tensor_tensor(x, x, m.xall[:, rows, :], ALU.add).then_inc(s.final, 1)
                dve.wait_ge(s.final, 2 * q + 1)
                dve.tensor_tensor(x, x, bo.unsqueeze(1).to_broadcast([P, TILES // 4, D]), ALU.add)\
                   .then_inc(s.final, 1)

        @block.sync
        def _(sp):
            for q in range(4):
                rows = slice(q * TILES // 4, (q + 1) * TILES // 4)
                sp.wait_ge(s.final, 2 * q + 2)
                sp.dma_start(out.rearrange("(t p) d -> p t d", p=P)[:, rows, :], m.x[:, rows, :])\
                  .then_inc(m.stored, 16)
            sp.wait_ge(m.stored, 64)


def moe_semaphores(sem, k):
    s = Names()
    s.group_sb = sem(f"moe{k}_group_sb")
    s.normed = sem(f"moe{k}_normed")
    s.logit_ps = sem(f"moe{k}_logit_ps")
    s.turned = sem(f"moe{k}_turned")
    s.route = sem(f"moe{k}_route")
    s.hot = sem(f"moe{k}_hot")
    s.gate_in = sem(f"moe{k}_gate_in")
    s.gate_exp = sem(f"moe{k}_gate_exp")
    s.prefix = sem(f"moe{k}_prefix")
    s.scattered = sem(f"moe{k}_scattered")
    s.added = sem(f"moe{k}_added")
    s.x_turned = sem(f"moe{k}_x_turned")
    s.y_row = sem(f"moe{k}_y_row")
    s.shared = sem(f"moe{k}_shared")
    s.shared_in = sem(f"moe{k}_shared_in")
    s.x_split = sem(f"moe{k}_x_split")
    s.h_ps = sem(f"moe{k}_h_ps")
    s.h_split = sem(f"moe{k}_h_split")
    s.y_ps = sem(f"moe{k}_y_ps")
    s.x_hi = sem(f"moe{k}_x_hi")
    s.h_act = sem(f"moe{k}_h_act")
    s.h_f = sem(f"moe{k}_h_f")
    s.h_hi = sem(f"moe{k}_h_hi")
    s.x_row = [sem(f"moe{k}_x_row{u}") for u in range(UNROLL)]
    s.y_done = [sem(f"moe{k}_y_done{u}") for u in range(UNROLL)]
    s.fetched = [sem(f"moe{k}_fetched{u}") for u in range(8)]
    return s


def bias0_semaphores(sem):
    s = Names()
    s.bias_in = sem("bias0_bias_in")
    s.bias_step = sem("bias0_bias_step")
    s.bias_rows = sem("bias0_bias_rows")
    s.rows_clear = sem("bias0_rows_clear")
    return s


def diag_semaphores(sem):
    s = Names()
    s.weights = sem("diag_weights")
    s.y_ps = sem("diag_y_ps")
    s.wvo_ps = sem("diag_wvo_ps")
    s.wvo = sem("diag_wvo")
    s.added = sem("diag_added")
    s.ctx = [sem("diag_ctx0"), sem("diag_ctx1")]
    return s


def quant_semaphores(sem):
    s = Names()
    s.weights = sem("quant_weights")
    s.step = sem("quant_step")
    s.step2 = sem("quant_step2")
    s.normed = sem("quant_normed")
    s.ext = sem("quant_ext")
    s.ext_all = sem("quant_ext_all")
    s.turned = sem("quant_turned")
    s.xqT = sem("quant_xqT")
    s.h_ps = sem("quant_h_ps")
    s.gelu = sem("quant_gelu")
    s.h_ext = sem("quant_h_ext")
    s.hq_step = sem("quant_hq_step")
    s.hq = sem("quant_hq")
    s.y_ps = sem("quant_y_ps")
    s.added = sem("quant_added")
    return s


def chosen_semaphores(sem):
    s = Names()
    s.weights = sem("chosen_weights")
    s.bias_in = sem("chosen_bias_in")
    s.bias_step = sem("chosen_bias_step")
    s.bias_rows = sem("chosen_bias_rows")
    s.rows_clear = sem("chosen_rows_clear")
    s.xT_lo = sem("chosen_xT_lo")
    s.xT_hi = sem("chosen_xT_hi")
    s.copied = sem("chosen_copied")
    s.normed = sem("chosen_normed")
    s.turned = sem("chosen_turned")
    s.nav_ps = sem("chosen_nav_ps")
    s.nav = sem("chosen_nav")
    s.pick = sem("chosen_pick")
    s.h_ps = sem("chosen_h_ps")
    s.h_split = sem("chosen_h_split")
    s.r_ps = sem("chosen_r_ps")
    s.reasoned = sem("chosen_reasoned")
    s.y_ps = sem("chosen_y_ps")
    s.gelu = sem("chosen_gelu")
    s.h_hi = sem("chosen_h_hi")
    s.y_free = sem("chosen_y_free")
    s.final = sem("chosen_final")
    return s


def build(nc, d, out):
    m = Names()
    m.ln_count = m.whole_count = 0
    with ExitStack() as ctx:
        def sb(name, shape, dt=F32):
            return ctx.enter_context(nc.sbuf_tensor(name, shape, dt))

        def ps(name):
            return ctx.enter_context(nc.psum_tensor(name, [P, 512], F32))

        def sem(name):
            return ctx.enter_context(nc.semaphore(name))

        m.d = d
        m.ctxT_dram = d["ctxT"]
        m.x = sb("x", [P, TILES, D])
        m.xn2 = sb("xn", [P, 2, GT, D])
        m.xnT2 = sb("xnT", [P, 2, GTOK])
        m.xn, m.xnT = m.xn2[:, 0, :, :], m.xnT2[:, 0, :]
        m.big = sb("big", [P, 16384])
        m.stage = m.big[:, 0:4096].rearrange("p (a n) -> p a n", a=2)
        m.w_hi = sb("w_hi", [P, 3 * EXPERTS * F], F16)
        m.w_lo = sb("w_lo", [P, 3 * EXPERTS * F], F16)
        m.b1_rows = sb("b1_rows", [P, EXPERTS * F], BF16)
        m.b2_rows = sb("b2_rows", [P, EXPERTS * D], BF16)
        m.ones3 = sb("ones3", [P, P], BF16)
        m.ones_b = sb("ones_b", [P, P], BF16)
        m.above = sb("above", [P, P], BF16)
        m.rev_index = sb("rev_index", [P, EXPERTS])
        m.tile_index = sb("tile_index", [P, SLOT_TILES])
        m.sorted_in = nc.dram_tensor("sorted_in", [SLOT_TILES * P, D], F32, kind="Internal").ap()
        m.sorted_out = nc.dram_tensor("sorted_out", [SLOT_TILES * P, D], F32, kind="Internal").ap()
        m.ln_stats = sb("ln_stats", [P, 2, GT, 6])
        m.ln_work = sb("ln_work", [P, 2, 8, GT])
        m.whole_stats = m.big[:, 15000:15000 + TILES * 6].rearrange("p (t s) -> p t s", t=TILES)
        m.whole_work = m.big[:, 15200:15200 + TILES * 8].rearrange("p (w t) -> p w t", w=8)
        m.eps = sb("eps", [P, TILES])
        m.minus_half = sb("minus_half", [P, TILES])
        m.ident = sb("ident", [P, P])
        m.ident_b = sb("ident_b", [P, P], BF16)
        att = Region(m.big, 4096)
        m.ctx = att.take((2, 2 * GT, 2, S))
        m.qbd = att.take((2, 2, GTOK))
        kexp = sb("kexp", [P, 2 * 2 * GT * HQ * S])
        m.kexp_buffer = kexp
        m.quant = sb("quant", [P, 2300])
        m.xall = kexp[:, :].rearrange("p (t d) -> p t d", t=TILES)
        m.kexp = kexp[:, :].rearrange("p (a g t h k) -> p a g t h k", a=2, g=2, t=GT, h=HQ)
        m.v2 = sb("v2", [P, 2, GT, 2, HEADS, DH + 1])
        m.neg_max = sb("neg_max", [P, 4, 2 * HQ], BF16)
        m.prob = att.take((2, 512))
        m.pT = att.take((2, 512))
        m.o_raw = sb("o_raw", [P, 2, HEADS, DH + 1])
        m.o_rec = sb("o_rec", [P, 2, HEADS])
        m.o_norm = sb("o_norm", [P, 2, D])
        m.oT = sb("oT", [P, 2 * P])
        m.batch_mask = sb("batch_mask", [P, GTOK])
        m.head_mask = sb("head_mask", [P, HQ])
        m.value_mask = sb("value_mask", [P, D])
        m.penalty = sb("penalty", [P, TILES, S], BF16)
        m.mask_in = att.take((TILES, S), I32)
        m.score = [ps(f"score{g}") for g in range(4)]
        m.pT_ps = ps("pT_ps")
        m.out_ps = [ps("out_ps0"), ps("out_ps1")]
        m.misc = ps("misc")
        m.xn_ready = sem("xn_ready")
        m.ln_step = sem("ln_step")
        m.whole_rows = sem("whole_rows")
        m.ln_eps_added = sem("ln_eps_added")
        m.ln_rstd_ready = sem("ln_rstd_ready")
        m.filled = sem("filled")
        m.emptied = sem("emptied")
        m.scored = sem("scored")
        m.maxed = sem("maxed")
        m.shifted = sem("shifted")
        m.probs = sem("probs")
        m.turned = sem("turned")
        m.turned_out = sem("turned_out")
        m.valued = sem("valued")
        m.o_copied = sem("o_copied")
        m.o_rec_ready = sem("o_rec_ready")
        m.o_ready = sem("o_ready")
        m.consts = sem("consts")
        m.x_in = sem("x_in")
        m.att_w = sem("att_w")
        m.bias_ps = sem("bias_ps")
        m.stored = sem("stored")
        m.zeroed = sem("zeroed")
        m.split_step = sem("split_step")
        m.zero_tile = sem("zero_tile")
        m.staged = [sem("staged0"), sem("staged1")]
        m.s_moe = [moe_semaphores(sem, k) for k in range(2)]
        m.s_bias0 = bias0_semaphores(sem)
        m.s_diag = diag_semaphores(sem)
        m.s_quant = quant_semaphores(sem)
        m.s_chosen = chosen_semaphores(sem)
        moes, chunk0 = [], 0
        for weights, chunks in ((d["moe0_w"], 4), (d["moe1_w"], 6), (d["chosen_w"], 2)):
            c = Names()
            c.weights, c.chunks, c.chunk0 = weights, chunks, chunk0
            chunk0 += chunks
            moes.append(c)
        for k, c in enumerate(moes[0:2]):
            c.router = sb(f"router{k}", [P, EXPERTS])
        m.ctx_loaded = [sem("ctx_loaded0"), sem("ctx_loaded1")]

        ws = []
        for a, layer in enumerate((0, 1, 3)):
            w = Names()
            w.wq = sb(f"wq{a}", [P, 2, P])
            w.wk = sb(f"wk{a}", [P, 2, 2, P])
            w.wv = sb(f"wv{a}", [P, D])
            w.wo = sb(f"wo{a}", [P, D])
            w.bq = sb(f"bq{a}", [P, 2])
            w.bk = sb(f"bk{a}", [P, 2])
            w.bk_heads = sb(f"bk_heads{a}", [P, 2, HQ])
            if a:
                w.bv = sb(f"bv{a}", [P, 1])
                w.bo = sb(f"bo{a}", [P, D])
                w.out_bias = sb(f"out_bias{a}", [P, D])
            w.layer = layer
            ws.append(w)

        setup = Region(m.big, att.at)
        bias_f = setup.take((2, 32))
        bias_b = setup.take((3, 2, 32), BF16)
        zero_tile = setup.take((P,))
        consts_in = setup.take((3 * P,))
        FIRST = 2 * GT

        with nc.Block(no_gpsimd_drain=True) as block:
            @block.sync
            def _(sp):
                x = d["x"].rearrange("(t p) d -> p t d", p=P)
                sp.dma_start(m.x[:, 0:FIRST, :], x[:, 0:FIRST, :]).then_inc(m.x_in, 16)
                sp.dma_start(m.ident[:, :], d["ident"]).then_inc(m.consts, 16)
                sp.dma_start(m.batch_mask[:, :], d["batch_mask"]).then_inc(m.consts, 16)
                sp.dma_start(m.head_mask[:, :], d["head_mask"]).then_inc(m.consts, 16)
                sp.dma_start(m.value_mask[:, :], d["value_mask"]).then_inc(m.consts, 16)

            @block.scalar
            def _(act):
                load_attention_weights(act, m, ws[0], False)

            @block.vector
            def _(dve):
                dve.memset(m.eps[:, :], EPS)
                dve.memset(m.minus_half[:, :], -0.5)
                dve.memset(ws[0].bq[:, :], 0.0)
                dve.memset(ws[0].bk_heads[:, :, :], 0.0)
                dve.memset(zero_tile, 0.0).then_inc(m.zero_tile, 1)
                clear_bias_rows(dve, m, m.s_bias0, bias_f)
                dve.wait_ge(m.consts, 64)
                dve.tensor_copy(m.ident_b[:, :], m.ident[:, :])
                for par in range(2):
                    for t in range(GT):
                        dve.tensor_copy(m.v2[:, par, t, :, :, DH],
                                        m.value_mask[:, 0:D:DH].unsqueeze(1).to_broadcast([P, 2, HEADS]))
                dve.wait_ge(m.x_in, 16)
                dve.wait_ge(m.att_w, 64)

        def later_loads(sp):
            x = d["x"].rearrange("(t p) d -> p t d", p=P)
            sp.dma_start(m.x[:, FIRST:, :], x[:, FIRST:, :]).then_inc(m.x_in, 16)
            sp.dma_start(m.mask_in[:, :, :], d["mask"].rearrange("(t p) k -> p t k", p=P)).then_inc(m.consts, 16)
            sp.dma_start(consts_in, d["consts"]).then_inc(m.consts, 16)
            sp.dma_start(m.rev_index[:, :], d["rev_index"].partition_broadcast(P)).then_inc(m.consts, 16)
            sp.dma_start(m.tile_index[:, :], d["tile_index"].partition_broadcast(P)).then_inc(m.consts, 16)
            for k, c in enumerate(moes[0:2]):
                sp.dma_start(c.router[:, :], d[f"router{k}"]).then_inc(m.consts, 16)
            for w in ws[1:]:
                load_attention_weights(sp, m, w, True)
            sp.wait_ge(m.zero_tile, 1)
            sp.dma_start(m.sorted_in.rearrange("(t p) d -> p t d", p=P),
                         zero_tile.unsqueeze(1).to_broadcast([P, SLOT_TILES, P])).then_inc(m.zeroed, 16)

        def later_rows(sp):
            load_bias_rows(sp, m, m.s_bias0, bias_f, bias_b, d["moe0_b1"], d["moe0_b2"])

        def later_split(pool):
            split_bias_rows(pool, m, m.s_bias0, bias_f, bias_b)

        def later_constants(dve):
            dve.wait_ge(m.consts, 64 + 16 * 6)
            dve.tensor_copy(m.ones3[:, :], consts_in[:, 0:P])
            dve.tensor_copy(m.ones_b[:, :], consts_in[:, P:2 * P])
            dve.tensor_copy(m.above[:, :], consts_in[:, 2 * P:3 * P])
            dve.tensor_scalar(m.penalty[:, :, :], m.mask_in[:, :, :], 0, MASKED, ALU.is_equal, ALU.mult)
            dve.wait_ge(m.att_w, 16 * 20)
            for w in ws[1:]:
                for gp in range(2):
                    dve.tensor_scalar(w.bk_heads[:, gp, :], m.head_mask[:, :], w.bk[:, gp:gp + 1], None, ALU.mult)

        def later_products(pe):
            pe.wait_ge(m.att_w, 16 * 20)
            pe.wait_ge(m.emptied, FILLS)
            for a, w in enumerate(ws[1:]):
                mm = pe.matmul(m.misc[:, a * D:(a + 1) * D], w.bv[:, :].to_broadcast([P, P]), w.wo[:, :],
                               start=True, stop=True, skip_group_check=True)
            mm.then_inc(m.bias_ps, 1)

        def later_biases(dve):
            dve.wait_ge(m.bias_ps, 1)
            for a, w in enumerate(ws[1:]):
                dve.tensor_tensor(w.out_bias[:, :], m.misc[:, a * D:(a + 1) * D], w.bo[:, :], ALU.add)

        later = Names()
        later.loads, later.rows, later.split = later_loads, later_rows, later_split
        later.constants, later.products, later.biases = later_constants, later_products, later_biases

        attention(nc, m, 0, ws[0], masked=False, biased=False, experts=moes[0], later=later)
        routed = moe(nc, m, 0, moes[0])
        attention(nc, m, 1, ws[1], masked=True, biased=True, experts=moes[1], fetch=routed)
        quantized_ffn(nc, m)
        diagonal_attention(nc, m)
        routed = moe(nc, m, 1, moes[1])
        attention(nc, m, 2, ws[2], masked=False, biased=True, experts=moes[2], fetch=routed)
        chosen_ffn(nc, m, out)


def _layout(i):
    f = {k: np.asarray(v) for k, v in i.items()}
    r = np.arange(P)
    d = {"ident": np.eye(P, dtype=np.float32)}
    d["batch_mask"] = (r[:, None] % 64 // 32 == np.arange(GTOK) // S % 2).astype(np.float32)
    d["head_mask"] = (r[:, None] % 32 // DH == np.arange(HQ)).astype(np.float32)
    d["value_mask"] = (r[:, None] // S == r[None, :] // DH % 2).astype(np.float32)
    d["x"] = f["x"].reshape(TOKENS, D)
    d["ctxT"] = f["ctx_1024"].reshape(TOKENS, D).T
    d["mask"] = f["mask_BxSxS2_ik1"].reshape(TOKENS, S)
    d["consts"] = np.concatenate([np.repeat((r < 3)[:, None], P, 1), np.ones((P, P)), r[:, None] < r[None, :]],
                                 1).astype(np.float32)
    d["rev_index"] = (EXPERTS - np.arange(EXPERTS)).astype(np.float32)
    d["tile_index"] = np.arange(SLOT_TILES).astype(np.float32)
    def up_of(w):
        return w.transpose(1, 0, 2).reshape(D, EXPERTS * F)

    def down_of(w):
        return w.reshape(EXPERTS, FB, P, D).transpose(2, 0, 1, 3).reshape(P, EXPERTS * F)
    d["router0"], d["router1"] = f["L0_ffn_router_w"].T, f["L2_ffn_router_w"]
    d["moe0_w"] = np.concatenate([up_of(f["L0_ffn_w1"].transpose(0, 2, 1)),
                                  down_of(f["L0_ffn_w2"].transpose(0, 2, 1))], 1)
    d["moe0_b1"], d["moe0_b2"] = f["L0_ffn_b1"].reshape(P, -1), f["L0_ffn_b2"].reshape(P, -1)
    both = [np.concatenate([f[f"L2_ffn_{n}_w"], f[f"L2_ffn_shared_{n}_w"][None]]) for n in ("up", "gate", "down")]
    d["moe1_w"] = np.concatenate([up_of(both[0]), up_of(both[1]), down_of(both[2])], 1)
    d["quant_w1"] = f["L1_ffn_W1"].T
    d["quant_w2"] = f["L1_ffn_W2"].T.reshape(FB, P, D).transpose(1, 0, 2).reshape(P, F)
    d["quant_b1"], d["quant_b2"] = f["L1_ffn_b1"].reshape(FB, P).T, f["L1_ffn_b2"]
    wide = DIAG_BLOCKS * P
    d["diag_wvT"] = f["L2_xattn_Wkv"][:, wide:].T.reshape(DIAG_BLOCKS, P, D).transpose(1, 0, 2).reshape(P, -1)
    d["diag_wout"] = f["L2_xattn_Wout"].reshape(DIAG_BLOCKS, P, D).transpose(1, 0, 2).reshape(P, -1)
    d["diag_bout"] = f["L2_xattn_bout"]
    d["chosen_w"] = np.concatenate([f["L3_ffn_W1"].transpose(1, 0, 2).reshape(D, -1),
                                    f["L3_ffn_W2"].reshape(EXPERTS, FB3, P, D).transpose(2, 0, 1, 3).reshape(P, -1)], 1)
    d["chosen_b1"], d["chosen_b2"] = f["L3_ffn_b1"].reshape(P, -1), f["L3_ffn_b2"].reshape(P, -1)
    d["chosen_wp1"], d["chosen_wp2"], d["chosen_wo"] = f["L3_ffn_Wp1"], f["L3_ffn_Wp2"], f["L3_ffn_Wo"]
    d["chosen_bp1"], d["chosen_bp2"], d["chosen_bo"] = f["L3_ffn_bp1"].reshape(P, 1), f["L3_ffn_bp2"], f["L3_ffn_bo"]
    w0 = f["L0_xattn_Wkv"]
    att = {0: (f["L0_xattn_Wq"], w0[:, :D], w0[:, D:], f["L0_xattn_Wout"]),
           1: tuple(f[f"L1_xattn_W{c}"] for c in "qkvo"),
           3: tuple(f[f"L3_xattn_W{c}"].T for c in "qkvo")}
    for n, (wq, wk, wv, wo) in att.items():
        def blocks(w):
            return w.reshape(-1, 2, 2, 32)
        d[f"wq{n}"] = np.stack([blocks(wq)] * 2, axis=3).reshape(D, 2 * P)
        k, z = blocks(wk), np.zeros_like(blocks(wk))
        d[f"wk{n}"] = np.stack([np.stack([k, z], 3), np.stack([z, k], 3)], 1).reshape(D, 4 * P)
        d[f"wv{n}"], d[f"wo{n}"] = wv, wo
        if n:
            for c in "qk":
                b = f[f"L{n}_xattn_b{c}"].reshape(2, 2, 32)
                d[f"b{c}{n}"] = np.stack([b] * 2, axis=2).reshape(2, P).T
            d[f"bv{n}"] = f[f"L{n}_xattn_bv"].reshape(D, 1)
            d[f"bo{n}"] = f[f"L{n}_xattn_bo"]
    return {k: np.ascontiguousarray(v) for k, v in d.items()}


def kernel(**inputs):
    import concourse.bacc as bacc
    from concourse.bass_utils import run_bass_kernel_spmd

    nc = bacc.Bacc("TRN2", target_bir_lowering=False, num_devices=1)
    arrays = _layout(inputs)
    d = {k: nc.dram_tensor(f"in_{k}", v.shape, mybir.dt.from_np(v.dtype), kind="ExternalInput").ap()
         for k, v in arrays.items()}
    out = nc.dram_tensor("out", (TOKENS, D), F32, kind="ExternalOutput").ap()
    build(nc, d, out)
    r = run_bass_kernel_spmd(nc, [{f"in_{k}": v for k, v in arrays.items()}], core_ids=[0])
    return r.results[0]["out"].reshape(B, S, D)
```

```python
from contextlib import ExitStack

import numpy as np
import concourse.bass as bass
from concourse import mybir

ALU = mybir.AluOpType
ACT = mybir.ActivationFunctionType
AX_X = mybir.AxisListType.X
F32 = mybir.dt.float32
BF16 = mybir.dt.bfloat16
F16 = mybir.dt.float16
I32 = mybir.dt.int32

P = 128
D = 128
B, S = 64, 64
TOKENS = B * S
TILES = TOKENS // P
GT = 4
GROUPS = TILES // GT
GTOK = GT * P
HEADS = 16
DH = D // HEADS
HQ = 32 // DH
ATT_SCALE = float(DH) ** -0.5
EPS = 1e-5
MASKED = -float(2 ** 31)
STEPS = 16


class Names:
    pass


LN_STEPS = 4


def group_statistics(dve, m, g, par, done):
    n0 = LN_STEPS * done
    stats, work = m.ln_stats[:, par, :, :], m.ln_work[:, par, :, :]
    even_mean, even_m2, odd_mean, odd_m2 = (stats[:, :, i] for i in (1, 2, 4, 5))
    both, diff, m2, sq, mean, var = (work[:, i, :] for i in range(6))
    for t in range(GT):
        last = dve.bn_stats(stats[:, t, :], flat(m.x[:, bass.ds(GT * g + t, 1), :]))
    last.then_inc(m.ln_step, 1)
    dve.wait_ge(m.ln_step, n0 + 1)
    dve.tensor_tensor(both, even_mean, odd_mean, ALU.add)
    dve.tensor_tensor(diff, even_mean, odd_mean, ALU.subtract)
    dve.tensor_tensor(m2, even_m2, odd_m2, ALU.add).then_inc(m.ln_step, 1)
    dve.wait_ge(m.ln_step, n0 + 2)
    dve.scalar_tensor_tensor(out=sq, in0=diff, scalar=0.25, in1=diff, op0=ALU.mult, op1=ALU.mult)
    dve.tensor_scalar(mean, both, 0.5, None, ALU.mult).then_inc(m.ln_step, 1)
    dve.wait_ge(m.ln_step, n0 + 3)
    dve.scalar_tensor_tensor(out=var, in0=m2, scalar=1.0 / D, in1=sq, op0=ALU.mult,
                             op1=ALU.add).then_inc(m.ln_step, 1)


def group_power(pool, m, par, done):
    pool.wait_ge(m.ln_step, LN_STEPS * (done + 1))
    pool.tensor_tensor(m.ln_work[:, par, 6, :], m.ln_work[:, par, 5, :], m.eps[:, 0:GT],
                       ALU.add).then_inc(m.ln_eps_added, 1)
    pool.wait_ge(m.ln_eps_added, done + 1)
    pool.tensor_tensor(m.ln_work[:, par, 7, :], m.ln_work[:, par, 6, :], m.minus_half[:, 0:GT],
                       ALU.pow).then_inc(m.ln_rstd_ready, 1)


def group_normalise(dve, m, g, par, out, done):
    dve.wait_ge(m.ln_rstd_ready, done + 1)
    for t in range(GT):
        last = dve.tensor_scalar(out(t), flat(m.x[:, bass.ds(GT * g + t, 1), :]), m.ln_work[:, par, 4, t:t + 1],
                                 m.ln_work[:, par, 7, t:t + 1], ALU.subtract, ALU.mult)
    return last


def whole_statistics(dve, m, done, made=False):
    n0 = LN_STEPS * done
    m.ln_count += GROUPS
    even_mean, even_m2, odd_mean, odd_m2 = (m.whole_stats[:, :, i] for i in (1, 2, 4, 5))
    both, diff, m2, sq, mean, var = (m.whole_work[:, i, :] for i in range(6))
    if not made:
        m.whole_count += 1
        for t in range(TILES):
            last = dve.bn_stats(m.whole_stats[:, t, :], m.x[:, t, :])
        last.then_inc(m.whole_rows, 1)
        dve.wait_ge(m.whole_rows, m.whole_count)
    dve.tensor_tensor(both, even_mean, odd_mean, ALU.add)
    dve.tensor_tensor(diff, even_mean, odd_mean, ALU.subtract)
    dve.tensor_tensor(m2, even_m2, odd_m2, ALU.add).then_inc(m.ln_step, 1)
    dve.wait_ge(m.ln_step, n0 + 1)
    dve.scalar_tensor_tensor(out=sq, in0=diff, scalar=0.25, in1=diff, op0=ALU.mult, op1=ALU.mult)
    dve.tensor_scalar(mean, both, 0.5, None, ALU.mult).then_inc(m.ln_step, 1)
    dve.wait_ge(m.ln_step, n0 + 2)
    dve.scalar_tensor_tensor(out=var, in0=m2, scalar=1.0 / D, in1=sq, op0=ALU.mult,
                             op1=ALU.add).then_inc(m.ln_step, LN_STEPS * GROUPS - 2)


def whole_power(pool, m, done, use=None):
    pool.wait_ge(m.ln_step, LN_STEPS * (done + GROUPS))
    pool.tensor_tensor(m.whole_work[:, 6, :], m.whole_work[:, 5, :], m.eps[:, :], ALU.add)\
        .then_inc(m.ln_eps_added, GROUPS)
    pool.wait_ge(m.ln_eps_added, done + GROUPS)
    for g in range(GROUPS):
        tiles = slice(g * GT, (g + 1) * GT)
        pool.tensor_tensor(m.whole_work[:, 7, tiles], m.whole_work[:, 6, tiles], m.minus_half[:, tiles],
                           ALU.pow).then_inc(m.ln_rstd_ready, 1)
        if use and g >= 2:
            use(g - 2)
    if use:
        use(GROUPS - 2)
        use(GROUPS - 1)


def normalise(dve, m, g, done, out):
    dve.wait_ge(m.ln_rstd_ready, done + g + 1)
    for t in range(GT):
        at = bass.ds(GT * g + t, 1)
        last = dve.tensor_scalar(out(t), flat(m.x[:, at, :]), m.whole_work[:, 4, at], m.whole_work[:, 7, at],
                                 ALU.subtract, ALU.mult)
    return last


FRONT = ("K", "xT", "Q0", "Q1", "V0", "V1")
FRONT_EARLY_X = ("xT", "Q0", "Q1", "K", "V0", "V1")
FRONT_LATE_X = ("K", "V0", "V1", "xT", "Q0", "Q1")
FRONT_STEPS = (0, 2, 3, 4, 5, 6)


def fills(step, first, last):
    j, before, after = step % 8, [], []
    for k in range(0 if first else -2, 4 if last else 3):
        if step == 4 * k + 7:
            before.append(("OT", k))
        if step == 4 * k + 8:
            before.append(("Y", k))
    if step < STEPS and not (last and step >= 8) and j in FRONT_STEPS:
        after.append((FRONT[FRONT_STEPS.index(j)], 0))
    return before, after


def fill_numbers(first, last):
    n, numbers = 0, {}
    for step in steps_of(last):
        for where, part in enumerate(fills(step, first, last)):
            for f in part:
                numbers[step, where, f] = n
                n += 1
    return numbers, n


def steps_of(last):
    return range(STEPS + 5 if last else STEPS)


BODIES = GROUPS // 2
KINDS = ((True, False), (False, False), (False, True))
NUMBERS = {kind: fill_numbers(*kind)[0] for kind in KINDS}
PER_FIRST, PER_BODY, PER_LAST = (fill_numbers(*kind)[1] for kind in KINDS)
FILLS = len(FRONT) + PER_FIRST + (BODIES - 2) * PER_BODY + PER_LAST


def fills_before(it):
    if isinstance(it, int) and it == 0:
        return len(FRONT)
    return (it * PER_BODY) + (len(FRONT) + PER_FIRST - PER_BODY)


ATT_STEPS = GROUPS * 8


def load_attention_weights(queue, m, w, biased):
    d, n = m.d, w.layer
    queue.dma_start(w.wq[:, :, :], d[f"wq{n}"].rearrange("c (g r) -> c g r", g=2)).then_inc(m.att_w, 16)
    queue.dma_start(w.wk[:, :, :, :], d[f"wk{n}"].rearrange("c (b g r) -> c b g r", g=2, b=2)).then_inc(m.att_w, 16)
    queue.dma_start(w.wv[:, :], d[f"wv{n}"]).then_inc(m.att_w, 16)
    queue.dma_start(w.wo[:, :], d[f"wo{n}"]).then_inc(m.att_w, 16)
    if biased:
        queue.dma_start(w.bq[:, :], d[f"bq{n}"]).then_inc(m.att_w, 16)
        queue.dma_start(w.bk[:, :], d[f"bk{n}"]).then_inc(m.att_w, 16)
        queue.dma_start(w.bv[:, :], d[f"bv{n}"]).then_inc(m.att_w, 16)
        queue.dma_start(w.bo[:, :], d[f"bo{n}"].partition_broadcast(P)).then_inc(m.att_w, 16)


def attention(nc, m, a, w, masked, biased, experts, later=None, fetch=None):
    fill0, step0, ln0, ctx0 = a * FILLS, a * ATT_STEPS, m.ln_count, a * GROUPS
    pair0 = a * 2 * GROUPS
    front_first = FRONT_LATE_X if fetch else FRONT_EARLY_X
    ctx_dma0 = a * 32 * GROUPS // 2
    m.ln_count += GROUPS
    with nc.Block(no_gpsimd_drain=True) as block:

        @block.sync
        def _(sp):
            def load_ctx(g, par):
                for copy in range(2):
                    sp.dma_start(m.ctx[:, par, :, copy, :], m.ctxT_dram[:, bass.ds(g * GTOK, GTOK)]
                                 .rearrange("d (c k) -> d c k", k=S)).then_inc(m.ctx_loaded[par], 16)
            load_ctx(0, 0)
            load_ctx(1, 1)
            if later:
                later.loads(sp)
            sp.wait_ge(m.filled, fill0 + len(FRONT))
            load_ctx(2, 0)

            def body(it, first, more):
                base = fill0 + fills_before(it)
                numbers = NUMBERS[first, False]
                sp.wait_ge(m.filled, base + (numbers[6, 1, ("V1", 0)] + 1))
                load_ctx(2 * it + 3, 1)
                if more:
                    sp.wait_ge(m.filled, base + (numbers[14, 1, ("V1", 0)] + 1))
                    load_ctx(2 * it + 4, 0)
            body(0, True, True)
            with sp.Fori(1, BODIES - 2) as it:
                body(it, False, True)
            body(BODIES - 2, False, False)
            if later:
                later.rows(sp)

        @block.tensor
        def _(pe):
            def front(f, par):
                if f == "xT":
                    for t in range(GT):
                        mm = pe.transpose(m.misc[:, t * P:(t + 1) * P], m.xn[:, t, :], m.ident[:, :])
                elif f in ("Q0", "Q1"):
                    mm = pe.matmul(m.misc[:, :], w.wq[:, int(f[1]), :], m.xnT[:, :], start=True, stop=True)
                elif f == "K":
                    for gp in range(2):
                        for b in range(2):
                            mm = pe.matmul(m.misc[:, gp * 256:(gp + 1) * 256], w.wk[:, b, gp, :],
                                           m.ctx[:, par, b::2, 0, :], start=(gp == 0 and b == 0),
                                           stop=(b == 1), skip_group_check=True)
                else:
                    for u in range(2):
                        for b in range(2):
                            c = (2 * u + b) * D
                            lhsT = m.ctx[:, par, 4 * int(f[1]) + 2 * u + b, :, :].rearrange("p c k -> p (c k)")
                            mm = pe.matmul(m.misc[:, c:c + D], lhsT, w.wv[:, :], start=True, stop=True,
                                           skip_group_check=True)
                mm.then_inc(m.filled, 1)

            def front_wait(f, par, g_expr, ctx_count, n):
                pe.wait_ge(m.emptied, n)
                if f == "xT":
                    pe.wait_ge(m.xn_ready, ctx0 + g_expr + 1)
                if f == "K":
                    pe.wait_ge(m.ctx_loaded[par], ctx_count)

            def out_part(kind, n, pair):
                pe.wait_ge(m.emptied, n)
                if kind == "OT":
                    pe.wait_ge(m.o_ready, pair + 1)
                    for u in range(2):
                        mm = pe.transpose(m.misc[:, u * P:(u + 1) * P], m.o_norm[:, u, :], m.ident[:, :])
                else:
                    for u in range(2):
                        mm = pe.matmul(m.misc[:, u * D:(u + 1) * D], m.oT[:, u * P:(u + 1) * P], w.wo[:, :],
                                       start=True, stop=True, skip_group_check=True)
                mm.then_inc(m.filled, 1)

            def scores(s, tile, par, ready):
                q, g = s // 4 % 2, s % 4
                if ready is not None:
                    pe.wait_ge(m.emptied, ready)
                rows = slice(64 * (g % 2), 64 * (g % 2) + 64)
                for u in range(2):
                    t = 2 * q + u
                    mm = pe.matmul(m.score[g][:, u * 256:(u + 1) * 256],
                                   m.qbd[rows, par, g // 2, t * P:(t + 1) * P],
                                   m.kexp[rows, par, g // 2, t, :, :].rearrange("p h k -> p (h k)"),
                                   start=(u == 0), stop=True, skip_group_check=True)
                if masked:
                    mm = pe.matmul(m.score[g][:, :], m.ident_b[:, :],
                                   m.penalty[:, bass.ds(tile, 2), :].unsqueeze(2).to_broadcast([P, 2, HQ, S]),
                                   start=False, stop=True, skip_group_check=True)
                mm.then_inc(m.scored, 1)

            def shift(s, n):
                pe.wait_ge(m.maxed, n + 1)
                pe.matmul(m.score[s % 4][:, :], m.ident_b[:, :],
                          m.neg_max[:, s % 4, :].unsqueeze(2).to_broadcast([P, 2 * HQ, S]),
                          start=False, stop=True, skip_group_check=True).then_inc(m.shifted, 1)

            def turn(s, n):
                pe.wait_ge(m.probs, n + 1)
                pe.wait_ge(m.turned_out, n)
                for x in range(4):
                    mm = pe.transpose(m.pT_ps[:, x * P:(x + 1) * P], m.prob[:, s % 2, x * P:(x + 1) * P],
                                      m.ident[:, :])
                mm.then_inc(m.turned, 1)

            def values(s, n, par, pair, ready):
                q, g = s // 4 % 2, s % 4
                pe.wait_ge(m.turned_out, n + 1)
                if s % 8 == 0:
                    pe.wait_ge(m.emptied, ready)
                if g == 0:
                    pe.wait_ge(m.o_copied, pair)
                for u in range(2):
                    for x in range(2):
                        slot = 2 * g + x
                        mm = pe.matmul(m.out_ps[u][:, slot * 36:(slot + 1) * 36],
                                       m.pT[:, s % 2, (2 * u + x) * P:(2 * u + x + 1) * P],
                                       m.v2[:, par, 2 * q + u, :, 2 * slot:2 * slot + 2, :]
                                       .rearrange("p b h e -> p b (h e)"),
                                       start=True, stop=True, skip_group_check=True)
                mm.then_inc(m.valued, 1)

            for i, f in enumerate(front_first):
                front_wait(f, 0, 0, ctx_dma0 + 32, fill0 + i)
                front(f, 0)
            scores(0, 0, 0, fill0 + len(FRONT))
            scores(1, 0, 0, None)
            shift(0, step0)

            def body(it, first, last):
                numbers = NUMBERS[first, last]
                base = fill0 + fills_before(it)
                n0 = step0 + it * STEPS
                for s in steps_of(last):
                    for where, part in enumerate(fills(s, first, last)):
                        if where == 1:
                            if s + 2 < STEPS or not last:
                                t = s + 2
                                scores(t, 8 * it + 2 * (t // 4), t // 8 % 2,
                                       base + (numbers[t - 4, 1, ("Q1", 0)] + 1) if t % 8 == 0 else None)
                            if s + 1 < STEPS or not last:
                                shift(s + 1, n0 + s + 1)
                            if s < STEPS:
                                turn(s, n0 + s)
                        for f in part:
                            n = base + numbers[s, where, f]
                            if f[0] in ("OT", "Y"):
                                out_part(f[0], n, pair0 + 4 * it + f[1])
                            else:
                                par = (s // 8 + 1) % 2
                                front_wait(f[0], par, 2 * it + s // 8 + 1,
                                           ctx_dma0 + 32 * (it + 1 + s // 8), n)
                                front(f[0], par)
                    if (s or not first) and s <= STEPS:
                        values(s - 1, n0 + (s - 1), (s - 1) // 8 % 2, pair0 + 4 * it + (s - 1) // 4,
                               base if s == 1 else base + (numbers[6, 1, ("V1", 0)] + 1))

            body(0, True, False)
            with pe.Fori(1, BODIES - 1) as it:
                body(it, False, False)
            body(BODIES - 1, False, True)
            if later:
                later.products(pe)

        @block.scalar
        def _(act):
            def take(f, n):
                if f == "xT":
                    act.wait_ge(m.filled, n + 1)
                    act.activation(m.xnT[:, :], m.misc[:, :], ACT.Copy).then_inc(m.emptied, 1)
                if f == "OT":
                    act.wait_ge(m.filled, n + 1)
                    act.activation(m.oT[:, :], m.misc[:, 0:2 * P], ACT.Copy).then_inc(m.emptied, 1)

            def take_keys(n, par, gp):
                act.wait_ge(m.filled, n + 1)
                for h in range(HQ):
                    last = act.activation(
                        m.kexp[:, par, gp, :, h, :],
                        m.misc[:, gp * 256:(gp + 1) * 256].rearrange("p (t k) -> p t k", t=GT),
                        ACT.Identity, bias=w.bk_heads[:, gp, h:h + 1], scale=m.head_mask[:, h:h + 1])
                if gp == 1:
                    last.then_inc(m.emptied, 1)

            def exp(s, n):
                act.wait_ge(m.shifted, n + 1)
                act.activation(m.prob[:, s % 2, :], m.score[s % 4][:, :], ACT.Exp,
                               scale=ATT_SCALE).then_inc(m.probs, 1)

            def take_turned(s, n):
                act.wait_ge(m.turned, n + 1)
                act.activation(m.pT[:, s % 2, :], m.pT_ps[:, :], ACT.Copy).then_inc(m.turned_out, 1)

            def copy_out(pair):
                act.wait_ge(m.valued, pair * 4 + 4)
                act.wait_ge(m.o_ready, pair)
                for u in range(2):
                    for b in range(2):
                        rows = slice(64 * b, 64 * b + 64)
                        last = act.activation(
                            m.o_raw[rows, u, :, :].rearrange("p (s h) e -> p s (h e)", h=2),
                            m.out_ps[u][rows, 0:288].rearrange("p (s b e) -> p s b e", b=2, e=18)[:, :, b, :],
                            ACT.Copy)
                last.then_inc(m.o_copied, 1)

            for i, f in enumerate(front_first):
                take(f, fill0 + i)
                if f == "K":
                    take_keys(fill0 + i, 0, 0)
                    take_keys(fill0 + i, 0, 1)
            exp(0, step0)

            def body(it, first, last):
                numbers = NUMBERS[first, last]
                base = fill0 + fills_before(it)
                n0 = step0 + it * STEPS
                for s in steps_of(last):
                    before, after = fills(s, first, last)
                    for f in before:
                        take(f[0], base + numbers[s, 0, f])
                    if s + 1 < STEPS or not last:
                        exp(s + 1, n0 + s + 1)
                    if s < STEPS:
                        take_turned(s, n0 + s)
                    for f in after:
                        take(f[0], base + numbers[s, 1, f])
                    keys = FRONT_STEPS[FRONT.index("K")]
                    if s % 8 in (keys, keys + 1) and s < STEPS and not (last and s >= 8):
                        half = s % 8 - keys
                        take_keys(base + numbers[s - half, 1, ("K", 0)], (s // 8 + 1) % 2, half)
                    if s % 4 == 0 and (s or not first) and s <= STEPS:
                        copy_out(pair0 + 4 * it + s // 4 - 1)

            body(0, True, False)
            with act.Fori(1, BODIES - 1) as it:
                body(it, False, False)
            body(BODIES - 1, False, True)

        @block.vector
        def _(dve):
            def normalise(g, par):
                group_normalise(dve, m, g, par, lambda t: m.xn[:, t, :], ln0 + g).then_inc(m.xn_ready, 1)

            def take(f, par, n, tile):
                if f in ("xT", "OT", "K"):
                    return
                dve.wait_ge(m.filled, n + 1)
                if f in ("Q0", "Q1"):
                    gp = int(f[1])
                    last = dve.scalar_tensor_tensor(
                        out=m.qbd[:, par, gp, :], in0=m.misc[:, :], scalar=w.bq[:, gp:gp + 1],
                        in1=m.batch_mask[:, :], op0=ALU.add, op1=ALU.mult)
                elif f in ("V0", "V1"):
                    t = 2 * int(f[1])
                    last = dve.tensor_tensor(
                        m.v2[:, par, t:t + 2, :, :, 0:DH].rearrange("p t b h e -> p (t b) h e"),
                        m.misc[:, :].rearrange("p (c h e) -> p c h e", c=4, h=HEADS),
                        m.value_mask[:, :].rearrange("p (h e) -> p h e", h=HEADS).unsqueeze(1)
                        .to_broadcast([P, 4, HEADS, DH]), ALU.mult)
                else:
                    xs = m.x[:, bass.ds(tile, 2), :]
                    last = dve.tensor_tensor(xs, xs, m.misc[:, 0:2 * D].rearrange("p (t d) -> p t d", t=2), ALU.add)
                last.then_inc(m.emptied, 1)
                if f == "Y" and biased:
                    dve.wait_ge(m.emptied, n + 1)
                    dve.tensor_tensor(xs, xs, w.out_bias[:, :].unsqueeze(1).to_broadcast([P, 2, D]),
                                      ALU.add).then_inc(m.x_whole, 1)

            def wait_whole(n, pair):
                if biased:
                    dve.wait_ge(m.x_whole, pair + 1 - 2 * GROUPS)
                else:
                    dve.wait_ge(m.emptied, n + 1)

            def statistics(tile):
                for u in range(2):
                    rows = bass.ds(tile + u, 1)
                    dve.bn_stats(flat(m.whole_stats[:, rows, :]), flat(m.x[:, rows, :]))

            def row_max(s, n):
                dve.wait_ge(m.scored, n + 1)
                dve.tensor_reduce(m.neg_max[:, s % 4, :], m.score[s % 4][:, :].rearrange("p (h k) -> p h k", k=S),
                                  AX_X, ALU.max, negate=True).then_inc(m.maxed, 1)

            def divide(pair):
                dve.wait_ge(m.o_copied, pair + 1)
                dve.reciprocal(m.o_rec[:, :, :], m.o_raw[:, :, :, DH]).then_inc(m.o_rec_ready, 1)
                dve.wait_ge(m.o_rec_ready, pair + 1)
                dve.tensor_tensor(m.o_norm[:, :, :].rearrange("p u (h e) -> p u h e", h=HEADS),
                                  m.o_raw[:, :, :, 0:DH],
                                  m.o_rec[:, :, :].unsqueeze(3).to_broadcast([P, 2, HEADS, DH]),
                                  ALU.mult).then_inc(m.o_ready, 1)

            def first_norm(g):
                if fetch:
                    if g == 0:
                        dve.wait_ge(fetch.s.y_row, SLOT_TILES)
                    add_rows(dve, m, fetch, g, (0, g))
                group_statistics(dve, m, g, g, ln0 + g)

            first_norm(0)
            normalise(0, 0)
            if not fetch:
                first_norm(1)
            for i, f in enumerate(front_first):
                take(f, 0, fill0 + i, None)
            if fetch:
                first_norm(1)
            row_max(0, step0)
            row_max(1, step0 + 1)

            def body(it, first, last):
                numbers = NUMBERS[first, last]
                base = fill0 + fills_before(it)
                n0 = step0 + it * STEPS
                for s in steps_of(last):
                    before, after = fills(s, first, last)
                    if s % 8 == 0 and s < STEPS and not (last and s >= 8):
                        normalise(2 * it + s // 8 + 1, (s // 8 + 1) % 2)
                    if s % 8 == 4 and not last:
                        g = 2 * it + s // 8 + 2
                        if later and first and s == 4:
                            dve.wait_ge(m.x_in, 32)
                        if fetch:
                            add_rows(dve, m, fetch, g, (it + 1, s // 8))
                    for f in before:
                        take(f[0], (s // 8 + 1) % 2, base + numbers[s, 0, f], 8 * it + 2 * f[1])
                    k = (s - 9) // 4
                    ready = s % 4 == 1 and ("Y", k) in fills(s - 1, first, last)[0]
                    if ready:
                        wait_whole(base + numbers[s - 1, 0, ("Y", k)], pair0 + 4 * it + k)
                    if s + 2 < STEPS or not last:
                        row_max(s + 2, n0 + s + 2)
                    if ready:
                        statistics(8 * it + 2 * k)
                    if s % 8 == 4 and not last:
                        group_statistics(dve, m, g, s // 8, ln0 + g)
                    for f in after:
                        take(f[0], (s // 8 + 1) % 2, base + numbers[s, 1, f], 8 * it + 2 * f[1])
                    if s % 4 == 0 and (s or not first) and s <= STEPS:
                        divide(pair0 + 4 * it + s // 4 - 1)

            body(0, True, False)
            if later:
                later.constants(dve)
            with dve.Fori(1, BODIES - 1) as it:
                body(it, False, False)
            body(BODIES - 1, False, True)
            wait_whole(fill0 + FILLS - 1, pair0 + 2 * GROUPS - 1)
            statistics(TILES - 2)
            if later:
                later.biases(dve)

        @block.gpsimd
        def _(pool):
            if fetch:
                for u in range(BUFFERS):
                    pool.wait_ge(fetch.s.y_done[u], fetch.stored)
                fetch_rows(pool, m, fetch, 0)
            stage_weights(pool, m, experts, 0)
            stage_weights(pool, m, experts, 1)
            group_power(pool, m, 0, ln0)
            for g in range(1, GROUPS):
                if fetch:
                    fetch_rows(pool, m, fetch, g)
                if later and g == experts.chunks + 2:
                    later.split(pool)
                chunk = g - 2
                if 0 <= chunk < experts.chunks:
                    split_weights(pool, m, experts, chunk, experts.chunk0 + chunk)
                    stage_weights(pool, m, experts, chunk + 2)
                group_power(pool, m, g % 2, ln0 + g)


EXPERTS = 8
F = 512
FB = F // P
SLOT_TILES = 72
ROUTED_ONE = 40
WSCALE = 64.0
ROUND = 1.5 * 2.0 ** 23
UNROLL = 8
BUFFERS = 4
KEPT_AT = 13200
BODIES_MOE = SLOT_TILES // UNROLL
LAG = 2
FAR = 1e30
assert SLOT_TILES * P >= 2 * TOKENS + EXPERTS * (P - 1) and ROUTED_ONE * P >= TOKENS + EXPERTS * (P - 1)
assert ROUTED_ONE + TILES == SLOT_TILES and SLOT_TILES % UNROLL == 0


class Region:

    def __init__(self, buffer, at=0):
        self.buffer, self.at = buffer, at

    def take(self, shape, dt=F32):
        n = int(np.prod(shape)) * (2 if dt in (F16, BF16) else 4) // 4
        ap = self.buffer[:, self.at:self.at + n]
        self.at += n
        if dt is not F32:
            ap = ap.bitcast(dt)
        if len(shape) > 1:
            names = " ".join("abcdef"[:len(shape)])
            ap = ap.rearrange(f"p ({names}) -> p {names}", **dict(zip("abcdef", shape)))
        return ap


def flat(ap):
    names = " ".join("abcd"[:len(ap.shape) - 1])
    return ap.rearrange(f"p {names} -> p ({names})") if len(ap.shape) > 2 else ap


def group_of(buffer, g, count=GT):
    return lambda t: flat(buffer[:, bass.ds(count * g + t, 1), :])


def norm_block(nc, m, s, router, logits, made):
    norms_before = m.ln_count
    banks = (m.out_ps[0], m.out_ps[1], m.score[0])
    with nc.Block(no_gpsimd_drain=True) as block:
        @block.vector
        def _(dve):
            def norm(g, par):
                if not isinstance(g, int):
                    dve.wait_ge(s.group_sb, g - 1)
                normalise(dve, m, g, norms_before, lambda t: m.xn2[:, par, t, :]).then_inc(s.normed, 1)

            def take_logits(g, bank):
                dve.wait_ge(s.logit_ps, g + 1)
                dve.tensor_copy(logits[:, bass.ds(GT * g, GT), :],
                                banks[bank][:, 0:GT * EXPERTS].rearrange("p (t e) -> p t e", t=GT))
            whole_statistics(dve, m, norms_before, made)
            norm(0, 0)
            norm(1, 1)
            with dve.Fori(1, GROUPS // 2) as i:
                norm(2 * i, 0)
                take_logits(2 * i - 2, 0)
                norm(2 * i + 1, 1)
                take_logits(2 * i - 1, 1)
            take_logits(GROUPS - 2, 0)
            take_logits(GROUPS - 1, 2)

        @block.gpsimd
        def _(pool):
            whole_power(pool, m, norms_before)

        @block.tensor
        def _(pe):
            turned_ps = (m.pT_ps, m.misc)

            def turn(g, par):
                pe.wait_ge(s.normed, g + 1)
                if not isinstance(g, int):
                    pe.wait_ge(s.group_sb, g - 1)
                for t in range(GT):
                    mm = pe.transpose(turned_ps[par][:, t * P:(t + 1) * P], m.xn2[:, par, t, :], m.ident[:, :])
                mm.then_inc(s.turned, 1)

            def route(g, par, bank):
                pe.wait_ge(s.group_sb, g + 1)
                for t in range(GT):
                    mm = pe.matmul(banks[bank][:, t * EXPERTS:(t + 1) * EXPERTS],
                                   m.xnT2[:, par, t * P:(t + 1) * P], router[:, :],
                                   start=True, stop=True, skip_group_check=True)
                mm.then_inc(s.logit_ps, 1)
            turn(0, 0)
            turn(1, 1)
            route(0, 0, 0)
            with pe.Fori(1, GROUPS // 2) as i:
                turn(2 * i, 0)
                route(2 * i - 1, 1, 1)
                turn(2 * i + 1, 1)
                route(2 * i, 0, 0)
            route(GROUPS - 1, 1, 2)

        @block.scalar
        def _(act):
            turned_ps = (m.pT_ps, m.misc)
            with act.Fori(0, GROUPS // 2) as i:
                for par in range(2):
                    g = 2 * i + par
                    act.wait_ge(s.turned, g + 1)
                    act.activation(m.xnT2[:, par, :], turned_ps[par][:, :], ACT.Copy)
                    act.activation(m.xall[:, bass.ds(GT * g, GT), :], m.xn2[:, par, :, :],
                                   ACT.Copy).then_inc(s.group_sb, 1)


def stage_weights(pool, m, c, chunk):
    if chunk < c.chunks:
        n, done = m.stage.shape[-1], c.chunk0 + chunk
        if done >= 2:
            pool.wait_ge(m.split_step, 3 * (done - 1))
        pool.dma_start(m.stage[:, done % 2, :], c.weights[:, chunk * n:(chunk + 1) * n])\
            .then_inc(m.staged[done % 2], 16)


def split_weights(pool, m, c, chunk, done):
    n = m.stage.shape[-1]
    cols = slice(chunk * n, (chunk + 1) * n)
    st = m.stage[:, done % 2, :]
    pool.wait_ge(m.staged[done % 2], 16 * (done // 2 + 1))
    pool.tensor_scalar(st, st, WSCALE, None, ALU.mult).then_inc(m.split_step, 1)
    pool.wait_ge(m.split_step, 3 * done + 1)
    pool.tensor_copy(m.w_hi[:, cols], st).then_inc(m.split_step, 1)
    pool.wait_ge(m.split_step, 3 * done + 2)
    pool.tensor_tensor(m.w_lo[:, cols], st, m.w_hi[:, cols], ALU.subtract).then_inc(m.split_step, 1)


def moe(nc, m, k, c):
    swiglu = k == 1
    CH = 1 if swiglu else 2
    NJ = TILES * CH
    NW = EXPERTS * F
    SHARED = TILES if swiglu else 0
    SB = SHARED // UNROLL
    r = Region(m.big)
    kept = Region(m.big, KEPT_AT)
    logits = r.take((TILES, EXPERTS))
    work = r.take((TILES, EXPERTS))
    work2 = r.take((TILES, EXPERTS))
    top = r.take((2, TILES))
    first = r.take((2, TILES))
    hot = r.take((TILES, CH, EXPERTS))
    hot_b = r.take((NJ, EXPERTS), BF16)
    cum = [r.take((NJ, EXPERTS)) for _ in range(2)]
    total = r.take((NJ, EXPERTS))
    upto = [r.take((EXPERTS,)) for _ in range(2)]
    tiles_of = r.take((EXPERTS,))
    row0 = r.take((EXPERTS,))
    slot_f = r.take((NJ,))
    slot = kept.take((NJ,), I32)
    gate = kept.take((2, TILES))
    expo = r.take((TILES, EXPERTS))
    denom = r.take((TILES,))
    tile_hit = r.take((SLOT_TILES, EXPERTS))
    tile_f = r.take((SLOT_TILES,))
    tile_w = r.take((LAG + SLOT_TILES,), I32)
    x_row = r.take((BUFFERS, D))
    x_hi, x_lo = r.take((2, P), F16), r.take((2, P), F16)
    h_f = r.take((2, F))
    h_act = r.take((2, F))
    h_hi, h_lo = r.take((BUFFERS, F), F16), r.take((2, F), F16)
    y_row = r.take((BUFFERS, D))
    fetched = kept.take((8, D))
    s = m.s_moe[k]
    norm_block(nc, m, s, c.router, logits, made=not swiglu)

    with nc.Block(no_gpsimd_drain=True) as block:
        steps = [0]

        @block.vector
        def _(dve):
            def step(ins):
                steps[0] += 1
                ins.then_inc(s.route, 1)
                dve.wait_ge(s.route, steps[0])

            def over_e(ap):
                return ap.unsqueeze(2).to_broadcast([P, TILES, EXPERTS])

            rev = m.rev_index[:, :].unsqueeze(1).to_broadcast([P, TILES, EXPERTS])
            left = logits
            for j in range(CH):
                step(dve.tensor_reduce(top[:, j, :], left, AX_X, ALU.max))
                step(dve.tensor_tensor(work, left, over_e(top[:, j, :]), ALU.is_equal))
                step(dve.tensor_tensor(work, work, rev, ALU.mult))
                step(dve.tensor_reduce(first[:, j, :], work, AX_X, ALU.max))
                step(dve.tensor_tensor(hot[:, :, j, :], rev, over_e(first[:, j, :]), ALU.is_equal))
                if j + 1 < CH:
                    step(dve.scalar_tensor_tensor(out=work2, in0=hot[:, :, j, :], scalar=-FAR, in1=left,
                                                  op0=ALU.mult, op1=ALU.add))
                    left = work2
            dve.tensor_copy(hot_b, hot.rearrange("p a b c -> p (a b) c")).then_inc(s.hot, 1)

            if swiglu:
                dve.tensor_tensor(work2, logits, over_e(top[:, 0, :]), ALU.subtract).then_inc(s.gate_in, 1)
                dve.wait_ge(s.gate_exp, 1)
                step(dve.tensor_reduce(denom, expo, AX_X, ALU.add))
                step(dve.reciprocal(gate[:, 0, :], denom))
                step(dve.tensor_scalar(gate[:, 1, :], hot[:, :, 0, EXPERTS - 1], -2.0, 2.0, ALU.mult, ALU.add))
                step(dve.tensor_tensor(gate[:, 0, :], gate[:, 0, :], gate[:, 1, :], ALU.mult))
            else:
                dve.tensor_tensor(denom, top[:, 1, :], top[:, 0, :], ALU.subtract).then_inc(s.gate_in, 1)
                dve.wait_ge(s.gate_exp, 1)
                step(dve.tensor_scalar(denom, expo[:, :, 0], 1.0, None, ALU.add))
                step(dve.reciprocal(gate[:, 0, :], denom))
                step(dve.tensor_tensor(gate[:, 1, :], gate[:, 0, :], expo[:, :, 0], ALU.mult))

            dve.wait_ge(s.prefix, 1)
            step(dve.tensor_copy(total, m.score[1][:, 0:NJ * EXPERTS].rearrange("p (j e) -> p j e", e=EXPERTS)))
            src, n, at = total, 1, 0
            while n < NJ:
                dst = cum[at]
                dve.tensor_copy(dst[:, 0:n, :], src[:, 0:n, :])
                step(dve.tensor_tensor(dst[:, n:, :], src[:, n:, :], src[:, 0:NJ - n, :], ALU.add))
                src, n, at = dst, 2 * n, 1 - at
            spare = cum[at]
            step(dve.tensor_scalar(tiles_of, src[:, NJ - 1, :], (P - 1) / 2.0, 1.0 / P, ALU.add, ALU.mult))
            step(dve.tensor_scalar(tiles_of, tiles_of, ROUND, None, ALU.add))
            step(dve.tensor_scalar(tiles_of, tiles_of, ROUND, None, ALU.subtract))
            ends, n, at = tiles_of, 1, 0
            while n < EXPERTS:
                dst = upto[at]
                dve.tensor_copy(dst[:, 0:n], ends[:, 0:n])
                step(dve.tensor_tensor(dst[:, n:], ends[:, n:], ends[:, 0:EXPERTS - n], ALU.add))
                ends, n, at = dst, 2 * n, 1 - at
            step(dve.tensor_tensor(row0, ends, tiles_of, ALU.subtract))
            step(dve.tensor_scalar(row0, row0, float(P), None, ALU.mult))
            step(dve.tensor_tensor(spare, src, total, ALU.subtract))
            step(dve.tensor_tensor(spare, spare, m.score[0][:, 0:NJ * EXPERTS]
                                   .rearrange("p (j e) -> p j e", e=EXPERTS), ALU.add))
            step(dve.tensor_tensor(spare, spare, row0.unsqueeze(1).to_broadcast([P, NJ, EXPERTS]), ALU.add))
            step(dve.tensor_tensor(spare, spare, hot.rearrange("p a b c -> p (a b) c"), ALU.mult))
            step(dve.tensor_reduce(slot_f, spare, AX_X, ALU.add))
            step(dve.tensor_copy(slot, slot_f))
            step(dve.tensor_tensor(tile_hit, m.tile_index[:, :].unsqueeze(2).to_broadcast([P, SLOT_TILES, EXPERTS]),
                                   ends.unsqueeze(1).to_broadcast([P, SLOT_TILES, EXPERTS]), ALU.is_ge))
            step(dve.tensor_reduce(tile_f, tile_hit, AX_X, ALU.add))
            step(dve.tensor_scalar(tile_f, tile_f, float(EXPERTS - 1), None, ALU.min))
            step(dve.tensor_scalar(tile_f, tile_f, float(F), None, ALU.mult))
            dve.memset(tile_w[:, 0:LAG], 0)
            step(dve.tensor_copy(tile_w[:, LAG:], tile_f))

        @block.scalar
        def _(act):
            act.wait_ge(s.gate_in, 1)
            if swiglu:
                act.activation(expo, work2, ACT.Exp).then_inc(s.gate_exp, 1)
            else:
                act.activation(expo[:, :, 0], denom, ACT.Exp).then_inc(s.gate_exp, 1)

        @block.tensor
        def _(pe):
            pe.wait_ge(s.hot, 1)
            pe.matmul(m.score[0][:, 0:NJ * EXPERTS], m.above[:, :], flat(hot_b), start=True, stop=True)
            pe.matmul(m.score[1][:, 0:NJ * EXPERTS], m.ones_b[:, :], flat(hot_b), start=True,
                      stop=True).then_inc(s.prefix, 1)

    h_ps = ((m.score[0], m.score[1]), (m.score[2], m.score[3]))
    x_ps = (m.pT_ps, m.misc)

    def in_shared(j):
        return j < SB if isinstance(j, int) else loop_shared[0]

    loop_shared = [False]

    def run_bodies(engine, body):
        body(0, True, False)
        if swiglu:
            loop_shared[0] = True
            with engine.Fori(1, SB) as j:
                body(j, False, False)
            loop_shared[0] = False
            body(SB, False, False)
        with engine.Fori(SB + 1, BODIES_MOE - 1) as j:
            body(j, False, False)
        body(BODIES_MOE - 1, False, True)

    with nc.Block(no_gpsimd_drain=True) as block:
        @block.gpsimd
        def _(pool):
            pool.wait_ge(m.zeroed, 16)
            for t in range(TILES):
                for j in range(CH):
                    pool.indirect_dma_start(
                        out=m.sorted_in, out_offset=bass.IndirectOffsetOnAxis(
                            ap=slot[:, t * CH + j:t * CH + j + 1], axis=0),
                        in_=m.xall[:, t, :], in_offset=None).then_inc(s.scattered, 16)
            with pool.Fori(SHARED // BUFFERS, SLOT_TILES // BUFFERS) as j:
                for u in range(BUFFERS):
                    i = BUFFERS * j + u
                    pool.wait_ge(s.y_row, i + 1)
                    pool.dma_start(m.sorted_out[bass.ds(i * P - SHARED * P, P), :],
                                   y_row[:, u, :]).then_inc(s.y_done[u], 16)

        @block.sync
        def _(sp):
            def load(i, u, shared):
                rows = flat(m.xall[:, bass.ds(i, 1), :]) if shared else m.sorted_in[bass.ds(i * P - SHARED * P, P), :]
                sp.dma_start(x_row[:, u, :], rows).then_inc(s.x_row[u], 16)

            def body(j, shared):
                for u in range(BUFFERS):
                    i = BUFFERS * j + u
                    sp.wait_ge(s.x_turned, i + 1)
                    load(i + BUFFERS, u, shared)
            if swiglu:
                for u in range(BUFFERS):
                    load(u, u, True)
                with sp.Fori(0, SHARED // BUFFERS - 1) as j:
                    body(j, True)
            sp.wait_ge(s.scattered, 16 * NJ)
            if swiglu:
                body(SHARED // BUFFERS - 1, False)
            else:
                for u in range(BUFFERS):
                    load(u, u, False)
            with sp.Fori(SHARED // BUFFERS, SLOT_TILES // BUFFERS - 1) as j:
                body(j, False)

        @block.tensor
        def _(pe):
            def experts(j):
                n, first = LAG + UNROLL, UNROLL * j - SHARED
                fixed = isinstance(j, int)
                regs = [pe.alloc_register(f"moe{k}_expert{u}_{j if fixed else 'loop'}") for u in range(n)]
                pe.load(regs, tile_w[0:1, first:first + n] if fixed else tile_w[0:1, bass.ds(first, n)])
                return [pe.snap(reg, donate=True, min_val=0, max_val=(EXPERTS - 1) * F) for reg in regs]

            def turn(i, u, par, j):
                pe.wait_ge(s.x_row[u], 16 * (j + 1))
                pe.transpose(x_ps[par][:, 0:P], x_row[:, u, :], m.ident[:, :]).then_inc(s.x_turned, 1)

            def hidden(i, par, e):
                pe.wait_ge(s.x_split, i + 1)
                for which in range(2 if swiglu else 1):
                    for fb in range(FB):
                        at = e + (which * NW + fb * P)
                        o = h_ps[par][which][:, fb * P:(fb + 1) * P]
                        hi, lo = m.w_hi[:, bass.ds(at, P)], m.w_lo[:, bass.ds(at, P)]
                        pe.matmul(o, hi, x_hi[:, par, :], start=(fb == 0), stop=False, skip_group_check=True)
                        pe.matmul(o, hi, x_lo[:, par, :], start=False, stop=False, skip_group_check=True)
                        mm = pe.matmul(o, lo, x_hi[:, par, :], start=False, stop=True, skip_group_check=True)
                        if not swiglu:
                            mm = pe.matmul(o, m.b1_rows[:, bass.ds(e + fb * P, P)], m.ones3[:, :],
                                           start=False, stop=True, skip_group_check=True)
                mm.then_inc(s.h_ps, 1)

            def down(i, u, par, e):
                pe.wait_ge(s.h_split, i + 1)
                o = m.out_ps[par][:, 0:D]
                for fb in range(FB):
                    at = e + ((1 + swiglu) * NW + fb * D)
                    f = slice(fb * P, (fb + 1) * P)
                    hi, lo = m.w_hi[:, bass.ds(at, D)], m.w_lo[:, bass.ds(at, D)]
                    pe.matmul(o, h_hi[:, u, f], hi, start=(fb == 0), stop=False, skip_group_check=True)
                    pe.matmul(o, h_lo[:, par, f], hi, start=False, stop=False, skip_group_check=True)
                    mm = pe.matmul(o, h_hi[:, u, f], lo, start=False, stop=True, skip_group_check=True)
                if not swiglu:
                    mm = pe.matmul(o, m.ones3[:, :], m.b2_rows[:, bass.ds(e // (F // D), D)], start=False, stop=True,
                                   skip_group_check=True)
                mm.then_inc(s.y_ps, 1)

            turn(0, 0, 0, 0)

            def body(j, start, end):
                if in_shared(j):
                    e = [(EXPERTS - 1) * F] * (LAG + UNROLL)
                else:
                    e = experts(j)
                    if swiglu and isinstance(j, int) and j == SB:
                        e[0:LAG] = [(EXPERTS - 1) * F] * LAG
                for u in range(UNROLL):
                    i = UNROLL * j + u
                    if not (end and u == UNROLL - 1):
                        turn(i + 1, (u + 1) % BUFFERS, (u + 1) % 2, UNROLL // BUFFERS * j + (u + 1) // BUFFERS)
                    hidden(i, u % 2, e[LAG + u])
                    if not (start and u < LAG):
                        down(i - LAG, (u - LAG) % BUFFERS, u % 2, e[u])
                if end:
                    down(i - 1, BUFFERS - 2, 0, e[UNROLL])
                    down(i, BUFFERS - 1, 1, e[UNROLL + 1])
            run_bodies(pe, body)

        @block.scalar
        def _(act):
            def take_x(i, par):
                act.wait_ge(s.x_turned, i + 1)
                act.activation(x_hi[:, par, :], x_ps[par][:, 0:P], ACT.Copy).then_inc(s.x_hi, 1)

            def activate(i, u, par):
                act.wait_ge(s.h_ps, i + 1)
                if not isinstance(i, int) or i > 1:
                    act.wait_ge(s.h_split, i - 1)
                if swiglu:
                    act.activation(h_act[:, par, :], h_ps[par][1][:, :], ACT.Silu,
                                   scale=1.0 / WSCALE).then_inc(s.h_act, 1)
                else:
                    act.activation(h_hi[:, u, :], h_ps[par][0][:, :], ACT.Gelu, scale=1.0 / WSCALE)
                    act.activation(h_f[:, par, :], h_ps[par][0][:, :], ACT.Gelu,
                                   scale=1.0 / WSCALE).then_inc(s.h_act, 1)
            take_x(0, 0)

            def body(j, start, end):
                for u in range(UNROLL):
                    i = UNROLL * j + u
                    if not (end and u == UNROLL - 1):
                        take_x(i + 1, (u + 1) % 2)
                    activate(i, u % BUFFERS, u % 2)
            run_bodies(act, body)

        @block.vector
        def _(dve):
            def split_x(i, par):
                dve.wait_ge(s.x_hi, i + 1)
                dve.tensor_tensor(x_lo[:, par, :], x_ps[par][:, 0:P], x_hi[:, par, :],
                                  ALU.subtract).then_inc(s.x_split, 1)

            def split_h(i, u, par):
                dve.wait_ge(s.h_act, i + 1)
                if swiglu:
                    dve.scalar_tensor_tensor(out=h_f[:, par, :], in0=h_ps[par][0][:, :], scalar=1.0 / WSCALE,
                                             in1=h_act[:, par, :], op0=ALU.mult, op1=ALU.mult).then_inc(s.h_f, 1)
                    dve.wait_ge(s.h_f, i + 1)
                    dve.tensor_copy(h_hi[:, u, :], h_f[:, par, :]).then_inc(s.h_hi, 1)
                    dve.wait_ge(s.h_hi, i + 1)
                dve.tensor_tensor(h_lo[:, par, :], h_f[:, par, :], h_hi[:, u, :],
                                  ALU.subtract).then_inc(s.h_split, 1)

            def take_y(i, u, par, j, uses):
                dve.wait_ge(s.y_ps, i + 1)
                if in_shared(j):
                    x = flat(m.x[:, bass.ds(i, 1), :])
                    dve.scalar_tensor_tensor(out=x, in0=m.out_ps[par][:, 0:D], scalar=1.0 / WSCALE, in1=x,
                                             op0=ALU.mult, op1=ALU.add).then_inc(s.y_row, 1)
                    return
                if not isinstance(uses, int) or uses > SHARED // BUFFERS:
                    dve.wait_ge(s.y_done[u], 16 * uses - 16 * (SHARED // BUFFERS))
                dve.tensor_scalar(y_row[:, u, :], m.out_ps[par][:, 0:D], 1.0 / WSCALE, None,
                                  ALU.mult).then_inc(s.y_row, 1)
            split_x(0, 0)

            def body(j, start, end):
                before = SB - 1 if isinstance(j, int) and j == SB else j - 1
                for u in range(UNROLL):
                    i = UNROLL * j + u
                    if not (end and u == UNROLL - 1):
                        split_x(i + 1, (u + 1) % 2)
                    if not (start and u < LAG):
                        take_y(i - LAG, (u - LAG) % BUFFERS, u % 2, before if u < LAG else j,
                               UNROLL // BUFFERS * j + (u - LAG) // BUFFERS)
                    split_h(i, u % BUFFERS, u % 2)
                if end:
                    take_y(i - 1, BUFFERS - 2, 0, j, SLOT_TILES // BUFFERS - 1)
                    take_y(i, BUFFERS - 1, 1, j, SLOT_TILES // BUFFERS - 1)
            run_bodies(dve, body)

    f = Names()
    f.s, f.slot, f.gate, f.fetched, f.choices = s, slot, gate, fetched, CH
    f.stored = 16 * (SLOT_TILES - SHARED) // BUFFERS
    return f


def fetch_rows(pool, m, f, g):
    for j in range(f.choices):
        for t in range(GT):
            n = GT * (f.choices * g + j) + t
            if n >= 8:
                pool.wait_ge(f.s.added, n - 7)
            at = (GT * g + t) * f.choices + j
            pool.indirect_dma_start(
                out=f.fetched[:, n % 8, :], out_offset=None, in_=m.sorted_out,
                in_offset=bass.IndirectOffsetOnAxis(ap=f.slot[:, at:at + 1], axis=0)).then_inc(f.s.fetched[n % 8], 16)


def add_rows(dve, m, f, g, halves):
    half, odd = halves
    for j in range(f.choices):
        for t in range(GT):
            c = GT * j + t
            buffer, times = (c, g + 1) if f.choices == 2 else (GT * odd + c, half + 1)
            dve.wait_ge(f.s.fetched[buffer], 16 * times)
            if j:
                dve.wait_ge(f.s.added, 2 * GT * g + (t + 1))
            x = flat(m.x[:, bass.ds(GT * g + t, 1), :])
            dve.scalar_tensor_tensor(out=x, in0=f.fetched[:, buffer, :], scalar=f.gate[:, j, bass.ds(GT * g + t, 1)],
                                     in1=x, op0=ALU.mult, op1=ALU.add).then_inc(f.s.added, 1)
    dve.wait_ge(f.s.added, GT * f.choices * g + GT * f.choices)


def load_bias_rows(sp, m, s, bias_f, bias_b, b1, b2):
    n1, n2 = b1.shape[1], b2.shape[1]
    sp.dma_start(bias_f[:, 0, 0:n1], b1).then_inc(s.bias_in, 16)
    sp.dma_start(bias_f[:, 1, 0:n2], b2).then_inc(s.bias_in, 16)
    sp.wait_ge(s.bias_step, BIAS_STEPS)
    sp.wait_ge(s.rows_clear, 1)
    for i in range(3):
        sp.dma_start(m.b1_rows[i:i + 1, 0:n1 * P], bias_b[:, i, 0, 0:n1]).then_inc(s.bias_rows, 16)
        sp.dma_start(m.b2_rows[i:i + 1, 0:n2 * P], bias_b[:, i, 1, 0:n2]).then_inc(s.bias_rows, 16)
    sp.wait_ge(s.bias_rows, 16 * 6)


def clear_bias_rows(dve, m, s, bias_f):
    dve.memset(bias_f[:, 1, EXPERTS:], 0.0).then_inc(s.bias_step, 1)
    dve.memset(m.b1_rows[:, :], 0.0)
    dve.memset(m.b2_rows[:, :], 0.0).then_inc(s.rows_clear, 1)


BIAS_STEPS = 7


def split_bias_rows(pool, m, s, bias_f, bias_b):
    pool.wait_ge(s.bias_step, 1)
    pool.wait_ge(s.bias_in, 32)
    pool.tensor_scalar(bias_f, bias_f, WSCALE, None, ALU.mult).then_inc(s.bias_step, 1)
    n = 2
    for i in range(3):
        pool.wait_ge(s.bias_step, n)
        pool.tensor_copy(bias_b[:, i, :, :], bias_f).then_inc(s.bias_step, 1)
        n += 1
        if i < 2:
            pool.wait_ge(s.bias_step, n)
            pool.tensor_tensor(bias_f, bias_f, bias_b[:, i, :, :], ALU.subtract).then_inc(s.bias_step, 1)
            n += 1
    assert n == BIAS_STEPS




QMIN, QMAX = -128.0, 127.0
DIAG_BLOCKS = 1024 // P
H_COLS = FB * TOKENS


def quantized_ffn(nc, m):
    s = m.s_quant
    q = Region(m.quant)
    wf = q.take((2, F))
    wq = q.take((2, F), BF16)
    b1 = q.take((FB,))
    b2 = q.take((D,))
    ext = q.take((4,))
    ext_all = q.take((4,))
    h_ext = q.take((2, FB * GROUPS))
    h_most = q.take((2,))
    h_all = q.take((2,))
    par_x, par_h = q.take((9,)), q.take((9,))
    w_scale, w_inverse = q.take((2,)), q.take((2,))
    out_scale = q.take((2,))
    xq = m.b1_rows[:, :].rearrange("p (t d) -> p t d", t=TILES)
    xqT = q.take((2, GTOK), BF16)
    late = Region(m.kexp_buffer)
    hq = late.take((2, FB, GTOK), BF16)
    h = m.big[:, 0:H_COLS].rearrange("p (b n) -> p b n", b=FB)
    one = m.s_diag
    wv, wout = late.take((DIAG_BLOCKS, D)), late.take((DIAG_BLOCKS, D))
    ctx = m.xn2[:, :, :, :].rearrange("p a t d -> p a (t d)")
    wvo, bout = m.xnT2[:, 0, 0:D], m.xnT2[:, 0, D:2 * D]

    PARTS = 4

    def part_of(x, part):
        return x[:, part * TILES // PARTS:(part + 1) * TILES // PARTS, :]

    def parameters(step, dve, ext, par):
        one = lambda i: par[:, i:i + 1]
        step(dve.tensor_tensor(one(0), ext[:, 0:1], ext[:, 1:2], ALU.add))
        step(dve.tensor_scalar(one(0), one(0), 1.0 / 255.0, 1e-8, ALU.mult, ALU.max))
        step(dve.reciprocal(one(4), one(0)))
        step(dve.tensor_tensor(one(1), ext[:, 1:2], one(4), ALU.mult))
        step(dve.tensor_scalar(one(1), one(1), ROUND, None, ALU.add))
        step(dve.tensor_scalar(one(1), one(1), ROUND, QMIN, ALU.subtract, ALU.add))
        step(dve.tensor_scalar(one(1), one(1), QMIN, QMAX, ALU.max, ALU.min))
        dve.memset(one(5), ROUND)
        dve.memset(one(8), -ROUND)
        dve.tensor_scalar(one(2), one(1), -1.0, QMIN, ALU.mult, ALU.add)
        step(dve.tensor_scalar(one(3), one(1), -1.0, QMAX, ALU.mult, ALU.add))
        dve.tensor_scalar(par[:, 6:8], par[:, 2:4], ROUND, None, ALU.add).then_inc(s.par, 1)

    norms_before = m.ln_count
    with nc.Block(no_gpsimd_drain=True) as block:
        steps = [0]

        @block.sync
        def _(sp):
            sp.dma_start(wf[:, 0, :], m.d["quant_w1"]).then_inc(s.weights, 16)
            sp.dma_start(wf[:, 1, :], m.d["quant_w2"]).then_inc(s.weights, 16)
            sp.dma_start(b1, m.d["quant_b1"]).then_inc(s.weights, 16)
            sp.dma_start(b2, m.d["quant_b2"].partition_broadcast(P)).then_inc(s.weights, 16)

        @block.vector
        def _(dve):
            def step(ins):
                steps[0] += 1
                ins.then_inc(s.step, 1)
                dve.wait_ge(s.step, steps[0])
            whole_statistics(dve, m, norms_before, made=True)
            with dve.Fori(0, GROUPS) as g:
                normalise(dve, m, g, norms_before, group_of(m.xall, g)).then_inc(s.normed, 1)
            dve.wait_ge(s.normed, GROUPS)
            dve.wait_ge(s.weights, 64)
            dve.tensor_reduce(ext[:, 0:1], flat(m.xall), AX_X, ALU.max)
            dve.tensor_reduce(ext[:, 1:2], flat(m.xall), AX_X, ALU.min)
            dve.tensor_reduce(ext[:, 2:4], wf, AX_X, ALU.max, apply_absolute_value=True).then_inc(s.step, 1)
            steps[0] += 1
            dve.wait_ge(s.step, steps[0])
            dve.tensor_scalar(ext[:, 1:2], ext[:, 1:2], -1.0, None, ALU.mult).then_inc(s.ext, 1)
            dve.wait_ge(s.ext_all, 1)
            parameters(step, dve, ext_all, par_x)
            step(dve.tensor_scalar(w_scale, ext_all[:, 2:4], 1.0 / QMAX, 1e-8, ALU.mult, ALU.max))
            step(dve.reciprocal(w_inverse, w_scale))
            dve.tensor_tensor(out_scale[:, 0:1], par_x[:, 0:1], w_scale[:, 0:1], ALU.mult)
            for i in range(2):
                step(dve.tensor_scalar(wf[:, i, :], wf[:, i, :], w_inverse[:, i:i + 1], ROUND, ALU.mult, ALU.add))
            step(dve.tensor_scalar(wf, wf, ROUND, -QMAX, ALU.subtract, ALU.max))
            step(dve.tensor_scalar(wq, wf, QMAX, None, ALU.min))
            for part in range(PARTS):
                x = part_of(m.xall, part)
                dve.wait_ge(s.rounded, part + 1)
                dve.tensor_scalar(x, x, par_x[:, 6:7], par_x[:, 7:8], ALU.max, ALU.min).then_inc(s.clipped, 1)

        @block.scalar
        def _(act):
            act.wait_ge(s.par, 1)
            for part in range(PARTS + 1):
                if part < PARTS:
                    x = part_of(m.xall, part)
                    act.activation(x, x, ACT.Identity, bias=par_x[:, 5:6], scale=par_x[:, 4:5]).then_inc(s.rounded, 1)
                if part:
                    act.wait_ge(s.clipped, part)
                    act.activation(part_of(xq, part - 1), part_of(m.xall, part - 1), ACT.Identity,
                                   bias=par_x[:, 8:9])

        @block.gpsimd
        def _(pool):
            whole_power(pool, m, norms_before)
            pool.wait_ge(s.ext, 1)
            pool.partition_all_reduce(ext_all, ext, P, bass.bass_isa.ReduceOp.max).then_inc(s.ext_all, 1)

    with nc.Block(no_gpsimd_drain=True) as block:
        @block.sync
        def _(sp):
            sp.dma_start(wv, m.d["diag_wvT"].rearrange("p (a b) -> p a b", a=DIAG_BLOCKS)).then_inc(one.weights, 16)
            sp.dma_start(wout, m.d["diag_wout"].rearrange("p (a b) -> p a b", a=DIAG_BLOCKS)).then_inc(one.weights, 16)
            sp.dma_start(bout, m.d["diag_bout"].partition_broadcast(P)).then_inc(one.weights, 16)

        @block.tensor
        def _(pe):
            def turn(g, par):
                for t in range(GT):
                    mm = pe.matmul((m.pT_ps, m.misc)[par][:, t * P:(t + 1) * P],
                                   flat(xq[:, bass.ds(GT * g + t, 1), :]), m.ident_b[:, :],
                                   start=True, stop=True, skip_group_check=True)
                mm.then_inc(s.turned, 1)

            def product(g, par):
                pe.wait_ge(s.xqT, g + 1)
                for fb in range(FB):
                    if not isinstance(g, int) or g:
                        pe.wait_ge(s.gelu, FB * g + (fb + 1 - FB))
                    pe.matmul(m.score[fb][:, :], wq[:, 0, fb * P:(fb + 1) * P], xqT[:, par, :],
                              start=True, stop=True).then_inc(s.h_ps, 1)
            turn(0, 0)
            turn(1, 1)
            product(0, 0)
            with pe.Fori(1, GROUPS // 2) as i:
                turn(2 * i, 0)
                product(2 * i - 1, 1)
                turn(2 * i + 1, 1)
                product(2 * i, 0)
            product(GROUPS - 1, 1)
            pe.wait_ge(one.weights, 48)
            for j in range(DIAG_BLOCKS):
                mm = pe.matmul(m.out_ps[0][:, 0:D], wv[:, j, :], wout[:, j, :], start=(j == 0),
                               stop=(j == DIAG_BLOCKS - 1))
            mm.then_inc(one.wvo_ps, 1)

        @block.scalar
        def _(act):
            def take(g, par):
                act.wait_ge(s.turned, g + 1)
                act.activation(xqT[:, par, :], (m.pT_ps, m.misc)[par][:, :], ACT.Copy).then_inc(s.xqT, 1)

            def gelu(g):
                for fb in range(FB):
                    act.wait_ge(s.h_ps, FB * g + fb + 1)
                    act.activation(h[:, fb, bass.ds(GTOK * g, GTOK)], m.score[fb][:, :], ACT.Gelu,
                                   bias=b1[:, fb:fb + 1], scale=out_scale[:, 0:1]).then_inc(s.gelu, 1)
            take(0, 0)
            take(1, 1)
            gelu(0)
            with act.Fori(1, GROUPS // 2) as i:
                take(2 * i, 0)
                gelu(2 * i - 1)
                take(2 * i + 1, 1)
                gelu(2 * i)
            gelu(GROUPS - 1)

        @block.vector
        def _(dve):
            with dve.Fori(0, GROUPS) as g:
                dve.wait_ge(s.gelu, FB * g + FB)
                part = h[:, :, bass.ds(GTOK * g, GTOK)]
                dve.tensor_reduce(h_ext[:, 0, bass.ds(FB * g, FB)], part, AX_X, ALU.max)
                dve.tensor_reduce(h_ext[:, 1, bass.ds(FB * g, FB)], part, AX_X, ALU.min)
            dve.wait_ge(one.wvo_ps, 1)
            dve.tensor_copy(wvo, m.out_ps[0][:, 0:D])
            dve.tensor_tensor(bout, bout, b2, ALU.add)

    with nc.Block(no_gpsimd_drain=True) as block:
        steps = [0]

        @block.vector
        def _(dve):
            def step(ins):
                steps[0] += 1
                ins.then_inc(s.step2, 1)
                dve.wait_ge(s.step2, steps[0])
            dve.tensor_reduce(h_most[:, 0:1], h_ext[:, 0, :], AX_X, ALU.max)
            step(dve.tensor_reduce(h_most[:, 1:2], h_ext[:, 1, :], AX_X, ALU.min))
            dve.tensor_scalar(h_most[:, 1:2], h_most[:, 1:2], -1.0, None, ALU.mult).then_inc(s.ext, 1)
            dve.wait_ge(s.ext_all, 2)
            parameters(step, dve, h_all, par_h)
            step(dve.tensor_tensor(out_scale[:, 1:2], par_h[:, 0:1], w_scale[:, 1:2], ALU.mult))

            def clip(g):
                part = h[:, :, bass.ds(GTOK * g, GTOK)]
                dve.wait_ge(s.rounded, PARTS + g + 1)
                dve.tensor_scalar(part, part, par_h[:, 6:7], par_h[:, 7:8], ALU.max, ALU.min).then_inc(s.clipped, 1)

            def add(g, par):
                x = m.x[:, bass.ds(GT * g, GT), :]
                dve.wait_ge(s.y_ps, g + 1)
                dve.scalar_tensor_tensor(out=flat(x), in0=m.out_ps[par][:, :], scalar=out_scale[:, 1:2],
                                         in1=flat(x), op0=ALU.mult, op1=ALU.add).then_inc(one.added, 1)
                dve.wait_ge(one.added, g + 1)
                dve.tensor_tensor(flat(x), flat(x), m.score[par][:, :], ALU.add).then_inc(s.added, 1)
                dve.wait_ge(s.added, g + 1)
                dve.tensor_tensor(x, x, bout.unsqueeze(1).to_broadcast([P, GT, D]), ALU.add)
            clip(0)
            clip(1)
            with dve.Fori(1, GROUPS // 2) as i:
                clip(2 * i)
                add(2 * i - 2, 0)
                clip(2 * i + 1)
                add(2 * i - 1, 1)
            add(GROUPS - 2, 0)
            add(GROUPS - 1, 1)

        @block.scalar
        def _(act):
            def divide(g):
                part = h[:, :, g * GTOK:(g + 1) * GTOK]
                act.activation(part, part, ACT.Identity, bias=par_h[:, 5:6], scale=par_h[:, 4:5]).then_inc(s.rounded, 1)

            def to_integers(g, par):
                act.wait_ge(s.clipped, PARTS + g + 1)
                if g > 1:
                    act.wait_ge(s.y_ps, g - 1)
                act.activation(hq[:, par, :, :], h[:, :, g * GTOK:(g + 1) * GTOK], ACT.Identity,
                               bias=par_h[:, 8:9]).then_inc(s.hq, 1)
            act.wait_ge(s.par, 2)
            divide(0)
            divide(1)
            for g in range(GROUPS):
                to_integers(g, g % 2)
                if g + 2 < GROUPS:
                    divide(g + 2)

        @block.gpsimd
        def _(pool):
            pool.wait_ge(s.ext, 2)
            pool.partition_all_reduce(h_all, h_most, P, bass.bass_isa.ReduceOp.max).then_inc(s.ext_all, 1)

        @block.tensor
        def _(pe):
            def product(g, par, times):
                pe.wait_ge(s.hq, g + 1)
                pe.wait_ge(one.ctx[par], times)
                if not isinstance(g, int):
                    pe.wait_ge(s.added, g - 1)
                for t in range(GT):
                    pe.matmul(m.score[par][:, t * D:(t + 1) * D], ctx[:, par, t * P:(t + 1) * P], wvo,
                              start=True, stop=True, skip_group_check=True)
                for t in range(GT):
                    for fb in range(FB):
                        mm = pe.matmul(m.out_ps[par][:, t * D:(t + 1) * D], hq[:, par, fb, t * P:(t + 1) * P],
                                       wq[:, 1, fb * D:(fb + 1) * D], start=(fb == 0), stop=(fb == FB - 1),
                                       skip_group_check=True)
                mm.then_inc(s.y_ps, 1)
            product(0, 0, 16)
            product(1, 1, 16)
            with pe.Fori(1, GROUPS // 2) as i:
                product(2 * i, 0, 16 * (i + 1))
                product(2 * i + 1, 1, 16 * (i + 1))

        @block.sync
        def _(sp):
            def load(g, par):
                sp.dma_start(ctx[:, par, :], m.ctxT_dram[:, bass.ds(g * GTOK, GTOK)]).then_inc(one.ctx[par], 16)
            load(0, 0)
            load(1, 1)
            with sp.Fori(1, GROUPS // 2) as i:
                for par in range(2):
                    sp.wait_ge(s.y_ps, 2 * i + par - 1)
                    load(2 * i + par, par)


F3 = 2 * D
FB3 = F3 // P


STORES = 8


def chosen_ffn(nc, m, out):
    s = m.s_chosen
    r = Region(m.big)
    xT_hi, xT_lo = r.take((TOKENS,), F16), r.take((TOKENS,), F16)
    last_T = r.take((B,))
    wp1, wp2 = r.take((D,)), r.take((EXPERTS,))
    bp1, bp2 = r.take((1,)), r.take((EXPERTS,))
    wo, bo = r.take((D,)), r.take((D,))
    nav = r.take((B,))
    logits = r.take((EXPERTS,))
    best = r.take((1,))
    hit = r.take((EXPERTS,))
    first = r.take((1,))
    sel_f = r.take((1,))
    sel = r.take((2 + B,), I32)
    h_f = r.take((2, F3))
    h_hi, h_lo = r.take((2, F3), F16), r.take((2, F3), F16)
    reasoned = r.take((2, P))
    bias_f = r.take((2, F3 * EXPERTS // P))
    bias_b = r.take((3, 2, F3 * EXPERTS // P), BF16)

    norms_before = m.ln_count
    with nc.Block(no_gpsimd_drain=True) as block:
        @block.sync
        def _(sp):
            for dst, name in ((wp1, "chosen_wp1"), (wp2, "chosen_wp2"), (bp1, "chosen_bp1"), (wo, "chosen_wo")):
                sp.dma_start(dst, m.d[name]).then_inc(s.weights, 16)
            sp.dma_start(bp2, m.d["chosen_bp2"].partition_broadcast(P)).then_inc(s.weights, 16)
            sp.dma_start(bo, m.d["chosen_bo"].partition_broadcast(P)).then_inc(s.weights, 16)
            load_bias_rows(sp, m, s, bias_f, bias_b, m.d["chosen_b1"], m.d["chosen_b2"])

        @block.vector
        def _(dve):
            clear_bias_rows(dve, m, s, bias_f)

            def norm(g, par):
                if not isinstance(g, int):
                    dve.wait_ge(s.xT_lo, g - 1)
                    dve.wait_ge(s.xn_added, g - 1)
                normalise(dve, m, g, norms_before, lambda t: m.xn2[:, par, t, :]).then_inc(s.normed, 1)

            def low(g, par):
                dve.wait_ge(s.xT_hi, g + 1)
                cols = bass.ds(GTOK * g, GTOK)
                dve.tensor_tensor(xT_lo[:, cols], (m.pT_ps, m.misc)[par][:, :], xT_hi[:, cols],
                                  ALU.subtract).then_inc(s.xT_lo, 1)
            whole_statistics(dve, m, norms_before, made=True)
            norm(0, 0)
            norm(1, 1)
            with dve.Fori(1, GROUPS // 2) as i:
                low(2 * i - 2, 0)
                norm(2 * i, 0)
                low(2 * i - 1, 1)
                norm(2 * i + 1, 1)
            low(GROUPS - 2, 0)
            low(GROUPS - 1, 1)

        @block.gpsimd
        def _(pool):
            def add_to_x(g):
                x = m.x[:, g * GT:(g + 1) * GT, :]
                pool.wait_ge(s.normed, g + 1)
                pool.tensor_tensor(x, x, m.xn2[:, g % 2, :, :], ALU.add).then_inc(s.xn_added, 1)
                pool.wait_ge(s.xn_added, g + 1)
                pool.tensor_tensor(x, x, bo.unsqueeze(1).to_broadcast([P, GT, D]), ALU.add).then_inc(s.based, 1)
            split_bias_rows(pool, m, s, bias_f, bias_b)
            pool.wait_ge(s.weights, 16 * 6)
            pool.tensor_scalar(bo, bo, 0.3, None, ALU.mult).then_inc(s.based, 1)
            pool.wait_ge(s.based, 1)
            whole_power(pool, m, norms_before, use=add_to_x)

        @block.tensor
        def _(pe):
            with pe.Fori(0, GROUPS // 2) as i:
                for par in range(2):
                    g = 2 * i + par
                    pe.wait_ge(s.normed, g + 1)
                    for t in range(GT):
                        mm = pe.transpose((m.pT_ps, m.misc)[par][:, t * P:(t + 1) * P], m.xn2[:, par, t, :],
                                          m.ident[:, :])
                    mm.then_inc(s.turned, 1)

        @block.scalar
        def _(act):
            with act.Fori(0, GROUPS // 2) as i:
                for par in range(2):
                    g = 2 * i + par
                    turned = (m.pT_ps, m.misc)[par]
                    act.wait_ge(s.turned, g + 1)
                    act.activation(last_T[:, bass.ds(2 * GT * g, 2 * GT)], turned[:, S - 1::S], ACT.Copy)
                    act.activation(xT_hi[:, bass.ds(GTOK * g, GTOK)], turned[:, :], ACT.Copy).then_inc(s.xT_hi, 1)

    with nc.Block(no_gpsimd_drain=True) as block:
        @block.tensor
        def _(pe):
            pe.wait_ge(s.weights, 16 * 6)
            pe.matmul(m.misc[:, 0:B], wp1, last_T, start=True, stop=True).then_inc(s.nav_ps, 1)
            pe.wait_ge(s.nav, 1)
            pe.matmul(m.pT_ps[0:B, 0:EXPERTS], nav, wp2, start=True, stop=True).then_inc(s.nav_ps, 1)
            pe.wait_ge(s.pick, 5)
            pe.matmul(m.misc[0:1, 0:B], sel_f[0:B, :], m.ident[0:B, 0:B], start=True, stop=True).then_inc(s.nav_ps, 1)

        @block.scalar
        def _(act):
            act.wait_ge(s.nav_ps, 1)
            act.activation(nav, m.misc[:, 0:B], ACT.Gelu, bias=bp1).then_inc(s.nav, 1)

        @block.vector
        def _(dve):
            rows = slice(0, B)
            dve.wait_ge(s.nav_ps, 2)
            dve.tensor_tensor(logits[rows, :], m.pT_ps[rows, 0:EXPERTS], bp2[rows, :], ALU.add).then_inc(s.pick, 1)
            dve.wait_ge(s.pick, 1)
            dve.tensor_reduce(best[rows, :], logits[rows, :], AX_X, ALU.max).then_inc(s.pick, 1)
            dve.wait_ge(s.pick, 2)
            dve.scalar_tensor_tensor(out=hit[rows, :], in0=logits[rows, :], scalar=best[rows, 0:1],
                                     in1=m.rev_index[rows, :], op0=ALU.is_equal, op1=ALU.mult).then_inc(s.pick, 1)
            dve.wait_ge(s.pick, 3)
            dve.tensor_reduce(first[rows, :], hit[rows, :], AX_X, ALU.max).then_inc(s.pick, 1)
            dve.wait_ge(s.pick, 4)
            dve.tensor_scalar(sel_f[rows, :], first[rows, :], -1.0, float(EXPERTS), ALU.mult,
                              ALU.add).then_inc(s.pick, 1)
            dve.wait_ge(s.nav_ps, 3)
            dve.memset(sel[0:1, 0:2], 0)
            dve.tensor_copy(sel[0:1, 2:], m.misc[0:1, 0:B])

    h_ps, r_ps, y_ps = m.score[0:2], m.score[2:4], m.out_ps
    with nc.Block(no_gpsimd_drain=True) as block:
        @block.tensor
        def _(pe):
            def chosen(i, tiles, name):
                n = 2 + 2 * tiles
                regs = [pe.alloc_register(f"chosen_{name}{b}") for b in range(n)]
                pe.load(regs, sel[0:1, 2 * i:2 * i + n] if isinstance(i, int) else sel[0:1, bass.ds(2 * i, n)])
                return [pe.snap(reg, donate=True, min_val=0, max_val=EXPERTS - 1) for reg in regs]

            def hidden(i, par, experts):
                for b in range(2):
                    e = experts[b]
                    cols = bass.ds(P * i + S * b, S)
                    for fb in range(FB3):
                        o = h_ps[par][:, fb * P + b * S:fb * P + (b + 1) * S]
                        w = bass.ds(e * F3 + fb * P, P)
                        pe.matmul(o, m.w_hi[:, w], xT_hi[:, cols], start=(fb == 0 and b == 0), stop=False,
                                  skip_group_check=True)
                        pe.matmul(o, m.w_hi[:, w], xT_lo[:, cols], start=False, stop=False, skip_group_check=True)
                        pe.matmul(o, m.w_lo[:, w], xT_hi[:, cols], start=False, stop=False, skip_group_check=True)
                        mm = pe.matmul(o, m.b1_rows[:, w], m.ones3[:, 0:S], start=False, stop=True,
                                       skip_group_check=True)
                mm.then_inc(s.h_ps, 1)

            def down(i, par, experts):
                for b in range(2):
                    e = experts[b]
                    if b == 0:
                        pe.wait_ge(s.h_split, i + 1)
                    o = r_ps[par][:, b * S:(b + 1) * S]
                    for fb in range(FB3):
                        w = bass.ds(e * F3 + (EXPERTS * F3 + fb * D), D)
                        f = slice(fb * P + b * S, fb * P + (b + 1) * S)
                        pe.matmul(o, m.w_hi[:, w], h_hi[:, par, f], start=(fb == 0 and b == 0), stop=False,
                                  skip_group_check=True)
                        pe.matmul(o, m.w_hi[:, w], h_lo[:, par, f], start=False, stop=False, skip_group_check=True)
                        pe.matmul(o, m.w_lo[:, w], h_hi[:, par, f], start=False, stop=False, skip_group_check=True)
                    mm = pe.matmul(o, m.b2_rows[:, bass.ds(e * D, D)], m.ones3[:, 0:S], start=False, stop=True,
                                   skip_group_check=True)
                mm.then_inc(s.r_ps, 1)

            def last(i, par):
                pe.wait_ge(s.reasoned, i + 1)
                if not isinstance(i, int) or i > 1:
                    pe.wait_ge(s.y_free, i - 1)
                pe.matmul(y_ps[par][:, 0:D], reasoned[:, par, :], wo, start=True, stop=True).then_inc(s.y_ps, 1)

            def body(i0, name, first):
                e = chosen(i0, 4, name)
                for u in range(4):
                    hidden(i0 + u, u % 2, e[2 + 2 * u:4 + 2 * u])
                    if u or not first:
                        down(i0 + (u - 1), (u + 1) % 2, e[2 * u:2 * u + 2])
                    if u > 1 or not first:
                        last(i0 + (u - 2), u % 2)
            body(0, "first", True)
            with pe.Fori(1, TILES // 4) as i:
                body(4 * i, "next", False)
            down(TILES - 1, 1, chosen(TILES, 0, "last"))
            last(TILES - 2, 0)
            last(TILES - 1, 1)

        @block.scalar
        def _(act):
            def gelu(i, par):
                act.wait_ge(s.h_ps, i + 1)
                act.activation(h_f[:, par, :], h_ps[par][:, 0:F3], ACT.Gelu, scale=1.0 / WSCALE).then_inc(s.gelu, 1)

            def take(i, par):
                act.wait_ge(s.r_ps, i + 1)
                act.activation(reasoned[:, par, :], r_ps[par][:, 0:P], ACT.Copy,
                               scale=1.0 / WSCALE).then_inc(s.reasoned, 1)
            gelu(0, 0)
            gelu(1, 1)
            take(0, 0)
            with act.Fori(1, TILES // 2) as i:
                gelu(2 * i, 0)
                take(2 * i - 1, 1)
                gelu(2 * i + 1, 1)
                take(2 * i, 0)
            take(TILES - 1, 1)

        @block.vector
        def _(dve):
            def split(i, par):
                dve.wait_ge(s.gelu, i + 1)
                dve.tensor_copy(h_hi[:, par, :], h_f[:, par, :]).then_inc(s.h_hi, 1)
                dve.wait_ge(s.h_hi, i + 1)
                dve.tensor_tensor(h_lo[:, par, :], h_f[:, par, :], h_hi[:, par, :], ALU.subtract)\
                   .then_inc(s.h_split, 1)

            def add(i, par):
                dve.wait_ge(s.y_ps, i + 1)
                x = flat(m.x[:, bass.ds(i, 1), :])
                dve.scalar_tensor_tensor(out=x, in0=y_ps[par][:, 0:D], scalar=0.3, in1=x, op0=ALU.mult,
                                         op1=ALU.add).then_inc(s.y_free, 1)
            dve.wait_ge(s.based, GROUPS + 1)
            split(0, 0)
            split(1, 1)
            with dve.Fori(1, TILES // 2) as i:
                split(2 * i, 0)
                add(2 * i - 2, 0)
                split(2 * i + 1, 1)
                add(2 * i - 1, 1)
            add(TILES - 2, 0)
            add(TILES - 1, 1)

        @block.sync
        def _(sp):
            for q in range(STORES):
                rows = slice(q * TILES // STORES, (q + 1) * TILES // STORES)
                sp.wait_ge(s.y_free, (q + 1) * TILES // STORES)
                sp.dma_start(out.rearrange("(t p) d -> p t d", p=P)[:, rows, :], m.x[:, rows, :])\
                  .then_inc(m.stored, 16)
            sp.wait_ge(m.stored, 16 * STORES)


def moe_semaphores(sem, k):
    s = Names()
    s.group_sb = sem(f"moe{k}_group_sb")
    s.normed = sem(f"moe{k}_normed")
    s.logit_ps = sem(f"moe{k}_logit_ps")
    s.turned = sem(f"moe{k}_turned")
    s.route = sem(f"moe{k}_route")
    s.hot = sem(f"moe{k}_hot")
    s.gate_in = sem(f"moe{k}_gate_in")
    s.gate_exp = sem(f"moe{k}_gate_exp")
    s.prefix = sem(f"moe{k}_prefix")
    s.scattered = sem(f"moe{k}_scattered")
    s.added = sem(f"moe{k}_added")
    s.x_turned = sem(f"moe{k}_x_turned")
    s.y_row = sem(f"moe{k}_y_row")
    s.x_split = sem(f"moe{k}_x_split")
    s.h_ps = sem(f"moe{k}_h_ps")
    s.h_split = sem(f"moe{k}_h_split")
    s.y_ps = sem(f"moe{k}_y_ps")
    s.x_hi = sem(f"moe{k}_x_hi")
    s.h_act = sem(f"moe{k}_h_act")
    s.h_f = sem(f"moe{k}_h_f")
    s.h_hi = sem(f"moe{k}_h_hi")
    s.x_row = [sem(f"moe{k}_x_row{u}") for u in range(BUFFERS)]
    s.y_done = [sem(f"moe{k}_y_done{u}") for u in range(BUFFERS)]
    s.fetched = [sem(f"moe{k}_fetched{u}") for u in range(8)]
    return s


def bias0_semaphores(sem):
    s = Names()
    s.bias_in = sem("bias0_bias_in")
    s.bias_step = sem("bias0_bias_step")
    s.bias_rows = sem("bias0_bias_rows")
    s.rows_clear = sem("bias0_rows_clear")
    return s


def diag_semaphores(sem):
    s = Names()
    s.weights = sem("diag_weights")
    s.wvo_ps = sem("diag_wvo_ps")
    s.added = sem("diag_added")
    s.ctx = [sem("diag_ctx0"), sem("diag_ctx1")]
    return s


def quant_semaphores(sem):
    s = Names()
    s.weights = sem("quant_weights")
    s.step = sem("quant_step")
    s.step2 = sem("quant_step2")
    s.normed = sem("quant_normed")
    s.ext = sem("quant_ext")
    s.ext_all = sem("quant_ext_all")
    s.turned = sem("quant_turned")
    s.xqT = sem("quant_xqT")
    s.h_ps = sem("quant_h_ps")
    s.gelu = sem("quant_gelu")
    s.par = sem("quant_par")
    s.rounded = sem("quant_rounded")
    s.clipped = sem("quant_clipped")
    s.hq = sem("quant_hq")
    s.y_ps = sem("quant_y_ps")
    s.added = sem("quant_added")
    return s


def chosen_semaphores(sem):
    s = Names()
    s.weights = sem("chosen_weights")
    s.bias_in = sem("chosen_bias_in")
    s.bias_step = sem("chosen_bias_step")
    s.bias_rows = sem("chosen_bias_rows")
    s.rows_clear = sem("chosen_rows_clear")
    s.xT_lo = sem("chosen_xT_lo")
    s.xT_hi = sem("chosen_xT_hi")
    s.xn_added = sem("chosen_xn_added")
    s.based = sem("chosen_based")
    s.normed = sem("chosen_normed")
    s.turned = sem("chosen_turned")
    s.nav_ps = sem("chosen_nav_ps")
    s.nav = sem("chosen_nav")
    s.pick = sem("chosen_pick")
    s.h_ps = sem("chosen_h_ps")
    s.h_split = sem("chosen_h_split")
    s.r_ps = sem("chosen_r_ps")
    s.reasoned = sem("chosen_reasoned")
    s.y_ps = sem("chosen_y_ps")
    s.gelu = sem("chosen_gelu")
    s.h_hi = sem("chosen_h_hi")
    s.y_free = sem("chosen_y_free")
    return s


def build(nc, d, out):
    m = Names()
    m.ln_count = m.whole_count = 0
    with ExitStack() as ctx:
        def sb(name, shape, dt=F32):
            return ctx.enter_context(nc.sbuf_tensor(name, shape, dt))

        def ps(name):
            return ctx.enter_context(nc.psum_tensor(name, [P, 512], F32))

        def sem(name):
            return ctx.enter_context(nc.semaphore(name))

        m.d = d
        m.ctxT_dram = d["ctxT"]
        m.x = sb("x", [P, TILES, D])
        m.xn2 = sb("xn", [P, 2, GT, D])
        m.xnT2 = sb("xnT", [P, 2, GTOK])
        m.xn, m.xnT = m.xn2[:, 0, :, :], m.xnT2[:, 0, :]
        m.big = sb("big", [P, 16384])
        m.stage = m.big[:, 0:4096].rearrange("p (a n) -> p a n", a=2)
        m.w_hi = sb("w_hi", [P, 3 * EXPERTS * F], F16)
        m.w_lo = sb("w_lo", [P, 3 * EXPERTS * F], F16)
        m.b1_rows = sb("b1_rows", [P, EXPERTS * F], BF16)
        m.b2_rows = sb("b2_rows", [P, EXPERTS * D], BF16)
        m.ones3 = sb("ones3", [P, P], BF16)
        m.ones_b = sb("ones_b", [P, P], BF16)
        m.above = sb("above", [P, P], BF16)
        m.rev_index = sb("rev_index", [P, EXPERTS])
        m.tile_index = sb("tile_index", [P, SLOT_TILES])
        m.sorted_in = nc.dram_tensor("sorted_in", [SLOT_TILES * P, D], F32, kind="Internal").ap()
        m.sorted_out = nc.dram_tensor("sorted_out", [SLOT_TILES * P, D], F32, kind="Internal").ap()
        m.ln_stats = sb("ln_stats", [P, 2, GT, 6])
        m.ln_work = sb("ln_work", [P, 2, 8, GT])
        m.whole_stats = m.big[:, 15000:15000 + TILES * 6].rearrange("p (t s) -> p t s", t=TILES)
        m.whole_work = m.big[:, 15200:15200 + TILES * 8].rearrange("p (w t) -> p w t", w=8)
        m.eps = sb("eps", [P, TILES])
        m.minus_half = sb("minus_half", [P, TILES])
        m.ident = sb("ident", [P, P])
        m.ident_b = sb("ident_b", [P, P], BF16)
        att = Region(m.big, 4096)
        m.ctx = att.take((2, 2 * GT, 2, S))
        m.qbd = att.take((2, 2, GTOK))
        kexp = sb("kexp", [P, 2 * 2 * GT * HQ * S])
        m.kexp_buffer = kexp
        m.quant = sb("quant", [P, 2300])
        m.xall = kexp[:, :].rearrange("p (t d) -> p t d", t=TILES)
        m.kexp = kexp[:, :].rearrange("p (a g t h k) -> p a g t h k", a=2, g=2, t=GT, h=HQ)
        m.v2 = sb("v2", [P, 2, GT, 2, HEADS, DH + 1])
        m.neg_max = sb("neg_max", [P, 4, 2 * HQ], BF16)
        m.prob = att.take((2, 512))
        m.pT = att.take((2, 512))
        m.o_raw = sb("o_raw", [P, 2, HEADS, DH + 1])
        m.o_rec = sb("o_rec", [P, 2, HEADS])
        m.o_norm = sb("o_norm", [P, 2, D])
        m.oT = sb("oT", [P, 2 * P])
        m.batch_mask = sb("batch_mask", [P, GTOK])
        m.head_mask = sb("head_mask", [P, HQ])
        m.value_mask = sb("value_mask", [P, D])
        m.penalty = sb("penalty", [P, TILES, S], BF16)
        m.mask_in = att.take((TILES, S), I32)
        m.score = [ps(f"score{g}") for g in range(4)]
        m.pT_ps = ps("pT_ps")
        m.out_ps = [ps("out_ps0"), ps("out_ps1")]
        m.misc = ps("misc")
        m.xn_ready = sem("xn_ready")
        m.ln_step = sem("ln_step")
        m.whole_rows = sem("whole_rows")
        m.x_whole = sem("x_whole")
        m.ln_eps_added = sem("ln_eps_added")
        m.ln_rstd_ready = sem("ln_rstd_ready")
        m.filled = sem("filled")
        m.emptied = sem("emptied")
        m.scored = sem("scored")
        m.maxed = sem("maxed")
        m.shifted = sem("shifted")
        m.probs = sem("probs")
        m.turned = sem("turned")
        m.turned_out = sem("turned_out")
        m.valued = sem("valued")
        m.o_copied = sem("o_copied")
        m.o_rec_ready = sem("o_rec_ready")
        m.o_ready = sem("o_ready")
        m.consts = sem("consts")
        m.x_in = sem("x_in")
        m.att_w = sem("att_w")
        m.bias_ps = sem("bias_ps")
        m.stored = sem("stored")
        m.zeroed = sem("zeroed")
        m.split_step = sem("split_step")
        m.zero_tile = sem("zero_tile")
        m.staged = [sem("staged0"), sem("staged1")]
        m.s_moe = [moe_semaphores(sem, k) for k in range(2)]
        m.s_bias0 = bias0_semaphores(sem)
        m.s_diag = diag_semaphores(sem)
        m.s_quant = quant_semaphores(sem)
        m.s_chosen = chosen_semaphores(sem)
        moes, chunk0 = [], 0
        for weights, chunks in ((d["moe0_w"], 4), (d["moe1_w"], 6), (d["chosen_w"], 2)):
            c = Names()
            c.weights, c.chunks, c.chunk0 = weights, chunks, chunk0
            chunk0 += chunks
            moes.append(c)
        for k, c in enumerate(moes[0:2]):
            c.router = sb(f"router{k}", [P, EXPERTS])
        m.ctx_loaded = [sem("ctx_loaded0"), sem("ctx_loaded1")]

        ws = []
        for a, layer in enumerate((0, 1, 3)):
            w = Names()
            w.wq = sb(f"wq{a}", [P, 2, P])
            w.wk = sb(f"wk{a}", [P, 2, 2, P])
            w.wv = sb(f"wv{a}", [P, D])
            w.wo = sb(f"wo{a}", [P, D])
            w.bq = sb(f"bq{a}", [P, 2])
            w.bk = sb(f"bk{a}", [P, 2])
            w.bk_heads = sb(f"bk_heads{a}", [P, 2, HQ])
            if a:
                w.bv = sb(f"bv{a}", [P, 1])
                w.bo = sb(f"bo{a}", [P, D])
                w.out_bias = sb(f"out_bias{a}", [P, D])
            w.layer = layer
            ws.append(w)

        setup = Region(m.big, att.at)
        bias_f = setup.take((2, 32))
        bias_b = setup.take((3, 2, 32), BF16)
        zero_tile = setup.take((P,))
        consts_in = setup.take((3 * P,))
        FIRST = 2 * GT

        with nc.Block(no_gpsimd_drain=True) as block:
            @block.sync
            def _(sp):
                x = d["x"].rearrange("(t p) d -> p t d", p=P)
                sp.dma_start(m.x[:, 0:FIRST, :], x[:, 0:FIRST, :]).then_inc(m.x_in, 16)
                sp.dma_start(m.ident[:, :], d["ident"]).then_inc(m.consts, 16)
                sp.dma_start(m.batch_mask[:, :], d["batch_mask"]).then_inc(m.consts, 16)
                sp.dma_start(m.head_mask[:, :], d["head_mask"]).then_inc(m.consts, 16)
                sp.dma_start(m.value_mask[:, :], d["value_mask"]).then_inc(m.consts, 16)

            @block.scalar
            def _(act):
                load_attention_weights(act, m, ws[0], False)

            @block.vector
            def _(dve):
                dve.memset(m.eps[:, :], EPS)
                dve.memset(m.minus_half[:, :], -0.5)
                dve.memset(ws[0].bq[:, :], 0.0)
                dve.memset(ws[0].bk_heads[:, :, :], 0.0)
                dve.memset(zero_tile, 0.0).then_inc(m.zero_tile, 1)
                clear_bias_rows(dve, m, m.s_bias0, bias_f)
                dve.wait_ge(m.consts, 64)
                dve.tensor_copy(m.ident_b[:, :], m.ident[:, :])
                for par in range(2):
                    for t in range(GT):
                        dve.tensor_copy(m.v2[:, par, t, :, :, DH],
                                        m.value_mask[:, 0:D:DH].unsqueeze(1).to_broadcast([P, 2, HEADS]))
                dve.wait_ge(m.x_in, 16)
                dve.wait_ge(m.att_w, 64)

        def later_loads(sp):
            x = d["x"].rearrange("(t p) d -> p t d", p=P)
            sp.dma_start(m.x[:, FIRST:, :], x[:, FIRST:, :]).then_inc(m.x_in, 16)
            sp.dma_start(m.mask_in[:, :, :], d["mask"].rearrange("(t p) k -> p t k", p=P)).then_inc(m.consts, 16)
            sp.dma_start(consts_in, d["consts"]).then_inc(m.consts, 16)
            sp.dma_start(m.rev_index[:, :], d["rev_index"].partition_broadcast(P)).then_inc(m.consts, 16)
            sp.dma_start(m.tile_index[:, :], d["tile_index"].partition_broadcast(P)).then_inc(m.consts, 16)
            for k, c in enumerate(moes[0:2]):
                sp.dma_start(c.router[:, :], d[f"router{k}"]).then_inc(m.consts, 16)
            for w in ws[1:]:
                load_attention_weights(sp, m, w, True)
            sp.wait_ge(m.zero_tile, 1)
            sp.dma_start(m.sorted_in.rearrange("(t p) d -> p t d", p=P),
                         zero_tile.unsqueeze(1).to_broadcast([P, SLOT_TILES, P])).then_inc(m.zeroed, 16)

        def later_rows(sp):
            load_bias_rows(sp, m, m.s_bias0, bias_f, bias_b, d["moe0_b1"], d["moe0_b2"])

        def later_split(pool):
            split_bias_rows(pool, m, m.s_bias0, bias_f, bias_b)

        def later_constants(dve):
            dve.wait_ge(m.consts, 64 + 16 * 6)
            dve.tensor_copy(m.ones3[:, :], consts_in[:, 0:P])
            dve.tensor_copy(m.ones_b[:, :], consts_in[:, P:2 * P])
            dve.tensor_copy(m.above[:, :], consts_in[:, 2 * P:3 * P])
            dve.tensor_scalar(m.penalty[:, :, :], m.mask_in[:, :, :], 0, MASKED, ALU.is_equal, ALU.mult)
            dve.wait_ge(m.att_w, 16 * 20)
            for w in ws[1:]:
                for gp in range(2):
                    dve.tensor_scalar(w.bk_heads[:, gp, :], m.head_mask[:, :], w.bk[:, gp:gp + 1], None, ALU.mult)

        def later_products(pe):
            pe.wait_ge(m.att_w, 16 * 20)
            pe.wait_ge(m.emptied, FILLS)
            for a, w in enumerate(ws[1:]):
                mm = pe.matmul(m.misc[:, a * D:(a + 1) * D], w.bv[:, :].to_broadcast([P, P]), w.wo[:, :],
                               start=True, stop=True, skip_group_check=True)
            mm.then_inc(m.bias_ps, 1)

        def later_biases(dve):
            dve.wait_ge(m.bias_ps, 1)
            for a, w in enumerate(ws[1:]):
                dve.tensor_tensor(w.out_bias[:, :], m.misc[:, a * D:(a + 1) * D], w.bo[:, :], ALU.add)

        later = Names()
        later.loads, later.rows, later.split = later_loads, later_rows, later_split
        later.constants, later.products, later.biases = later_constants, later_products, later_biases

        attention(nc, m, 0, ws[0], masked=False, biased=False, experts=moes[0], later=later)
        routed = moe(nc, m, 0, moes[0])
        attention(nc, m, 1, ws[1], masked=True, biased=True, experts=moes[1], fetch=routed)
        quantized_ffn(nc, m)
        routed = moe(nc, m, 1, moes[1])
        attention(nc, m, 2, ws[2], masked=False, biased=True, experts=moes[2], fetch=routed)
        chosen_ffn(nc, m, out)


def _layout(i):
    f = {k: np.asarray(v) for k, v in i.items()}
    r = np.arange(P)
    d = {"ident": np.eye(P, dtype=np.float32)}
    d["batch_mask"] = (r[:, None] % 64 // 32 == np.arange(GTOK) // S % 2).astype(np.float32)
    d["head_mask"] = (r[:, None] % 32 // DH == np.arange(HQ)).astype(np.float32)
    d["value_mask"] = (r[:, None] // S == r[None, :] // DH % 2).astype(np.float32)
    d["x"] = f["x"].reshape(TOKENS, D)
    d["ctxT"] = f["ctx_1024"].reshape(TOKENS, D).T
    d["mask"] = f["mask_BxSxS2_ik1"].reshape(TOKENS, S)
    d["consts"] = np.concatenate([np.repeat((r < 3)[:, None], P, 1), np.ones((P, P)), r[:, None] < r[None, :]],
                                 1).astype(np.float32)
    d["rev_index"] = (EXPERTS - np.arange(EXPERTS)).astype(np.float32)
    d["tile_index"] = np.arange(SLOT_TILES).astype(np.float32)
    def up_of(w):
        return w.transpose(1, 0, 2).reshape(D, EXPERTS * F)

    def down_of(w):
        return w.reshape(EXPERTS, FB, P, D).transpose(2, 0, 1, 3).reshape(P, EXPERTS * F)
    d["router0"], d["router1"] = f["L0_ffn_router_w"].T, f["L2_ffn_router_w"]
    d["moe0_w"] = np.concatenate([up_of(f["L0_ffn_w1"].transpose(0, 2, 1)),
                                  down_of(f["L0_ffn_w2"].transpose(0, 2, 1))], 1)
    d["moe0_b1"], d["moe0_b2"] = f["L0_ffn_b1"].reshape(P, -1), f["L0_ffn_b2"].reshape(P, -1)
    both = [np.concatenate([f[f"L2_ffn_{n}_w"], f[f"L2_ffn_shared_{n}_w"][None]]) for n in ("up", "gate", "down")]
    d["moe1_w"] = np.concatenate([up_of(both[0]), up_of(both[1]), down_of(both[2])], 1)
    d["quant_w1"] = f["L1_ffn_W1"].T
    d["quant_w2"] = f["L1_ffn_W2"].T.reshape(FB, P, D).transpose(1, 0, 2).reshape(P, F)
    d["quant_b1"], d["quant_b2"] = f["L1_ffn_b1"].reshape(FB, P).T, f["L1_ffn_b2"]
    wide = DIAG_BLOCKS * P
    d["diag_wvT"] = f["L2_xattn_Wkv"][:, wide:].T.reshape(DIAG_BLOCKS, P, D).transpose(1, 0, 2).reshape(P, -1)
    d["diag_wout"] = f["L2_xattn_Wout"].reshape(DIAG_BLOCKS, P, D).transpose(1, 0, 2).reshape(P, -1)
    d["diag_bout"] = f["L2_xattn_bout"]
    d["chosen_w"] = np.concatenate([f["L3_ffn_W1"].transpose(1, 0, 2).reshape(D, -1),
                                    f["L3_ffn_W2"].reshape(EXPERTS, FB3, P, D).transpose(2, 0, 1, 3).reshape(P, -1)], 1)
    d["chosen_b1"], d["chosen_b2"] = f["L3_ffn_b1"].reshape(P, -1), f["L3_ffn_b2"].reshape(P, -1)
    d["chosen_wp1"], d["chosen_wp2"], d["chosen_wo"] = f["L3_ffn_Wp1"], f["L3_ffn_Wp2"], f["L3_ffn_Wo"]
    d["chosen_bp1"], d["chosen_bp2"], d["chosen_bo"] = f["L3_ffn_bp1"].reshape(P, 1), f["L3_ffn_bp2"], f["L3_ffn_bo"]
    w0 = f["L0_xattn_Wkv"]
    att = {0: (f["L0_xattn_Wq"], w0[:, :D], w0[:, D:], f["L0_xattn_Wout"]),
           1: tuple(f[f"L1_xattn_W{c}"] for c in "qkvo"),
           3: tuple(f[f"L3_xattn_W{c}"].T for c in "qkvo")}
    for n, (wq, wk, wv, wo) in att.items():
        def blocks(w):
            return w.reshape(-1, 2, 2, 32)
        d[f"wq{n}"] = np.stack([blocks(wq)] * 2, axis=3).reshape(D, 2 * P)
        k, z = blocks(wk), np.zeros_like(blocks(wk))
        d[f"wk{n}"] = np.stack([np.stack([k, z], 3), np.stack([z, k], 3)], 1).reshape(D, 4 * P)
        d[f"wv{n}"], d[f"wo{n}"] = wv, wo
        if n:
            for c in "qk":
                b = f[f"L{n}_xattn_b{c}"].reshape(2, 2, 32)
                d[f"b{c}{n}"] = np.stack([b] * 2, axis=2).reshape(2, P).T
            d[f"bv{n}"] = f[f"L{n}_xattn_bv"].reshape(D, 1)
            d[f"bo{n}"] = f[f"L{n}_xattn_bo"]
    return {k: np.ascontiguousarray(v) for k, v in d.items()}


def kernel(**inputs):
    import concourse.bacc as bacc
    from concourse.bass_utils import run_bass_kernel_spmd

    nc = bacc.Bacc("TRN2", target_bir_lowering=False, num_devices=1)
    arrays = _layout(inputs)
    d = {k: nc.dram_tensor(f"in_{k}", v.shape, mybir.dt.from_np(v.dtype), kind="ExternalInput").ap()
         for k, v in arrays.items()}
    out = nc.dram_tensor("out", (TOKENS, D), F32, kind="ExternalOutput").ap()
    build(nc, d, out)
    r = run_bass_kernel_spmd(nc, [{f"in_{k}": v for k, v in arrays.items()}], core_ids=[0])
    return r.results[0]["out"].reshape(B, S, D)
```
